# Optimizing a Trainium2 kernel written in Bass

```python
import numpy as np
import jax
import jax.numpy as jnp

def _softmax(x, axis=-1):
    return jax.nn.softmax(x, axis=axis)

def _gelu(x):
    return jax.nn.gelu(x, approximate=True)

def _silu(x):
    return jax.nn.silu(x)

def _sigmoid(x):
    return jax.nn.sigmoid(x)

def _layernorm(x, axis=-1, eps=1e-05):
    m = jnp.mean(x, axis=axis, keepdims=True)
    v = jnp.var(x, axis=axis, keepdims=True)
    return (x - m) / jnp.sqrt(v + eps)

def _scatter_add(tgt, idx, src, axis=0):
    return tgt.at[idx].add(src)

def _segment_sum(src, seg, n):
    return jax.ops.segment_sum(src, seg, n)
kernel_name = 'mk_decoder_postln_d2_seqx_r8_85ab14'

def setup_inputs(seed: int=0):
    np.random.seed(seed)
    _w = jnp.asarray

    def _rec_inputs():
        import jax
        import jax.numpy as jnp
        _rk = jax.random.key(seed)
        x = -0.0002928 + 1 * jax.random.normal(jax.random.fold_in(_rk, 1), (8, 128, 128), jnp.float32)
        _lenS = 128 - jax.random.randint(jax.random.fold_in(_rk, 7), (8,), 0, max(1, 128 // 4) + 1, jnp.int32)
        _lenS2 = 77 - jax.random.randint(jax.random.fold_in(_rk, 8), (8,), 0, max(1, 77 // 4) + 1, jnp.int32)
        _ctx_1024P = jax.random.normal(jax.random.fold_in(_rk, 11), (8, 16, 128), jnp.float32)
        _ctx_1024c = jax.random.dirichlet(jax.random.fold_in(_rk, 511), 0.3 * jnp.ones((16,), jnp.float32), (8, 77))
        _ctx_1024t = jnp.einsum('bsk,bkd->bsd', _ctx_1024c, _ctx_1024P)
        _ctx_1024t = _ctx_1024t * jax.lax.rsqrt(jnp.mean(jnp.square(_ctx_1024t)) + 1e-12) * 0.953939
        ctx_1024 = -1.39393e-06 + 0.999914 * (_ctx_1024t + 0.3 * jax.random.normal(jax.random.fold_in(_rk, 611), (8, 77, 128), jnp.float32))
        return (x, ctx_1024)
    x, ctx_1024 = _rec_inputs()

    def _L0_attn_setup():
        import jax, jax.numpy as jnp
        import numpy as np
        DIM = 128
        HEADS = 16
        HEAD_DIM = DIM // HEADS

        def _xavier(key, shape):
            fan_out, fan_in = shape
            limit = float(np.sqrt(6.0 / (fan_in + fan_out)))
            return jax.random.uniform(key, shape, jnp.float32, -limit, limit)
        key = jax.random.key(seed)
        kx, kv, kk, kq = jax.random.split(key, 4)
        x = jax.random.normal(kx, (4, 256, DIM), jnp.float32)
        Wv = _xavier(kv, (DIM, DIM))
        Wk = _xavier(kk, (DIM, DIM))
        Wq = _xavier(kq, (DIM, DIM))
        return {'x': x, 'Wq': Wq, 'Wk': Wk, 'Wv': Wv}
    _L0_attn_all = _L0_attn_setup()
    _L0_attn_in = {k: v for k, v in _L0_attn_all.items() if k in ('Wq', 'Wk', 'Wv')}
    del _L0_attn_all

    def _L0_xattn_setup():
        import jax, jax.numpy as jnp
        import numpy as np
        D_MODEL = 128
        N_HEADS = 16
        D_HIDDEN = D_MODEL // N_HEADS
        key = jax.random.key(seed)
        ks = jax.random.split(key, 11)
        B, S = (2, 256)
        scale = 1.0 / np.sqrt(D_MODEL)
        inp = {'q': jax.random.normal(ks[0], (B, S, D_MODEL), dtype=jnp.float32), 'k': jax.random.normal(ks[1], (B, S, D_MODEL), dtype=jnp.float32), 'v': jax.random.normal(ks[2], (B, S, D_MODEL), dtype=jnp.float32), 'Wq': jax.random.normal(ks[3], (D_MODEL, D_MODEL), dtype=jnp.float32) * scale, 'bq': jnp.zeros((D_MODEL,), dtype=jnp.float32), 'Wk': jax.random.normal(ks[4], (D_MODEL, D_MODEL), dtype=jnp.float32) * scale, 'bk': jnp.zeros((D_MODEL,), dtype=jnp.float32), 'Wv': jax.random.normal(ks[5], (D_MODEL, D_MODEL), dtype=jnp.float32) * scale, 'bv': jnp.zeros((D_MODEL,), dtype=jnp.float32), 'Wo': jax.random.normal(ks[6], (D_MODEL, D_MODEL), dtype=jnp.float32) * scale, 'bo': jnp.zeros((D_MODEL,), dtype=jnp.float32)}
        return inp
    _L0_xattn_all = _L0_xattn_setup()
    _L0_xattn_in = {k: v for k, v in _L0_xattn_all.items() if k in ('Wq', 'bq', 'Wk', 'bk', 'Wv', 'bv', 'Wo', 'bo')}
    del _L0_xattn_all

    def _L0_ffn_setup():
        import jax, jax.numpy as jnp
        import numpy as np
        TOP_K = 2
        CAPACITY_FACTOR = 1.0
        key = jax.random.key(seed)
        ks = jax.random.split(key, 4)
        sl, bs, hs, ffn, E = (256, 8, 128, 512, 8)
        x = jax.random.normal(ks[0], (sl, bs, hs), dtype=jnp.float32)
        w_router = jax.random.normal(ks[1], (hs, E), dtype=jnp.float32) * 0.02
        w1 = jax.random.normal(ks[2], (E, hs, ffn), dtype=jnp.float32) * 0.02
        w2 = jax.random.normal(ks[3], (E, ffn, hs), dtype=jnp.float32) * 0.02
        bias = jnp.zeros((1, 1, hs), dtype=jnp.float32)
        return {'x': x, 'w_router': w_router, 'w1': w1, 'w2': w2, 'bias': bias}
    _L0_ffn_all = _L0_ffn_setup()
    _L0_ffn_in = {k: v for k, v in _L0_ffn_all.items() if k in ('w_router', 'w1', 'w2', 'bias')}
    del _L0_ffn_all

    def _L1_attn_setup():
        import jax, jax.numpy as jnp
        import numpy as np
        B, T, D_DENSE = (4, 256, 128)
        SPARSE = 128
        NH = 8
        HD = SPARSE // NH
        K = 32
        WIN = 64
        RANK = HD // 4
        key = jax.random.key(seed)
        ks = jax.random.split(key, 8)
        n = lambda k, shape, scale=1.0: jax.random.normal(k, shape, dtype=jnp.float32) * scale
        return {'x': n(ks[0], (B, T, D_DENSE)), 'encoder_query': n(ks[1], (NH, D_DENSE, HD), 0.02), 'encoder_value': n(ks[2], (NH, D_DENSE, HD), 0.02), 'mn_w1': n(ks[3], (SPARSE, SPARSE // 2), 1.0 / np.sqrt(SPARSE)), 'mn_b1': jnp.zeros((SPARSE // 2,), jnp.float32), 'mn_w2': n(ks[4], (SPARSE // 2, NH * HD), 1.0 / np.sqrt(SPARSE // 2)), 'mn_b2': jnp.zeros((NH * HD,), jnp.float32), 'base_metric': jnp.ones((NH, HD), jnp.float32) * 0.1, 'decoder': n(ks[5], (NH * HD, D_DENSE), 0.02), 'hebbian_U': n(ks[6], (NH, HD, RANK), 0.01), 'hebbian_V': n(ks[7], (NH, RANK, HD), 0.01)}
    _L1_attn_all = _L1_attn_setup()
    _L1_attn_in = {k: v for k, v in _L1_attn_all.items() if k in ('encoder_query', 'encoder_value', 'mn_w1', 'mn_b1', 'mn_w2', 'mn_b2', 'base_metric', 'decoder', 'hebbian_U', 'hebbian_V')}
    del _L1_attn_all

    def _L1_xattn_setup():
        import jax, jax.numpy as jnp
        import numpy as np
        key = jax.random.key(seed)
        k1, k2 = jax.random.split(key)
        B, L, V, D = (8, 256, 128, 128)
        hidden_states = jax.random.normal(k1, (B, L, D), dtype=jnp.float32)
        visual_hidden_state = jax.random.normal(k2, (B, V, D), dtype=jnp.float32)
        return {'hidden_states': hidden_states, 'visual_hidden_state': visual_hidden_state}
    _L1_xattn_all = _L1_xattn_setup()
    _L1_xattn_in = {k: v for k, v in _L1_xattn_all.items() if k in ()}
    del _L1_xattn_all

    def _L1_ffn_setup():
        import jax, jax.numpy as jnp
        import numpy as np
        EPS = 1e-08

        def _ste(x, q):
            return x + jax.lax.stop_gradient(q - x)

        def quant_act_uint8(x):
            s = jax.lax.stop_gradient(jnp.maximum(jnp.max(x), EPS)) / 255.0
            q = jnp.clip(jnp.round(x / s), 0.0, 255.0) * s
            return (_ste(x, q), s)

        def quant_weight_int8_perchannel(w):
            s = jax.lax.stop_gradient(jnp.maximum(jnp.max(jnp.abs(w), axis=1, keepdims=True), EPS)) / 127.0
            q = jnp.clip(jnp.round(w / s), -128.0, 127.0) * s
            return (_ste(w, q), s[:, 0])

        def quant_bias_int32(b, s_in, s_w):
            s = jax.lax.stop_gradient(s_in * s_w)
            q = jnp.round(b / s) * s
            return _ste(b, q)

        def quant_linear(x, w, b):
            xq, s_in = quant_act_uint8(x)
            wq, s_w = quant_weight_int8_perchannel(w)
            bq = quant_bias_int32(b, s_in, s_w)
            return jnp.einsum('btd,fd->btf', xq, wq) + bq
        key = jax.random.key(seed)
        k1, k2, k3, k4, k5 = jax.random.split(key, 5)
        B, S, D, F = (4, 256, 128, 512)
        return {'x': jax.random.normal(k1, (B, S, D), dtype=jnp.float32), 'w1': jax.random.normal(k2, (F, D), dtype=jnp.float32) * (1.0 / np.sqrt(D)), 'b1': jax.random.normal(k3, (F,), dtype=jnp.float32) * 0.01, 'w2': jax.random.normal(k4, (D, F), dtype=jnp.float32) * (1.0 / np.sqrt(F)), 'b2': jax.random.normal(k5, (D,), dtype=jnp.float32) * 0.01}
    _L1_ffn_all = _L1_ffn_setup()
    _L1_ffn_in = {k: v for k, v in _L1_ffn_all.items() if k in ('w1', 'b1', 'w2', 'b2')}
    del _L1_ffn_all
    return {'x': x, 'ctx_1024': ctx_1024, 'L0_attn_Wq': _L0_attn_in['Wq'], 'L0_attn_Wk': _L0_attn_in['Wk'], 'L0_attn_Wv': _L0_attn_in['Wv'], 'L0_xattn_Wq': _L0_xattn_in['Wq'], 'L0_xattn_bq': _L0_xattn_in['bq'], 'L0_xattn_Wk': _L0_xattn_in['Wk'], 'L0_xattn_bk': _L0_xattn_in['bk'], 'L0_xattn_Wv': _L0_xattn_in['Wv'], 'L0_xattn_bv': _L0_xattn_in['bv'], 'L0_xattn_Wo': _L0_xattn_in['Wo'], 'L0_xattn_bo': _L0_xattn_in['bo'], 'L0_ffn_w_router': _L0_ffn_in['w_router'], 'L0_ffn_w1': _L0_ffn_in['w1'], 'L0_ffn_w2': _L0_ffn_in['w2'], 'L0_ffn_bias': _L0_ffn_in['bias'], 'L1_attn_encoder_query': _L1_attn_in['encoder_query'], 'L1_attn_encoder_value': _L1_attn_in['encoder_value'], 'L1_attn_mn_w1': _L1_attn_in['mn_w1'], 'L1_attn_mn_b1': _L1_attn_in['mn_b1'], 'L1_attn_mn_w2': _L1_attn_in['mn_w2'], 'L1_attn_mn_b2': _L1_attn_in['mn_b2'], 'L1_attn_base_metric': _L1_attn_in['base_metric'], 'L1_attn_decoder': _L1_attn_in['decoder'], 'L1_attn_hebbian_U': _L1_attn_in['hebbian_U'], 'L1_attn_hebbian_V': _L1_attn_in['hebbian_V'], 'L1_ffn_w1': _L1_ffn_in['w1'], 'L1_ffn_b1': _L1_ffn_in['b1'], 'L1_ffn_w2': _L1_ffn_in['w2'], 'L1_ffn_b2': _L1_ffn_in['b2']}

def reference(x, ctx_1024, L0_attn_Wq, L0_attn_Wk, L0_attn_Wv, L0_xattn_Wq, L0_xattn_bq, L0_xattn_Wk, L0_xattn_bk, L0_xattn_Wv, L0_xattn_bv, L0_xattn_Wo, L0_xattn_bo, L0_ffn_w_router, L0_ffn_w1, L0_ffn_w2, L0_ffn_bias, L1_attn_encoder_query, L1_attn_encoder_value, L1_attn_mn_w1, L1_attn_mn_b1, L1_attn_mn_w2, L1_attn_mn_b2, L1_attn_base_metric, L1_attn_decoder, L1_attn_hebbian_U, L1_attn_hebbian_V, L1_ffn_w1, L1_ffn_b1, L1_ffn_w2, L1_ffn_b2):
    import jax
    import jax.numpy as jnp

    def _L0_attn_ref(x, Wq, Wk, Wv):
        import jax, jax.numpy as jnp
        import numpy as np
        DIM = 128
        HEADS = 16
        HEAD_DIM = DIM // HEADS

        def _xavier(key, shape):
            fan_out, fan_in = shape
            limit = float(np.sqrt(6.0 / (fan_in + fan_out)))
            return jax.random.uniform(key, shape, jnp.float32, -limit, limit)
        B, S, D = x.shape
        H, Hd = (HEADS, HEAD_DIM)
        q = (x @ Wq.T).reshape(B, S, H, Hd)
        k = (x @ Wk.T).reshape(B, S, H, Hd)
        v = (x @ Wv.T).reshape(B, S, H, Hd)
        energy = jnp.einsum('bqhd,bkhd->bhqk', q, k)
        attn = jax.nn.softmax(energy / jnp.sqrt(jnp.float32(D)), axis=-1)
        out = jnp.einsum('bhqk,bkhd->bqhd', attn, v).reshape(B, S, D)
        return out

    def _L0_xattn_ref(q, k, v, Wq, bq, Wk, bk, Wv, bv, Wo, bo):
        import jax, jax.numpy as jnp
        import numpy as np
        D_MODEL = 128
        N_HEADS = 16
        D_HIDDEN = D_MODEL // N_HEADS
        B, S, _ = q.shape

        def proj(x, W, b):
            y = jnp.einsum('bsd,de->bse', x, W) + b
            return y.reshape(B, -1, N_HEADS, D_HIDDEN).transpose(0, 2, 1, 3)
        qh = proj(q, Wq, bq)
        kh = proj(k, Wk, bk)
        vh = proj(v, Wv, bv)
        scores = jnp.einsum('bhqd,bhkd->bhqk', qh, kh) / np.sqrt(D_HIDDEN)
        scores = jax.nn.softmax(scores, axis=-1)
        attn = jnp.einsum('bhqk,bhkd->bhqd', scores, vh)
        concat = attn.transpose(0, 2, 1, 3).reshape(B, -1, D_MODEL)
        return jnp.einsum('bsd,de->bse', concat, Wo) + bo

    def _L0_ffn_ref(x, w_router, w1, w2, bias):
        import jax, jax.numpy as jnp
        import numpy as np
        TOP_K = 2
        CAPACITY_FACTOR = 1.0
        sl, bs, hs = x.shape
        E = w_router.shape[1]
        xf = x.reshape(-1, hs)
        T = xf.shape[0]
        capacity = int(CAPACITY_FACTOR * TOP_K * T / E)
        scores = jax.nn.softmax(xf @ w_router, axis=-1)
        expert_weights, top_experts = jax.lax.top_k(scores, TOP_K)
        flat_e = top_experts.reshape(-1)
        flat_w = expert_weights.reshape(-1)
        N = flat_e.shape[0]
        order = jnp.argsort(flat_e, stable=True)
        bin_ids = flat_e[order]
        tpe = jnp.zeros((E,), jnp.int32).at[flat_e].add(1)
        starts = jnp.cumsum(tpe) - tpe
        offsets = jnp.arange(N) - starts[bin_ids]
        valid = offsets < capacity
        slot = jnp.where(valid, bin_ids * capacity + offsets, E * capacity)
        src = order // TOP_K
        xb = jnp.zeros((E * capacity + 1, hs), x.dtype).at[slot].set(xf[src])
        xb = xb[:-1].reshape(E, capacity, hs)
        h = jax.nn.gelu(jnp.einsum('ech,ehf->ecf', xb, w1))
        y = jnp.einsum('ecf,efh->ech', h, w2).reshape(E * capacity, hs)
        yv = jnp.where(valid[:, None], y[jnp.minimum(slot, E * capacity - 1)], 0.0)
        out = jnp.zeros((T, hs), x.dtype).at[src].add(flat_w[order][:, None] * yv)
        return out.reshape(sl, bs, hs) + bias

    def _L1_attn_ref(x, encoder_query, encoder_value, mn_w1, mn_b1, mn_w2, mn_b2, base_metric, decoder, hebbian_U, hebbian_V):
        import jax, jax.numpy as jnp
        import numpy as np
        B, T, D_DENSE = (4, 256, 128)
        SPARSE = 128
        NH = 8
        HD = SPARSE // NH
        K = 32
        WIN = 64
        RANK = HD // 4
        Bv, Tv, _ = x.shape
        q = jax.nn.relu(jnp.einsum('btd,nde->btne', x, encoder_query))
        v = jax.nn.relu(jnp.einsum('btd,nde->btne', x, encoder_value))
        qflat = q.reshape(Bv, Tv, -1)
        sig = qflat.mean(axis=1)
        if Tv >= 8:
            sig = sig + qflat[:, ::8].mean(axis=1) * 0.5
        hidden = jax.nn.gelu(sig @ mn_w1 + mn_b1, approximate=False)
        mod = (hidden @ mn_w2 + mn_b2).reshape(Bv, NH, HD)
        metric = jax.nn.softplus(base_metric[None] + 0.1 * mod)
        pos = jnp.arange(Tv)
        offs = jnp.arange(0, -WIN, -1)
        idx = jnp.clip(pos[:, None] + offs[None, :], 0, Tv - 1)
        mask = idx <= pos[:, None]
        k_act = min(K, WIN)
        batch_ix = jnp.arange(Bv)[:, None, None]
        outs = []
        for h in range(NH):
            q_h = q[:, :, h, :]
            v_h = v[:, :, h, :]
            kw = q_h[:, idx, :]
            diff = kw - q_h[:, :, None, :]
            wsq = diff * diff * metric[:, h][:, None, None, :]
            dist = jnp.sqrt(wsq.sum(-1) + 1e-08)
            dist = jnp.where(mask[None], dist, jnp.inf)
            neg, loc = jax.lax.top_k(-dist, k_act)
            topd = -neg
            topi = jnp.take_along_axis(jnp.broadcast_to(idx[None], (Bv, Tv, WIN)), loc, axis=2)
            infl = jnp.exp(-topd)
            infl = infl / (infl.sum(-1, keepdims=True) + 1e-08)
            nv = v_h[batch_ix, topi]
            context = jnp.einsum('btk,btkd->btd', infl, nv)
            q_norm = jnp.linalg.norm(q_h, axis=-1, keepdims=True)
            gate = (q_norm > 0.2).astype(q_h.dtype)
            Hm = hebbian_U[h] @ hebbian_V[h]
            qhat = q_h / jnp.maximum(q_norm, 1e-12)
            context = context + gate * 0.1 * (qhat @ Hm)
            outs.append(q_h * context)
        out_sparse = jnp.stack(outs, axis=2).reshape(Bv, Tv, -1)
        return out_sparse @ decoder

    def _L1_xattn_ref(hidden_states, visual_hidden_state):
        import jax, jax.numpy as jnp
        import numpy as np
        scores = jnp.einsum('bld,bvd->blv', hidden_states, visual_hidden_state)
        probs = jax.nn.softmax(scores, axis=-1)
        return jnp.einsum('blv,bvd->bld', probs, visual_hidden_state)

    def _L1_ffn_ref(x, w1, b1, w2, b2):
        import jax, jax.numpy as jnp
        import numpy as np
        EPS = 1e-08

        def _ste(x, q):
            return x + jax.lax.stop_gradient(q - x)

        def quant_act_uint8(x):
            s = jax.lax.stop_gradient(jnp.maximum(jnp.max(x), EPS)) / 255.0
            q = jnp.clip(jnp.round(x / s), 0.0, 255.0) * s
            return (_ste(x, q), s)

        def quant_weight_int8_perchannel(w):
            s = jax.lax.stop_gradient(jnp.maximum(jnp.max(jnp.abs(w), axis=1, keepdims=True), EPS)) / 127.0
            q = jnp.clip(jnp.round(w / s), -128.0, 127.0) * s
            return (_ste(w, q), s[:, 0])

        def quant_bias_int32(b, s_in, s_w):
            s = jax.lax.stop_gradient(s_in * s_w)
            q = jnp.round(b / s) * s
            return _ste(b, q)

        def quant_linear(x, w, b):
            xq, s_in = quant_act_uint8(x)
            wq, s_w = quant_weight_int8_perchannel(w)
            bq = quant_bias_int32(b, s_in, s_w)
            return jnp.einsum('btd,fd->btf', xq, wq) + bq
        h = jax.nn.relu(quant_linear(x, w1, b1))
        return quant_linear(h, w2, b2)
    x = _layernorm(x + _L0_attn_ref(x, L0_attn_Wq, L0_attn_Wk, L0_attn_Wv), axis=-1)
    x = _layernorm(x + _L0_xattn_ref(x, ctx_1024, ctx_1024, L0_xattn_Wq, L0_xattn_bq, L0_xattn_Wk, L0_xattn_bk, L0_xattn_Wv, L0_xattn_bv, L0_xattn_Wo, L0_xattn_bo), axis=-1)
    x = _layernorm(x + _L0_ffn_ref(x, L0_ffn_w_router, L0_ffn_w1, L0_ffn_w2, L0_ffn_bias), axis=-1)
    x = _layernorm(x + _L1_attn_ref(x, L1_attn_encoder_query, L1_attn_encoder_value, L1_attn_mn_w1, L1_attn_mn_b1, L1_attn_mn_w2, L1_attn_mn_b2, L1_attn_base_metric, L1_attn_decoder, L1_attn_hebbian_U, L1_attn_hebbian_V), axis=-1)
    x = _layernorm(x + _L1_xattn_ref(x, ctx_1024), axis=-1)
    x = _layernorm(x + _L1_ffn_ref(x, L1_ffn_w1, L1_ffn_b1, L1_ffn_w2, L1_ffn_b2), axis=-1)
    return x

_drawn_inputs = setup_inputs


def setup_inputs(seed=0):
    import zlib

    import numpy as np

    out = dict(_drawn_inputs(seed))
    spreads = {'L0_xattn_bq': (0.0, 0.1),
     'L0_xattn_bk': (0.0, 2.0),
     'L0_xattn_bv': (0.0, 0.1),
     'L0_xattn_bo': (0.0, 0.1),
     'L0_ffn_bias': (0.0, 0.1),
     'L1_attn_mn_b1': (0.0, 2.0),
     'L1_attn_mn_b2': (0.0, 2.0),
     'L1_attn_base_metric': (0.10000000149011612, 0.6)}
    factors = {'L0_ffn_w_router': 3.049,
     'L0_ffn_w1': 2.67,
     'L0_ffn_w2': 2.671,
     'L1_attn_encoder_query': 7.777,
     'L1_attn_encoder_value': 8.0,
     'L1_attn_mn_w1': 8.0,
     'L1_attn_mn_w2': 8.0,
     'L1_attn_decoder': 5.93,
     'L1_attn_hebbian_U': 64.0,
     'L1_attn_hebbian_V': 64.0,
     'L1_ffn_b1': 7.361,
     'L1_ffn_b2': 6.139}
    for name, (base, spread) in spreads.items():
        noise = np.random.default_rng([zlib.crc32(name.encode()), seed]).standard_normal(out[name].shape)
        drawn = base * np.exp(spread * noise) if base else spread * noise
        out[name] = jnp.asarray(drawn.astype(out[name].dtype))
    for name, factor in factors.items():
        out[name] = (out[name] * factor).astype(out[name].dtype)
    return out
```

```python
from contextlib import ExitStack

import concourse.bass as bass
from concourse import mybir

F32 = mybir.dt.float32
BF16 = mybir.dt.bfloat16
U32 = mybir.dt.uint32
ALU = mybir.AluOpType
ACT = mybir.ActivationFunctionType
AX = mybir.AxisListType

P = 128
B, T, D = 8, 128, 128
TOK = B * T
CTX = 77
PAIRS = B // 2
HEADS, HD, G, J = 16, 8, 4, 4
MAXROW = HD
LN_EPS = 1e-5
E, FF, CAP = 8, 512, 256
FC = FF // P
SLOTS = E * CAP
NH, HE, WIN, TOPK = 8, 16, 64, 32
G2 = NH // 4
HID = WIN
QUARTER = 32
SEEN = QUARTER + WIN
TX = T + WIN
NTILE = G2 * T // QUARTER
HALF = NTILE // 2 * SEEN
MASKED = -1e30
TAKEN = -2e30
ROUND = 12582912.0

PACK_A = [("wq", G * P), ("wk", G * P), ("wv", P), ("max_col", 1), ("ident", P), ("wq2", G * P), ("wk2", G * P),
          ("wv2", P), ("bq2", G), ("bk2", G), ("bv2", P), ("wo", P), ("bo", P), ("router", E)]
PACK_B = [("tri", P), ("iota_e", E), ("slot_e", E), ("ffn_bias", P), ("key_w", G2 * P), ("qv_w", 2 * P),
          ("mn_w1", G2 * HID), ("mn_b1", 1), ("mn_w2", G2 * P), ("mn_b2", G2), ("base_metric", G2),
          ("is_square", 1), ("sig_w", P), ("heb_u", G2 * P), ("heb_v", G2 * 64), ("decoder", P),
          ("mask", SEEN), ("w1f", FF), ("b1f", FC), ("w2f", FF), ("b2f", 1)]


def columns(pack):
    at, out = 0, {}
    for name, width in pack:
        out[name] = (at, width)
        at += width
    return out, at


COLS_A, WIDTH_A = columns(PACK_A)
COLS_B, WIDTH_B = columns(PACK_B)


def decoder_kernel(nc, x_rows, x_cols, ctx_rows, ctx_cols, pack_a, pack_b, w1, w2, out, xb_dram, y_dram):
    with ExitStack() as stack:
        made = {}

        def S(name):
            if name not in made:
                made[name] = stack.enter_context(nc.semaphore(name))
            return made[name]

        def sb(name, shape, dt=F32):
            return stack.enter_context(nc.sbuf_tensor(name, shape, dt))

        bank = [stack.enter_context(nc.psum_tensor(f"bank{i}", [P, 512], F32)) for i in range(8)]

        wa = sb("wa", [P, WIDTH_A])
        wb = sb("wb", [P, WIDTH_B])

        def A(name, rows=P):
            at, width = COLS_A[name]
            return wa[0:rows, at:at + width]

        def W(name, rows=P):
            at, width = COLS_B[name]
            return wb[0:rows, at:at + width]

        ident = A("ident")
        hid = sb("hid", [P, FC, TOK])
        w_div = hid[:, 0, :].rearrange("p (i f) -> p i f", i=2)
        w_int = hid[:, 1, :].rearrange("p (i f) -> p i f", i=2)
        w_clip = hid[:, 2, :].rearrange("p (i f) -> p i f", i=2)
        sig_p = hid[:, 0:2, :].rearrange("p g (b t) -> p g b t", b=B)
        ones_row = sb("ones_row", [1, P])
        ones_bf = sb("ones_bf", [P, P], BF16)
        tri_bf = sb("tri_bf", [P, P], BF16)
        neg_half = sb("neg_half", [P, B])
        half = sb("half", [P, B])
        tiny = sb("tiny", [P, 1])
        x3T_all = sb("x3T_all", [P, TOK])
        zeros = x3T_all

        xT_in = [sb(f"xT_in{p}", [P, T]) for p in (0, 1)]
        x_in = [sb(f"x_in{p}", [P, D]) for p in (0, 1)]
        cT_in = [sb(f"cT_in{p}", [P, CTX]) for p in (0, 1)]
        qT = {a: [sb(f"{a}_qT{p}", [P, G, T]) for p in (0, 1)] for a in ("self", "cross")}
        kT = {"self": [sb(f"self_kT{p}", [P, G, T]) for p in (0, 1)],
              "cross": [sb(f"cross_kT{p}", [P, G, CTX]) for p in (0, 1)]}
        v_aug = {a: [sb(f"{a}_v{p}", [P, HEADS, HD + 1]) for p in (0, 1)] for a in ("self", "cross")}
        maxes = {a: [sb(f"{a}_max{p}", [P, G, P]) for p in (0, 1)] for a in ("self", "cross")}
        probs = [sb(f"probs{j}", [P, G, T]) for j in range(J)]
        rec = [sb(f"rec{p}", [P, HEADS]) for p in (0, 1)]
        attn = [sb(f"attn{p}", [P, D]) for p in (0, 1)]
        bk2 = sb("bk2", [P, G])
        y_sum = [sb(f"y_sum{p}", [P, D]) for p in (0, 1)]
        stats = [sb(f"stats{p}", [P, 6]) for p in (0, 1)]
        mv = [sb(f"mv{p}", [P, 2]) for p in (0, 1)]
        var_eps = [sb(f"var_eps{p}", [P, 1]) for p in (0, 1)]
        rstd = [sb(f"rstd{p}", [P, 1]) for p in (0, 1)]
        x1 = [sb(f"x1_{p}", [P, D]) for p in (0, 1)]
        x1T = [sb(f"x1T{p}", [P, T]) for p in (0, 1)]
        a2T = [sb(f"a2T{p}", [P, T]) for p in (0, 1)]
        x2 = [sb(f"x2_{p}", [P, D]) for p in (0, 1)]
        x2T = [sb(f"x2T{p}", [P, T]) for p in (0, 1)]
        x2_all = sb("x2_all", [P, B, D])
        logits = sb("logits", [P, B, E])

        top8 = sb("top8", [P, B, 8])
        index8 = sb("index8", [P, B, 8], U32)
        index_f = sb("index_f", [P, B, 2])
        shifted = sb("shifted", [P, B, E])
        exps = sb("exps", [P, B, E])
        gap = sb("gap", [P, B])
        exp_gap = sb("exp_gap", [P, B])
        denom = sb("denom", [P, B])
        gate = sb("gate", [P, 2, B])
        onehot = [sb(f"onehot{k}", [P, B, E]) for k in (0, 1)]
        chosen = sb("chosen", [P, B, E], BF16)
        place = sb("place", [P, B, E])
        slot_of = sb("slot_of", [P, B, E])
        picked = [sb(f"picked{i}", [P, B, E]) for i in range(4)]
        place_k = sb("place_k", [P, 2, B])
        slot_k = sb("slot_k", [P, 2, B])
        fits = sb("fits", [P, 2, B])
        over = sb("over", [P, 2, B])
        put_f = sb("put_f", [P, 2, B])
        get_f = sb("get_f", [P, 2, B])
        put = sb("put", [P, 2, B], U32)
        get = sb("get", [P, 2, B], U32)
        gates = sb("gates", [P, 2, B])
        xb_in = [sb(f"xb_in{p}", [P, 2, D]) for p in (0, 1)]
        w1_in = [sb(f"w1_in{p}", [P, FF]) for p in (0, 1)]
        w2_in = [sb(f"w2_in{p}", [P, FC, D]) for p in (0, 1)]
        xbT = [sb(f"xbT{p}", [P, CAP]) for p in (0, 1)]
        hT = [sb(f"hT{p}", [P, FC, CAP]) for p in (0, 1)]
        yb = [sb(f"yb{p}", [P, 2, D]) for p in (0, 1)]
        got = [sb(f"got{k}", [P, B, D]) for k in (0, 1)]
        x2b = sb("x2b", [P, B, D])
        mix = [sb(f"mix{p}", [P, D]) for p in (0, 1)]

        x3 = [sb(f"x3_{p}", [P, D]) for p in (0, 1)]
        x3_all = sb("x3_all", [P, B, D])
        uT = sb("uT", [P, G2, B, T])
        sig = sb("sig", [P, G2, B])
        hidden = sb("hidden", [HID, B])
        pre = sb("pre", [P, G2])
        zm = sb("zm", [P, G2, B])
        zabs = sb("zabs", [P, G2, B])
        zexp = sb("zexp", [P, G2, B])
        zln = sb("zln", [P, G2, B])
        zpos = sb("zpos", [P, G2, B])
        metric = sb("metric", [P, G2, B])
        q_scale = sb("q_scale", [P, G2, B])
        q_bias = sb("q_bias", [P, G2, B])
        two_key = sb("two_key", [P, 1])
        not_square = sb("not_square", [P, 1])
        neg_square = sb("neg_square", [P, 1])
        heb = sb("heb", [P, G2, 64])
        k_all = sb("k_all", [P, G2, B, T])
        qs = [sb(f"qs{p}", [P, G2, T]) for p in (0, 1)]
        ks = [sb(f"ks{p}", [P, G2, TX]) for p in (0, 1)]
        x3T = [sb(f"x3T{p}", [P, TX]) for p in (0, 1)]
        q_tok = [sb(f"q_tok{p}", [P, D]) for p in (0, 1)]
        vw = [sb(f"vw{p}", [SEEN, 4, NH, HE + 1]) for p in (0, 1)]
        score = [sb(f"score{p}", [P, NTILE, SEEN]) for p in (0, 1)]
        work = [hT[p][:].rearrange("p c s -> p (c s)")[:, 0:NTILE * SEEN].rearrange("p (n w) -> p n w", w=SEEN)
                for p in (0, 1)]
        best = [sb(f"best{p}", [P, TOPK // 8, NTILE, 8]) for p in (0, 1)]
        infl = [sb(f"infl{p}", [P, NTILE, SEEN]) for p in (0, 1)]
        kept = [sb(f"kept{p}", [P, NTILE, SEEN]) for p in (0, 1)]
        keptT = hid[0:SEEN, 3, :].rearrange("p (n t) -> p n t", n=NTILE)
        qq = [sb(f"qq{p}", [P, D]) for p in (0, 1)]
        q_n2 = [sb(f"q_n2_{p}", [P, NH]) for p in (0, 1)]
        q_norm = [sb(f"q_norm{p}", [P, NH]) for p in (0, 1)]
        q_gate = [sb(f"q_gate{p}", [P, NH]) for p in (0, 1)]
        q_floor = [sb(f"q_floor{p}", [P, NH]) for p in (0, 1)]
        q_rec = [sb(f"q_rec{p}", [P, NH]) for p in (0, 1)]
        heb_scale = [sb(f"heb_scale{p}", [P, NH]) for p in (0, 1)]
        infl_sum = [sb(f"infl_sum{p}", [P, NH]) for p in (0, 1)]
        infl_rec = [sb(f"infl_rec{p}", [P, NH]) for p in (0, 1)]
        heb_out = [sb(f"heb_out{p}", [P, D]) for p in (0, 1)]
        context = [sb(f"context{p}", [P, D]) for p in (0, 1)]
        both = [sb(f"both{p}", [P, D]) for p in (0, 1)]
        sparse = [sb(f"sparse{p}", [P, D]) for p in (0, 1)]
        sparseT = [sb(f"sparseT{p}", [P, T]) for p in (0, 1)]

        cT_all = sb("cT_all", [P, B, CTX])
        c_all = sb("c_all", [CTX, B, D])
        x4 = [sb(f"x4_{p}", [P, D]) for p in (0, 1)]
        x4T = [sb(f"x4T{p}", [P, T]) for p in (0, 1)]
        neg_max = [sb(f"neg_max{p}", [P, 1]) for p in (0, 1)]
        pr = [sb(f"pr{p}", [P, CTX]) for p in (0, 1)]
        pr_sum = [sb(f"pr_sum{p}", [P, 1]) for p in (0, 1)]
        pr_rec = [sb(f"pr_rec{p}", [P, 1]) for p in (0, 1)]
        prT = [sb(f"prT{p}", [CTX, T]) for p in (0, 1)]
        x5 = [sb(f"x5_{p}", [P, D]) for p in (0, 1)]
        x5T = x2b[:].rearrange("p b d -> p (b d)")

        w_abs = sb("w_abs", [P, FC + 1])
        w_floor = sb("w_floor", [P, FC + 1])
        w_step = sb("w_step", [P, FC + 1])
        w1q = sb("w1q", [P, FF], BF16)
        w2q = sb("w2q", [P, FC, P], BF16)
        w_rec = sb("w_rec", [P, FC + 1])
        a_max = [sb(f"a_max{i}", [P, 1]) for i in (0, 1)]
        a_top = [sb(f"a_top{i}", [P, 1]) for i in (0, 1)]
        a_floor = [sb(f"a_floor{i}", [P, 1]) for i in (0, 1)]
        a_step = [sb(f"a_step{i}", [P, 1]) for i in (0, 1)]
        a_rec = [sb(f"a_rec{i}", [P, 1]) for i in (0, 1)]
        b_rec = [sb(f"b_rec{i}", [P, (FC, 1)[i]]) for i in (0, 1)]
        o_step = [sb(f"o_step{i}", [P, (FC, 1)[i]]) for i in (0, 1)]
        b_div = [sb(f"b_div{i}", [P, (FC, 1)[i]]) for i in (0, 1)]
        b_int = [sb(f"b_int{i}", [P, (FC, 1)[i]]) for i in (0, 1)]
        b_q = [sb(f"b_q{i}", [P, (FC, 1)[i]]) for i in (0, 1)]
        xq = x3_all[:].rearrange("p b d -> p (b d)").bitcast(BF16)[:, 0:TOK]
        h_max = sb("h_max", [P, 8])
        hq = uT[:].rearrange("p g b t -> p (g b t)").bitcast(BF16).rearrange("p (c t) -> p c t", c=FC)
        ff_out = got[0][:].rearrange("p b d -> p (b d)")
        zT = got[1][:].rearrange("p b d -> p (b d)")
        fstats = sb("fstats", [P, B, 6])
        fmv = sb("fmv", [P, B, 2])
        fvar = sb("fvar", [P, B])
        frstd = sb("frstd", [P, B])
        final = x2_all

        block = stack.enter_context(nc.Block())

        SCALE = {"self": 1.0 / float(D) ** 0.5, "cross": 1.0 / float(HD) ** 0.5}
        KEYS = {"self": T, "cross": CTX}
        KINDS = ("self", "cross")
        MISC = (4, 5)
        WIDE = (6, 7)

        def wait_apart(engine, name, value):
            engine.wait_ge(S(name), value)
            engine.sem_inc(S("wait_passed"), 1)

        TURNS = {"x1": (0, 6, 0), "attn2": (0, 6, 1), "x2": (0, 6, 2), "x3": (24, 2, 0),
                 "sparse": (32, 8, 0), "x4": (32, 8, 1), "pr": (32, 8, 2), "x5": (32, 8, 3)}

        def turned(name, t, p):
            before, per, which = TURNS[name]
            return t * per + (before + 2 * which + p + 1)

        @block.sync
        def _(sp):
            sp.dma_start(xT_in[0][:], x_cols[0]).then_inc(S("xT_loaded0"), 16)
            sp.dma_start(xT_in[1][:], x_cols[1]).then_inc(S("xT_loaded1"), 16)
            sp.dma_start(wa[:, 0:COLS_A["wq2"][0]], pack_a[:, 0:COLS_A["wq2"][0]]).then_inc(S("wa_loaded"), 16)
            for p in (0, 1):
                sp.dma_start(x_in[p][:], x_rows[p]).then_inc(S(f"x_loaded{p}"), 16)
                sp.dma_start(cT_in[p][:], ctx_cols[p]).then_inc(S(f"cT_loaded{p}"), 16)
            sp.dma_start(wa[:, COLS_A["wq2"][0]:WIDTH_A], pack_a[:, COLS_A["wq2"][0]:WIDTH_A]).then_inc(S("wa2_loaded"), 16)
            sp.dma_start(wb[:], pack_b).then_inc(S("wb_loaded"), 16)
            sp.dma_start(cT_all[:], ctx_cols.rearrange("b d c -> d b c")).then_inc(S("ctx_loaded"), 16)
            sp.dma_start(c_all[:], ctx_rows.rearrange("b c d -> c b d")).then_inc(S("ctx_loaded"), 16)
            sp.wait_ge(S("zeros_ready"), 1)
            for h in (0, 1):
                sp.dma_start(xb_dram[h * SLOTS // 2:(h + 1) * SLOTS // 2, :].rearrange("(p r) d -> p (r d)", p=P),
                             zeros[:]).then_inc(S("xb_zeroed"), 16)
            for p in (0, 1):
                sp.dma_start(w1_in[p][:], w1[p]).then_inc(S(f"w_loaded{p}"), 16)
                sp.dma_start(w2_in[p][:], w2[p]).then_inc(S(f"w_loaded{p}"), 16)
            with sp.Fori(0, PAIRS - 1) as t:
                for p in (0, 1):
                    n = t * 2 + p + 1
                    sp.wait_ge(S("self_v_done"), n)
                    sp.dma_start(xT_in[p][:], x_cols[bass.ds(t * 2 + (2 + p), 1)].rearrange("b d t -> (b d) t")
                                 ).then_inc(S(f"xT_loaded{p}"), 16)
                    sp.wait_ge(S("self_sum_done"), n)
                    sp.dma_start(x_in[p][:], x_rows[bass.ds(t * 2 + (2 + p), 1)].rearrange("b t d -> (b t) d")
                                 ).then_inc(S(f"x_loaded{p}"), 16)
                    sp.wait_ge(S("cross_v_done"), n)
                    sp.dma_start(cT_in[p][:], ctx_cols[bass.ds(t * 2 + (2 + p), 1)].rearrange("b d c -> (b d) c")
                                 ).then_inc(S(f"cT_loaded{p}"), 16)
            sp.wait_ge(S("scattered"), 16 * 2 * B)
            with sp.Fori(0, PAIRS) as t:
                for p in (0, 1):
                    e = t * 2 + p
                    sp.wait_ge(S("xb_free"), e + 1)
                    sp.dma_start(xb_in[p][:], xb_dram[bass.ds(e * CAP, CAP), :].rearrange("(h s) d -> s h d", h=2)
                                 ).then_inc(S(f"xb_loaded{p}"), 16)
                for p in (0, 1):
                    e = t * 2 + p
                    sp.wait_ge(S("yb_ready"), e + 1)
                    sp.dma_start(y_dram[bass.ds(e * CAP, CAP), :].rearrange("(h s) d -> s h d", h=2), yb[p][:]
                                 ).then_inc(S(f"y_stored{p}"), 16)
            sp.wait_ge(S("final_ready"), B)
            sp.dma_start(out.rearrange("b t d -> t b d"), final[:]).then_inc(S("out_stored"), 16)
            sp.wait_ge(S("out_stored"), 16)

        @block.gpsimd
        def _(pool):
            g = nc.gpsimd
            g.memset(neg_half[:], -0.5).then_inc(S("pool_consts"), 1)
            g.memset(half[:], 0.5).then_inc(S("pool_consts"), 1)
            g.memset(ones_row[:], 1.0).then_inc(S("pool_consts"), 1)
            g.memset(ones_bf[:], 1.0).then_inc(S("pool_consts"), 1)
            g.memset(tiny[:], 1e-8).then_inc(S("pool_consts"), 1)
            for a in KINDS:
                for p in (0, 1):
                    g.memset(maxes[a][p][:], 0.0).then_inc(S("pool_consts"), 1)
                    g.memset(v_aug[a][p][:, :, HD:HD + 1], 1.0).then_inc(S("pool_consts"), 1)
            for p in (0, 1):
                g.memset(vw[p][:, :, :, HE:HE + 1], 1.0).then_inc(S("pool_consts"), 1)
            g.memset(zeros[:], 0.0).then_inc(S("zeros_ready"), 1)

            def power(n, p):
                pool.wait_ge(S("ln_var"), n)
                g.tensor_tensor(rstd[p][:], var_eps[p][:], neg_half[:, 0:1], ALU.pow).then_inc(S("ln_rstd"), 1)

            with pool.Fori(0, PAIRS) as t:
                for i in (1, 3):
                    for p in (0, 1):
                        power(t * 4 + (i + p), p)
                for p in (0, 1):
                    pool.wait_ge(S("x2_ready"), t * 2 + p + 1)
                    g.tensor_copy(x2_all[:, bass.ds(t * 2 + p, 1), :], x2[p][:].rearrange("q (b d) -> q b d", b=1)
                                  ).then_inc(S("x2_kept"), 1)

            pool.wait_ge(S("xb_zeroed"), 32)
            pool.wait_ge(S("put_ready"), 1)
            pool.wait_ge(S("x2_kept"), B)
            for b in range(B):
                for k in (0, 1):
                    g.indirect_dma_start(out=xb_dram, out_offset=bass.IndirectOffsetOnAxis(ap=put[:, k, b:b + 1], axis=0),
                                         in_=x2_all[:, b, :], in_offset=None, bounds_check=SLOTS - 1,
                                         oob_is_err=False).then_inc(S("scattered"), 16)
            pool.wait_ge(S("wb_loaded"), 16)
            g.tensor_tensor(x2b[:], x2_all[:], W("ffn_bias").rearrange("p (b d) -> p b d", b=1).broadcast_to([P, B, D]),
                            ALU.add).then_inc(S("x2b_ready"), 1)
            for p in (0, 1):
                pool.wait_ge(S(f"y_stored{p}"), 16 * PAIRS)
            pool.wait_ge(S("put_ready"), 1)
            for b in range(B):
                for k in (0, 1):
                    g.indirect_dma_start(out=got[k][:, b, :], out_offset=None, in_=y_dram,
                                         in_offset=bass.IndirectOffsetOnAxis(ap=get[:, k, b:b + 1], axis=0),
                                         bounds_check=SLOTS - 1, oob_is_err=False).then_inc(S("gathered"), 16)
            with pool.Fori(0, PAIRS) as t:
                for p in (0, 1):
                    power(t * 2 + (2 * B + 1 + p), p)
                for p in (0, 1):
                    pool.wait_ge(S("x3_ready"), t * 2 + p + 1)
                    g.tensor_copy(x3_all[:, bass.ds(t * 2 + p, 1), :], x3[p][:].rearrange("q (b d) -> q b d", b=1)
                                  ).then_inc(S("x3_kept"), 1)

            pool.wait_ge(S("k_all_ready"), 1)
            pool.wait_ge(S("turned_copied"), turned("x3", PAIRS - 1, 1))
            with pool.Fori(0, PAIRS) as t:
                for p in (0, 1):
                    b = t * 2 + p
                    n = b + 1
                    pool.wait_ge(S("win_free"), n)
                    g.tensor_copy(x3T[p][:, 0:T], x3T_all[:, bass.ds(b * T, T)]).then_inc(S("x3T_here"), 1)
                    g.tensor_copy(x3T[p][:, T:TX], x3T_all[:, bass.ds(b * T + (T - 1), 1)].broadcast_to([P, WIN])
                                  ).then_inc(S("x3T_here"), 1)
                    g.tensor_copy(ks[p][:, :, 0:T], k_all[:, :, bass.ds(b, 1), :].rearrange("q g b t -> q g (b t)")
                                  ).then_inc(S("ks_here"), 1)
                    g.tensor_copy(ks[p][:, :, T:TX], k_all[:, :, bass.ds(b, 1), T - 1:T]
                                  .rearrange("q g b t -> q g (b t)").broadcast_to([P, G2, WIN])
                                  ).then_inc(S("ks_here"), 1)
                for p in (0, 1):
                    n = t * 2 + p + 1
                    pool.wait_ge(S("qv_ready"), 2 * n)
                    g.tensor_tensor(qq[p][:], q_tok[p][:], q_tok[p][:], ALU.mult).then_inc(S("qq_ready"), 1)
                    pool.wait_ge(S("sorted"), (n - 1) * 64 + NTILE)
                    g.tensor_tensor(infl[p][:], best[p][:, 0, :, 0:1].broadcast_to([P, NTILE, SEEN]), score[p][:],
                                    ALU.subtract).then_inc(S("dist2_ready"), 1)
                    pool.wait_ge(S("q_n2_ready"), n)
                    g.tensor_tensor(q_norm[p][:], q_n2[p][:], half[:, 0:NH], ALU.pow).then_inc(S("q_norm_ready"), 1)
                for p in (0, 1):
                    power(t * 4 + (3 * B + 1 + p), p)
                for p in (0, 1):
                    power(t * 4 + (3 * B + 3 + p), p)

            for i in (0, 1):
                pool.wait_ge(S(f"a_max_ready{i}"), 1)
                g.partition_all_reduce(a_top[i][:], a_max[i][:], P, bass.bass_isa.ReduceOp.max).then_inc(S(f"a_top_ready{i}"), 1)
            pool.wait_ge(S("final_var"), 1)
            g.tensor_tensor(frstd[:], fvar[:], neg_half[:], ALU.pow).then_inc(S("final_rstd"), 1)

        @block.tensor
        def _(pe):
            mm = pe.matmul

            def project(a, what, n, p, src, dst_bank):
                w = A({"self": {"q": "wq", "k": "wk"}, "cross": {"q": "wq2", "k": "wk2"}}[a][what])
                width = src.shape[1]
                for gi in range(G):
                    last = mm(bank[dst_bank][:, gi * width:(gi + 1) * width], w[:, gi * P:(gi + 1) * P], src,
                              start=True, stop=True)
                last.then_inc(S(f"{a}_{what}_proj"), 1)

            def score_units(lhs, rhs, rows, width, name):
                for j0 in (0, 2):
                    for gi in range(G):
                        for j in (j0, j0 + 1):
                            last = mm(bank[j][0:rows, gi * width:(gi + 1) * width],
                                      lhs[32 * j:32 * j + 32, gi, :], rhs[32 * j:32 * j + 32, gi, :],
                                      start=True, stop=True)
                            if gi == G - 1:
                                last.then_inc(S(name), 1)

            def max_scores(a, n, m, p):
                pe.wait_ge(S(f"{a}_q_ready"), n)
                pe.wait_ge(S(f"{a}_k_ready"), n)
                if p == 1:
                    pe.wait_ge(S("max_ready"), (m - 1) * 4)
                score_units(qT[a][p], kT[a][p], T, KEYS[a], "scores")

            def turn_maxes(a, m, p):
                pe.wait_ge(S("max_ready"), m * 4)
                for gi in range(G):
                    last = pe.transpose(bank[WIDE[p]][:, gi * T:(gi + 1) * T], maxes[a][p][:, gi, :], ident)
                last.then_inc(S("max_turned"), 1)

            def exp_scores(a, m, p, j0):
                K = KEYS[a]
                if j0 == 0:
                    pe.wait_ge(S("qm_ready"), m)
                for gi in range(G):
                    for j in (j0, j0 + 1):
                        last = mm(bank[j][0:K, gi * T:(gi + 1) * T], kT[a][p][32 * j:32 * j + 32, gi, :],
                                  qT[a][p][32 * j:32 * j + 32, gi, :], start=True, stop=True)
                        if gi == G - 1:
                            last.then_inc(S("scoresT"), 1)

            def weigh(a, n, m, p, j0):
                K = KEYS[a]
                for j in (j0, j0 + 1):
                    pe.wait_ge(S("probs_ready"), (m - 1) * 4 + (j + 1))
                    if j == 0:
                        pe.wait_ge(S(f"{a}_v_done"), n)
                    for gi in range(G):
                        h = 4 * gi + j
                        last = mm(bank[WIDE[p]][:, h * (HD + 1):(h + 1) * (HD + 1)], probs[j][0:K, gi, :],
                                  v_aug[a][p][0:K, h, :], start=True, stop=True)
                    last.then_inc(S("weighed"), 1)

            def attend(a, n, m):
                pe.wait_ge(S("max_ready"), (m + 1) * 4)
                exp_scores(a, m, 0, 0)
                exp_scores(a, m, 0, 2)
                weigh(a, n, m, 0, 0)
                exp_scores(a, m + 1, 1, 0)
                weigh(a, n, m, 0, 2)
                exp_scores(a, m + 1, 1, 2)
                weigh(a, n + 1, m + 1, 1, 0)
                weigh(a, n + 1, m + 1, 1, 2)

            def turn(name, n, src, bank_no, rows=P):
                pe.wait_ge(S(f"{name}_ready"), n)
                pe.transpose(bank[bank_no][0:rows, 0:P], src, ident).then_inc(S("turned"), 1)

            pe.wait_ge(S("wa_loaded"), 16)
            pe.wait_ge(S("pool_consts"), 15)

            pe.wait_ge(S("w_clip_ready"), 1)
            for i in (0, 1):
                for c in range(FC):
                    last = pe.transpose(bank[i][:, c * P:(c + 1) * P], w_clip[:, i, c * P:(c + 1) * P], ident)
                last.then_inc(S("wq_turned"), 1)
            pe.wait_ge(S("wq_kept"), 2)

            with pe.Fori(0, PAIRS) as t:
                n0 = t * 2 + 1
                for p in (0, 1):
                    pe.wait_ge(S(f"xT_loaded{p}"), (t + 1) * 16)
                    project("self", "q", n0 + p, p, xT_in[p][:], MISC[p])
                    project("self", "k", n0 + p, p, xT_in[p][:], WIDE[p])
                for p in (0, 1):
                    pe.wait_ge(S("self_q_ready"), n0 + p)
                    mm(bank[MISC[p]][:, 0:D], xT_in[p][:], A("wv"), start=True, stop=True).then_inc(S("self_v_proj"), 1)
                for p in (0, 1):
                    max_scores("self", n0 + p, t * 4 + (1 + p), p)
                pe.wait_ge(S("wa2_loaded"), 16)
                for p in (0, 1):
                    pe.wait_ge(S("self_v_done"), n0 + p)
                    pe.wait_ge(S(f"cT_loaded{p}"), (t + 1) * 16)
                    project("cross", "k", n0 + p, p, cT_in[p][:], MISC[p])
                for p in (0, 1):
                    turn_maxes("self", t * 4 + (1 + p), p)
                attend("self", n0, t * 4 + 1)
                for p in (0, 1):
                    pe.wait_ge(S("cross_k_ready"), n0 + p)
                    mm(bank[MISC[p]][0:CTX, 0:D], cT_in[p][:], A("wv2"), start=True, stop=False)
                    mm(bank[MISC[p]][0:CTX, 0:D], ones_row[0:1, 0:CTX], A("bv2", 1), start=False, stop=True
                       ).then_inc(S("cross_v_proj"), 1)
                for p in (0, 1):
                    pe.wait_ge(S("cross_v_done"), n0 + p)
                    turn("x1", n0 + p, x1[p][:], MISC[p])
                for p in (0, 1):
                    pe.wait_ge(S("turned_copied"), turned("x1", t, p))
                    project("cross", "q", n0 + p, p, x1T[p][:], WIDE[p])
                for p in (0, 1):
                    max_scores("cross", n0 + p, t * 4 + (3 + p), p)
                for p in (0, 1):
                    turn_maxes("cross", t * 4 + (3 + p), p)
                attend("cross", n0, t * 4 + 3)
                for p in (0, 1):
                    turn("attn2", n0 + p, attn[p][:], MISC[p])
                for p in (0, 1):
                    pe.wait_ge(S("turned_copied"), turned("attn2", t, p))
                    mm(bank[MISC[p]][:, 0:D], a2T[p][:], A("wo"), start=True, stop=False)
                    mm(bank[MISC[p]][:, 0:D], ones_row[:], A("bo", 1), start=False, stop=True).then_inc(S("wo_done"), 1)
                for p in (0, 1):
                    turn("x2", n0 + p, x2[p][:], WIDE[p])
                for p in (0, 1):
                    pe.wait_ge(S("turned_copied"), turned("x2", t, p))
                    mm(bank[MISC[p]][:, 0:E], x2T[p][:], A("router"), start=True, stop=True).then_inc(S("routed"), 1)
                pe.wait_ge(S("logits_ready"), t * 2 + 2)

            pe.wait_ge(S("chosen_ready"), 1)
            pe.wait_ge(S("tri_ready"), 1)
            mm(bank[0][:, 0:B * E], tri_bf[:], chosen[:].rearrange("p b e -> p (b e)"), start=True, stop=False)
            for b in range(B - 1):
                later = B - 1 - b
                last = mm(bank[0][:, (b + 1) * E:B * E], ones_bf[:], chosen[:, b:b + 1, :].broadcast_to([P, later, E]),
                          start=False, stop=(b == B - 2))
            last.then_inc(S("places"), 1)

            pe.wait_ge(S("place_ready"), 1)
            with pe.Fori(0, PAIRS) as t:
                for p in (0, 1):
                    e1 = t * 2 + p + 1
                    pe.wait_ge(S(f"xb_loaded{p}"), (t + 1) * 16)
                    for h in (0, 1):
                        last = pe.transpose(bank[p][:, h * P:(h + 1) * P], xb_in[p][:, h, :], ident)
                    last.then_inc(S("xb_turned"), 1)
                for p in (0, 1):
                    e1 = t * 2 + p + 1
                    pe.wait_ge(S("xbT_ready"), e1)
                    pe.wait_ge(S(f"w_loaded{p}"), (t + 1) * 32)
                    for c in range(FC):
                        last = mm(bank[2 + 2 * p + c // 2][:, (c % 2) * CAP:(c % 2 + 1) * CAP],
                                  w1_in[p][:, c * P:(c + 1) * P], xbT[p][:], start=True, stop=True)
                        if c % 2:
                            last.then_inc(S("hidden_done"), 1)
                for p in (0, 1):
                    e1 = t * 2 + p + 1
                    pe.wait_ge(S("hT_ready"), e1 * 2)
                    for h in (0, 1):
                        for c in range(FC):
                            last = mm(bank[6 + p][:, h * D:(h + 1) * D], hT[p][:, c, h * P:(h + 1) * P],
                                      w2_in[p][:, c, :], start=(c == 0), stop=(c == FC - 1))
                    last.then_inc(S("y_done"), 1)

            with pe.Fori(0, PAIRS) as t:
                for p in (0, 1):
                    turn("x3", t * 2 + p + 1, x3[p][:], p)
                pe.wait_ge(S("turned_copied"), turned("x3", t, 1))

            pe.wait_ge(S("turned_copied"), turned("x3", PAIRS - 1, 1))
            pe.wait_ge(S("yb_ready"), E)
            for gi in range(G2):
                for h in (0, 1):
                    mm(bank[4 + 2 * gi + h][:], W("key_w")[:, gi * P:(gi + 1) * P], x3T_all[:, h * 512:(h + 1) * 512],
                       start=True, stop=True).then_inc(S("u_done"), 1)
            for gi in range(G2):
                last = mm(bank[2][:, gi * 64:(gi + 1) * 64], W("heb_u", 16)[:, gi * P:(gi + 1) * P],
                          W("heb_v", 16)[:, gi * 64:(gi + 1) * 64], start=True, stop=True)
            last.then_inc(S("heb_done"), 1)
            pe.wait_ge(S("sig_ready"), 1)
            for gi in range(G2):
                last = mm(bank[0][0:HID, 0:B], W("mn_w1")[:, gi * HID:(gi + 1) * HID], sig[:, gi, :],
                          start=(gi == 0), stop=(gi == G2 - 1))
            last.then_inc(S("mn_hidden"), 1)
            pe.wait_ge(S("mn_gelu"), 1)
            for gi in range(G2):
                last = mm(bank[1][:, gi * B:(gi + 1) * B], W("mn_w2", HID)[:, gi * P:(gi + 1) * P], hidden[:],
                          start=True, stop=True)
            last.then_inc(S("mn_mod"), 1)

            pe.wait_ge(S("heb_kept"), 1)
            pe.wait_ge(S("ctx_loaded"), 32)
            with pe.Fori(0, PAIRS) as t:
                n0 = t * 2 + 1
                for p in (0, 1):
                    n = n0 + p
                    pe.wait_ge(S("x3T_here"), 2 * n)
                    mm(bank[6 + p][:, 0:D], x3T[p][:, 0:T], W("qv_w")[:, 0:D], start=True, stop=True
                       ).then_inc(S("q_done"), 1)
                    if p == 1:
                        pe.wait_ge(S("qv_ready"), 2 * (n - 1))
                    for q in range(4):
                        last = mm(bank[0][0:SEEN, q * D:(q + 1) * D], x3T[p][:, q * QUARTER:q * QUARTER + SEEN],
                                  W("qv_w")[:, D:2 * D], start=True, stop=True)
                    last.then_inc(S("v_done"), 1)
                    pe.wait_ge(S("ks_here"), 2 * n)
                    if p == 1:
                        pe.wait_ge(S("score_ready"), 2 * (n - 1))
                    wait_apart(pe, "qs_ready", n * 2)
                    for q in range(4):
                        for gi in range(G2):
                            at = (gi * 2 + q % 2) * SEEN
                            for j in range(4):
                                rows = slice(32 * j, 32 * j + 32)
                                last = mm(bank[1 + q // 2][rows, at:at + SEEN],
                                          qs[p][rows, gi, q * QUARTER:(q + 1) * QUARTER],
                                          ks[p][rows, gi, q * QUARTER:q * QUARTER + SEEN], start=True, stop=True)
                        if q % 2:
                            last.then_inc(S("win_scores"), 1)
                for p in (0, 1):
                    n = n0 + p
                    pe.wait_ge(S("kept_ready"), n)
                    if p == 1:
                        pe.wait_ge(S("keptT_ready"), 2 * (n - 1))
                    for h in (0, 1):
                        for i in range(4):
                            last = pe.transpose(bank[3 + h][0:SEEN, i * P:(i + 1) * P], kept[p][:, 4 * h + i, :], ident)
                        last.then_inc(S("kept_turned"), 1)
                    pe.wait_ge(S("keptT_ready"), 2 * n)
                    if p == 1:
                        pe.wait_ge(S("both_ready"), n - 1)
                    for q in range(4):
                        for h in range(NH):
                            gi, j = h // 4, h % 4
                            mm(bank[5][32 * q:32 * q + 32, h * (HE + 1):(h + 1) * (HE + 1)],
                               keptT[:, q // 2 * 4 + gi * 2 + q % 2, 32 * j:32 * j + 32], vw[p][:, q, h, :],
                               start=True, stop=True)
                    for gi in range(G2):
                        last = mm(bank[5][:, 256 + gi * 64:256 + (gi + 1) * 64], ks[p][:, gi, 0:T], heb[:, gi, :],
                                  start=True, stop=True)
                    last.then_inc(S("win_context"), 1)
                for p in (0, 1):
                    turn("sparse", n0 + p, sparse[p][:], 6 + p)
                for p in (0, 1):
                    pe.wait_ge(S("turned_copied"), turned("sparse", t, p))
                    mm(bank[6 + p][:, 0:D], sparseT[p][:], W("decoder"), start=True, stop=True).then_inc(S("decoded"), 1)
                for p in (0, 1):
                    turn("x4", n0 + p, x4[p][:], 6 + p)
                for p in (0, 1):
                    pe.wait_ge(S("turned_copied"), turned("x4", t, p))
                    mm(bank[6 + p][:, 0:CTX], x4T[p][:],
                       cT_all[:, bass.ds(t * 2 + p, 1), :].rearrange("q b c -> q (b c)"),
                       start=True, stop=True).then_inc(S("plain_scores"), 1)
                for p in (0, 1):
                    pe.wait_ge(S("pr_ready"), n0 + p)
                    pe.transpose(bank[6 + p][0:CTX, 0:T], pr[p][:], ident).then_inc(S("turned"), 1)
                for p in (0, 1):
                    pe.wait_ge(S("turned_copied"), turned("pr", t, p))
                    mm(bank[6 + p][:, 0:D], prT[p][:],
                       c_all[:, bass.ds(t * 2 + p, 1), :].rearrange("q b d -> q (b d)"),
                       start=True, stop=True).then_inc(S("plain_out"), 1)
                for p in (0, 1):
                    turn("x5", n0 + p, x5[p][:], 6 + p)
                pe.wait_ge(S("turned_copied"), turned("x5", t, 1))

            pe.wait_ge(S("xq_ready"), 1)
            pe.wait_ge(S("turned_copied"), turned("x5", PAIRS - 1, 1))
            for c in range(FC):
                for h in (0, 1):
                    mm(bank[2 * c + h][:], w1q[:, c * P:(c + 1) * P], xq[:, h * 512:(h + 1) * 512],
                       start=True, stop=True).then_inc(S("ff_hidden"), 1)
            for c in range(FC):
                pe.wait_ge(S("hq_ready"), c + 1)
                for h in (0, 1):
                    last = mm(bank[h][:], w2q[:, c, :], hq[:, c, h * 512:(h + 1) * 512],
                              start=(c == 0), stop=(c == FC - 1))
                    if c == FC - 1:
                        last.then_inc(S("ff_done"), 1)
            for h in (0, 1):
                pe.wait_ge(S("zT_ready"), h + 1)
                for i in range(4):
                    last = pe.transpose(bank[2 + h][:, i * D:(i + 1) * D], zT[:, (4 * h + i) * T:(4 * h + i + 1) * T], ident)
                last.then_inc(S("z_turned"), 1)

        @block.scalar
        def _(act):
            sc = nc.scalar

            def copy_turned(name, t, p, dst, bank_no, rows=P):
                act.wait_ge(S("turned"), turned(name, t, p))
                sc.activation(dst, bank[bank_no][0:rows, 0:P], ACT.Copy).then_inc(S("turned_copied"), 1)

            def exps_of(a, n, p, j0):
                K = KEYS[a]
                for j in (j0, j0 + 1):
                    act.wait_ge(S("scoresT"), (n - 1) * 4 + (j + 1))
                    if p == 1:
                        act.wait_ge(S("weighed"), (n - 2) * 4 + (j + 1))
                    sc.activation(probs[j][0:K, :, :].rearrange("p g t -> p (g t)"), bank[j][0:K, :], ACT.Exp,
                                  scale=SCALE[a]).then_inc(S("probs_ready"), 1)

            act.wait_ge(S("wa_loaded"), 16)
            for i in (0, 1):
                act.wait_ge(S("wq_turned"), i + 1)
                dst = w1q[:] if i == 0 else w2q[:].rearrange("p c d -> p (c d)")
                sc.activation(dst, bank[i][:], ACT.Copy).then_inc(S("wq_kept"), 1)
            with act.Fori(0, PAIRS) as t:
                n0 = t * 2 + 1
                for p in (0, 1):
                    act.wait_ge(S("self_q_proj"), n0 + p)
                    sc.activation(qT["self"][p][:].rearrange("q g t -> q (g t)"), bank[MISC[p]][:], ACT.Copy
                                  ).then_inc(S("self_q_ready"), 1)
                    act.wait_ge(S("self_k_proj"), n0 + p)
                    sc.activation(kT["self"][p][:].rearrange("q g t -> q (g t)"), bank[WIDE[p]][:], ACT.Identity,
                                  bias=A("max_col")).then_inc(S("self_k_ready"), 1)
                for p in (0, 1):
                    act.wait_ge(S("self_v_proj"), n0 + p)
                    sc.activation(v_aug["self"][p][:, :, 0:HD], bank[MISC[p]][:, 0:D].rearrange("q (h d) -> q h d", h=HEADS),
                                  ACT.Copy).then_inc(S("self_v_done"), 1)
                for p in (0, 1):
                    exps_of("self", t * 4 + (1 + p), p, 0)
                    exps_of("self", t * 4 + (1 + p), p, 2)
                for p in (0, 1):
                    act.wait_ge(S("cross_v_proj"), n0 + p)
                    sc.activation(v_aug["cross"][p][0:CTX, :, 0:HD],
                                  bank[MISC[p]][0:CTX, 0:D].rearrange("q (h d) -> q h d", h=HEADS),
                                  ACT.Copy).then_inc(S("cross_v_done"), 1)
                for p in (0, 1):
                    copy_turned("x1", t, p, x1T[p][:], MISC[p])
                for p in (0, 1):
                    exps_of("cross", t * 4 + (3 + p), p, 0)
                    exps_of("cross", t * 4 + (3 + p), p, 2)
                for p in (0, 1):
                    copy_turned("attn2", t, p, a2T[p][:], MISC[p])
                for p in (0, 1):
                    copy_turned("x2", t, p, x2T[p][:], WIDE[p])
                for p in (0, 1):
                    act.wait_ge(S("routed"), n0 + p)
                    sc.activation(logits[:, bass.ds(t * 2 + p, 1), :].rearrange("q b e -> q (b e)"),
                                  bank[MISC[p]][:, 0:E], ACT.Copy).then_inc(S("logits_ready"), 1)

            act.wait_ge(S("shifted_ready"), 2)
            sc.activation(exps[:], shifted[:], ACT.Exp).then_inc(S("exps_ready"), 1)
            sc.activation(exp_gap[:], gap[:], ACT.Exp).then_inc(S("exps_ready"), 1)

            def expert_pair(t, more):
                for p in (0, 1):
                    e1 = t * 2 + p + 1
                    act.wait_ge(S("xb_turned"), e1)
                    sc.activation(xbT[p][:], bank[p][:, 0:CAP], ACT.Copy).then_inc(S("xbT_ready"), 1)
                for p in (0, 1):
                    e1 = t * 2 + p + 1
                    for h in (0, 1):
                        act.wait_ge(S("hidden_done"), (e1 - 1) * 2 + (h + 1))
                        sc.activation(hT[p][:, 2 * h:2 * h + 2, :].rearrange("q c s -> q (c s)"), bank[2 + 2 * p + h][:],
                                      ACT.Gelu_apprx_tanh).then_inc(S("hT_ready"), 1)
                for p in (0, 1):
                    e1 = t * 2 + p + 1
                    if more:
                        act.wait_ge(S("y_done"), e1)
                        act.dma_start(w1_in[p][:], w1[bass.ds(t * 2 + (2 + p), 1)].rearrange("e d f -> (e d) f")
                                      ).then_inc(S(f"w_loaded{p}"), 16)
                        act.dma_start(w2_in[p][:], w2[bass.ds(t * 2 + (2 + p), 1)].rearrange("e f c d -> (e f) c d")
                                      ).then_inc(S(f"w_loaded{p}"), 16)

            with act.Fori(0, PAIRS - 1) as t:
                expert_pair(t, True)
            expert_pair(PAIRS - 1, False)

            with act.Fori(0, PAIRS) as t:
                for p in (0, 1):
                    copy_turned("x3", t, p, x3T_all[:, bass.ds((t * 2 + p) * T, T)], p)
            for gi in range(G2):
                for h in (0, 1):
                    act.wait_ge(S("u_done"), gi * 2 + h + 1)
                    sc.activation(uT[:, gi, 4 * h:4 * h + 4, :].rearrange("q b t -> q (b t)"), bank[4 + 2 * gi + h][:],
                                  ACT.Relu).then_inc(S("uT_ready"), 1)
            act.wait_ge(S("heb_done"), 1)
            sc.activation(heb[:].rearrange("q g c -> q (g c)"), bank[2][:, 0:G2 * 64], ACT.Copy).then_inc(S("heb_kept"), 1)
            act.wait_ge(S("mn_hidden"), 1)
            sc.activation(hidden[:], bank[0][0:HID, 0:B], ACT.Gelu, bias=W("mn_b1", HID)).then_inc(S("mn_gelu"), 1)
            act.wait_ge(S("zabs_ready"), 1)
            sc.activation(zexp[:], zabs[:], ACT.Exp, scale=-1.0).then_inc(S("zexp_ready"), 1)
            act.wait_ge(S("zexp_ready"), 1)
            sc.activation(zln[:], zexp[:], ACT.Ln, bias=1.0).then_inc(S("zln_ready"), 1)

            act.wait_ge(S("q_coef_ready"), 2)
            with act.Fori(0, PAIRS) as t:
                n0 = t * 2 + 1
                for p in (0, 1):
                    b = t * 2 + p
                    act.wait_ge(S("win_free"), n0 + p)
                    for gi in range(G2):
                        sc.activation(qs[p][:, gi, :], uT[:, gi, bass.ds(b, 1), :].rearrange("q b t -> q (b t)"),
                                      ACT.Identity, bias=q_bias[:, gi, bass.ds(b, 1)],
                                      scale=q_scale[:, gi, bass.ds(b, 1)]).then_inc(S("qs_ready"), 1)
                for p in (0, 1):
                    n = n0 + p
                    act.wait_ge(S("q_done"), n)
                    sc.activation(q_tok[p][:], bank[6 + p][:, 0:D], ACT.Relu).then_inc(S("qv_ready"), 1)
                    act.wait_ge(S("v_done"), n)
                    sc.activation(vw[p][:, :, :, 0:HE], bank[0][0:SEEN, :].rearrange("q (s h e) -> q s h e", s=4, h=NH),
                                  ACT.Relu).then_inc(S("qv_ready"), 1)
                for p in (0, 1):
                    n = n0 + p
                    act.wait_ge(S("dist2_ready"), n)
                    sc.activation(infl[p][:], infl[p][:], ACT.Sqrt, bias=tiny[:]).then_inc(S("dist_ready"), 1)
                for p in (0, 1):
                    act.wait_ge(S("dist_ready"), n0 + p)
                    sc.activation(infl[p][:], infl[p][:], ACT.Exp, scale=-1.0).then_inc(S("infl_ready"), 1)
                for p in (0, 1):
                    n = n0 + p
                    for h in (0, 1):
                        act.wait_ge(S("kept_turned"), (n - 1) * 2 + h + 1)
                        sc.activation(keptT[:, 4 * h:4 * h + 4, :].rearrange("q n t -> q (n t)"), bank[3 + h][0:SEEN, :],
                                      ACT.Copy).then_inc(S("keptT_ready"), 1)
                for p in (0, 1):
                    copy_turned("sparse", t, p, sparseT[p][:], 6 + p)
                for p in (0, 1):
                    copy_turned("x4", t, p, x4T[p][:], 6 + p)
                for p in (0, 1):
                    act.wait_ge(S("neg_max_ready"), n0 + p)
                    sc.activation(pr[p][:], bank[6 + p][:, 0:CTX], ACT.Exp, bias=neg_max[p][:], accum_out=pr_sum[p][:]
                                  ).then_inc(S("pr_ready"), 1)
                for p in (0, 1):
                    copy_turned("pr", t, p, prT[p][:], 6 + p, CTX)
                for p in (0, 1):
                    copy_turned("x5", t, p, x5T[:, bass.ds((t * 2 + p) * T, T)], 6 + p)

            act.wait_ge(S("ff_coef_ready"), 1)
            for c in range(FC):
                for h in (0, 1):
                    act.wait_ge(S("ff_hidden"), 2 * c + h + 1)
                    sc.activation(hid[:, c, h * 512:(h + 1) * 512], bank[2 * c + h][:], ACT.Relu, bias=b_q[0][:, c:c + 1],
                                  scale=o_step[0][:, c:c + 1]).then_inc(S("hid_ready"), 1)
            act.wait_ge(S("ff2_coef_ready"), 1)
            for h in (0, 1):
                act.wait_ge(S("ff_done"), h + 1)
                sc.activation(ff_out[:, h * 512:(h + 1) * 512], bank[h][:], ACT.Identity, bias=b_q[1][:],
                              scale=o_step[1][:]).then_inc(S("ff_out_ready"), 1)

        @block.vector
        def _(dve):
            v = nc.vector

            class Steps:

                def __init__(self, name, per=0):
                    self.name, self.per, self.n, self.t = name, per, 0, None

                def turn(self, t):
                    self.n, self.t = 0, t

                def add(self, instruction):
                    instruction.then_inc(S(self.name), 1)
                    self.n += 1

                def wait(self):
                    dve.wait_ge(S(self.name), self.n if self.t is None else self.t * self.per + self.n)

                def wait_apart(self):
                    wait_apart(dve, self.name, self.t * self.per + self.n)

                def link(self, instruction):
                    self.add(instruction)
                    self.wait()

            def layernorm_stats(chain, src):
                p = chain.parity
                chain.add(v.bn_stats(stats[p][:], src))
                chain.wait_apart()
                chain.link(v.bn_aggr(mv[p][:], stats[p][:]))
                v.tensor_scalar(var_eps[p][:], mv[p][:, 1:2], LN_EPS, None, ALU.add).then_inc(S("ln_var"), 1)

            def layernorm_apply(n, out_name, p, src, dst):
                dve.wait_ge(S("ln_rstd"), n)
                v.tensor_scalar(dst, src, mv[p][:, 0:1], rstd[p][:], ALU.subtract, ALU.mult).then_inc(S(out_name), 1)

            def chains(name, per):
                pair = [Steps(f"{name}{p}", per) for p in (0, 1)]
                for p in (0, 1):
                    pair[p].parity = p
                return pair

            def row_maxes(a, n, p):
                K = KEYS[a]
                for j in range(J):
                    dve.wait_ge(S("scores"), (n - 1) * 4 + (j + 1))
                    v.tensor_reduce(maxes[a][p][:, :, 32 * j + MAXROW], bank[j][:, 0:G * K].rearrange("q (g k) -> q g k", g=G),
                                    AX.X, ALU.max).then_inc(S("max_ready"), 1)

            def lower_queries(a, n, p):
                dve.wait_ge(S("max_turned"), n)
                qf = qT[a][p][:].rearrange("q g t -> q (g t)")
                v.tensor_tensor(qf, qf, bank[WIDE[p]][:], ALU.subtract).then_inc(S("qm_ready"), 1)

            def normalise(a, m, p):
                dve.wait_ge(S("weighed"), m * 4)
                o = bank[WIDE[p]][:, 0:HEADS * (HD + 1)].rearrange("q (h c) -> q h c", h=HEADS)
                chain[p].link(v.reciprocal(rec[p][:], o[:, :, HD]))
                out_of = v.tensor_tensor(attn[p][:].rearrange("q (h d) -> q h d", h=HEADS), o[:, :, 0:HD],
                                rec[p][:].rearrange("q (h d) -> q h d", d=1).broadcast_to([P, HEADS, HD]), ALU.mult)
                if a == "self":
                    chain[p].link(out_of)
                else:
                    out_of.then_inc(S("attn2_ready"), 1)

            prep, route, metric_steps, net = (Steps(f"{name}_step") for name in ("prep", "route", "metric", "net"))
            dve.wait_ge(S("wb_loaded"), 16)
            dve.wait_ge(S("pool_consts"), 15)
            prep.add(v.tensor_reduce(w_abs[:, 0:FC], W("w1f").rearrange("p (c d) -> p c d", c=FC), AX.X, ALU.max,
                            apply_absolute_value=True))
            prep.add(v.tensor_reduce(w_abs[:, FC:FC + 1], W("w2f"), AX.X, ALU.max, apply_absolute_value=True
                            ))
            v.tensor_copy(tri_bf[:], W("tri")).then_inc(S("tri_ready"), 1)
            prep.add(v.tensor_scalar(two_key[:], W("is_square"), -2.0, 2.0, ALU.mult, ALU.add))
            prep.add(v.tensor_scalar(not_square[:], W("is_square"), -1.0, 1.0, ALU.mult, ALU.add))
            prep.add(v.tensor_scalar(neg_square[:], W("is_square"), -1.0, None, ALU.mult))
            dve.wait_ge(S("wa_loaded"), 16)
            dve.wait_ge(S("wa2_loaded"), 16)
            prep.add(v.tensor_scalar(bk2[:], A("bk2"), A("max_col"), None, ALU.add))
            prep.wait()
            prep.link(v.tensor_scalar(w_floor[:], w_abs[:], 1e-8, None, ALU.max))
            prep.link(v.tensor_scalar(w_step[:], w_floor[:], 1.0 / 127.0, None, ALU.mult))
            prep.link(v.reciprocal(w_rec[:], w_step[:]))
            for i in range(FC + 1):
                src, dst = (W("w1f"), w_div[:, 0, :]) if i < FC else (W("w2f"), w_div[:, 1, :])
                cols = slice(i * P, (i + 1) * P) if i < FC else slice(0, FF)
                prep.add(v.tensor_scalar(dst[:, cols], src[:, cols], w_rec[:, i:i + 1], ROUND, ALU.mult, ALU.add))
            prep.wait()
            prep.link(v.tensor_scalar(w_int, w_div, ROUND, 127.0, ALU.subtract, ALU.min))
            v.tensor_scalar(w_clip, w_int, -128.0, None, ALU.max).then_inc(S("w_clip_ready"), 1)

            chain = chains("att_step", 8)
            with dve.Fori(0, PAIRS) as t:
                n0 = t * 2 + 1
                for p in (0, 1):
                    chain[p].turn(t)
                for p in (0, 1):
                    row_maxes("self", t * 4 + (1 + p), p)
                for p in (0, 1):
                    dve.wait_ge(S("cross_k_proj"), n0 + p)
                    v.tensor_tensor(kT["cross"][p][:], bank[MISC[p]][:, 0:G * CTX].rearrange("q (g c) -> q g c", g=G),
                                    bk2[:].rearrange("q (g c) -> q g c", c=1).broadcast_to([P, G, CTX]), ALU.add
                                    ).then_inc(S("cross_k_ready"), 1)
                for p in (0, 1):
                    lower_queries("self", t * 4 + (1 + p), p)
                for p in (0, 1):
                    normalise("self", t * 4 + (1 + p), p)
                    dve.wait_ge(S(f"x_loaded{p}"), (t + 1) * 16)
                    v.tensor_tensor(y_sum[p][:], attn[p][:], x_in[p][:], ALU.add).then_inc(S("self_sum_done"), 1)
                    dve.wait_ge(S("self_sum_done"), n0 + p)
                    layernorm_stats(chain[p], y_sum[p][:])
                for p in (0, 1):
                    layernorm_apply(t * 4 + (1 + p), "x1_ready", p, y_sum[p][:], x1[p][:])
                for p in (0, 1):
                    dve.wait_ge(S("cross_q_proj"), n0 + p)
                    v.tensor_tensor(qT["cross"][p][:], bank[WIDE[p]][:].rearrange("q (g c) -> q g c", g=G),
                                    A("bq2").rearrange("q (g c) -> q g c", c=1).broadcast_to([P, G, T]), ALU.add
                                    ).then_inc(S("cross_q_ready"), 1)
                for p in (0, 1):
                    row_maxes("cross", t * 4 + (3 + p), p)
                for p in (0, 1):
                    lower_queries("cross", t * 4 + (3 + p), p)
                for p in (0, 1):
                    normalise("cross", t * 4 + (3 + p), p)
                for p in (0, 1):
                    dve.wait_ge(S("wo_done"), n0 + p)
                    chain[p].link(v.tensor_tensor(y_sum[p][:], bank[MISC[p]][:, 0:D], x1[p][:], ALU.add))
                    layernorm_stats(chain[p], y_sum[p][:])
                for p in (0, 1):
                    layernorm_apply(t * 4 + (3 + p), "x2_ready", p, y_sum[p][:], x2[p][:])

            dve.wait_ge(S("logits_ready"), B)
            for b in range(B):
                route.add(v.max(top8[:, b, :], logits[:, b, :]))
            route.wait()
            for b in range(B):
                route.add(v.max_index(index8[:, b, :], top8[:, b, :], logits[:, b, :]))
            v.tensor_tensor(shifted[:], logits[:], top8[:, :, 0:1].broadcast_to([P, B, E]), ALU.subtract
                            ).then_inc(S("shifted_ready"), 1)
            v.tensor_tensor(gap[:], top8[:, :, 1], top8[:, :, 0], ALU.subtract).then_inc(S("shifted_ready"), 1)
            route.wait()
            route.link(v.tensor_copy(index_f[:], index8[:, :, 0:2]))
            for k in (0, 1):
                route.add(v.tensor_tensor(onehot[k][:], W("iota_e").rearrange("p (b e) -> p b e", b=1).broadcast_to([P, B, E]),
                                index_f[:, :, k:k + 1].broadcast_to([P, B, E]), ALU.is_equal))
            route.wait()
            v.tensor_tensor(chosen[:], onehot[0][:], onehot[1][:], ALU.add).then_inc(S("chosen_ready"), 1)
            dve.wait_ge(S("exps_ready"), 2)
            route.link(v.tensor_reduce(denom[:], exps[:], AX.X, ALU.add))
            route.add(v.reciprocal(gate[:, 0, :], denom[:]))
            route.wait()
            route.add(v.tensor_tensor(gate[:, 1, :], gate[:, 0, :], exp_gap[:], ALU.mult))
            dve.wait_ge(S("places"), 1)
            places = bank[0][:, 0:B * E].rearrange("p (b e) -> p b e", b=B)
            v.tensor_copy(place[:], places).then_inc(S("place_ready"), 1)
            dve.wait_ge(S("place_ready"), 1)
            route.link(v.tensor_tensor(slot_of[:], place[:], W("slot_e").rearrange("p (b e) -> p b e", b=1).broadcast_to([P, B, E]),
                            ALU.add))
            for k in (0, 1):
                route.add(v.tensor_tensor(picked[k][:], onehot[k][:], place[:], ALU.mult))
                route.add(v.tensor_tensor(picked[2 + k][:], onehot[k][:], slot_of[:], ALU.mult))
            route.wait()
            for k in (0, 1):
                route.add(v.tensor_reduce(place_k[:, k, :], picked[k][:], AX.X, ALU.add))
                route.add(v.tensor_reduce(slot_k[:, k, :], picked[2 + k][:], AX.X, ALU.add))
            route.wait()
            route.add(v.tensor_scalar(over[:], place_k[:], float(CAP), 2.0 * SLOTS, ALU.is_ge, ALU.mult))
            route.add(v.tensor_scalar(fits[:], place_k[:], float(CAP), None, ALU.is_lt))
            route.add(v.tensor_scalar(get_f[:], slot_k[:], float(SLOTS - 1), None, ALU.min))
            route.wait()
            route.link(v.tensor_tensor(put_f[:], slot_k[:], over[:], ALU.add))
            v.tensor_copy(put[:], put_f[:]).then_inc(S("put_ready"), 1)
            v.tensor_copy(get[:], get_f[:]).then_inc(S("put_ready"), 1)
            route.wait()
            v.tensor_tensor(gates[:], gate[:], fits[:], ALU.mult).then_inc(S("gates_ready"), 1)

            dve.wait_ge(S("place_ready"), 1)
            v.memset(h_max[:, 0:2], 0.0).then_inc(S("xb_free"), 2)
            with dve.Fori(0, PAIRS) as t:
                for p in (0, 1):
                    e1 = t * 2 + p + 1
                    dve.wait_ge(S("xbT_ready"), e1)
                    v.memset(h_max[:, p:p + 1], 0.0).then_inc(S("xb_free"), 1)
                for p in (0, 1):
                    e1 = t * 2 + p + 1
                    dve.wait_ge(S("y_done"), e1)
                    v.tensor_copy(yb[p][:].rearrange("q h d -> q (h d)"), bank[6 + p][:, 0:2 * D]).then_inc(S("yb_ready"), 1)

            dve.wait_ge(S("gates_ready"), 1)
            dve.wait_ge(S("x2b_ready"), 1)
            dve.wait_ge(S("gathered"), 16 * 2 * B)
            chain = chains("mix_step", 4)
            with dve.Fori(0, PAIRS) as t:
                for p in (0, 1):
                    chain[p].turn(t)
                    b = t * 2 + p
                    n = b + 1

                    def row(tensor):
                        return tensor[:, bass.ds(b, 1), :].rearrange("q b d -> q (b d)")

                    chain[p].link(v.scalar_tensor_tensor(mix[p][:], row(got[0]), gates[:, 0, bass.ds(b, 1)], row(x2b),
                                           ALU.mult, ALU.add))
                    chain[p].link(v.scalar_tensor_tensor(y_sum[p][:], row(got[1]), gates[:, 1, bass.ds(b, 1)], mix[p][:],
                                           ALU.mult, ALU.add))
                    layernorm_stats(chain[p], y_sum[p][:])
                for p in (0, 1):
                    layernorm_apply(t * 2 + (2 * B + 1 + p), "x3_ready", p, y_sum[p][:], x3[p][:])
                dve.wait_ge(S("turned"), turned("x3", t, 1))
                dve.wait_ge(S("x3_kept"), t * 2 + 2)

            for gi in range(G2):
                dve.wait_ge(S("uT_ready"), 2 * gi + 2)
                metric_steps.link(v.tensor_tensor(sig_p[:, gi], uT[:, gi], W("sig_w").rearrange("p (b t) -> p b t", b=1).broadcast_to([P, B, T]),
                                ALU.mult))
                v.tensor_reduce(sig[:, gi, :], sig_p[:, gi], AX.X, ALU.add).then_inc(S("sig_half"), 1)
            dve.wait_ge(S("sig_half"), 2)
            v.scalar_tensor_tensor(pre[:], W("mn_b2"), 0.1, W("base_metric"), ALU.mult, ALU.add).then_inc(S("sig_ready"), 1)
            prep.wait()
            for gi in range(G2):
                metric_steps.link(v.tensor_scalar(sig_p[:, gi], uT[:, gi], W("is_square"), not_square[:], ALU.mult, ALU.add
                                ))
                v.tensor_tensor(k_all[:, gi], uT[:, gi], sig_p[:, gi], ALU.mult).then_inc(S("k_half"), 1)
            dve.wait_ge(S("k_half"), 2)
            dve.wait_ge(S("mn_mod"), 1)
            mod = bank[1][:, 0:G2 * B].rearrange("p (g b) -> p g b", g=G2)
            metric_steps.link(v.scalar_tensor_tensor(zm[:], mod, 0.1, pre[:].rearrange("p (g b) -> p g b", b=1).broadcast_to([P, G2, B]),
                                   ALU.mult, ALU.add))
            v.scalar_tensor_tensor(zabs[:], zm[:], -1.0, zm[:], ALU.mult, ALU.max).then_inc(S("zabs_ready"), 1)
            metric_steps.link(v.tensor_scalar(zpos[:], zm[:], 0.0, None, ALU.max))
            dve.wait_ge(S("zln_ready"), 1)
            metric_steps.link(v.tensor_tensor(metric[:], zpos[:], zln[:], ALU.add))
            v.tensor_scalar(q_scale[:], metric[:], two_key[:], None, ALU.mult).then_inc(S("q_coef_ready"), 1)
            v.tensor_scalar(q_bias[:], metric[:], neg_square[:], None, ALU.mult).then_inc(S("q_coef_ready"), 1)
            v.memset(h_max[:, 0:1], 0.0).then_inc(S("k_all_ready"), 1)
            v.memset(h_max[:, 1:2], 0.0).then_inc(S("win_free"), 2)

            chain = chains("win_step", 15)
            mask = W("mask").rearrange("p (n w) -> p n w", n=1).broadcast_to([P, 4, SEEN])
            with dve.Fori(0, PAIRS) as t:
                n0 = t * 2 + 1
                for p in (0, 1):
                    chain[p].turn(t)
                    n = n0 + p
                    for h in (0, 1):
                        dve.wait_ge(S("win_scores"), (n - 1) * 2 + h + 1)
                        v.tensor_tensor(score[p][:, 4 * h:4 * h + 4, :],
                                        bank[1 + h][:, 0:HALF].rearrange("q (n w) -> q n w", w=SEEN), mask, ALU.add
                                        ).then_inc(S("score_ready"), 1)
                for p in (0, 1):
                    n = n0 + p
                    wait_apart(dve, "score_ready", 2 * n)
                    for r in range(TOPK // 8):
                        for op in (0, 1):
                            for i in range(NTILE):
                                src = score[p] if r == 0 else work[p]
                                if i % 4 == 0 and r + op > 0:
                                    done = (r * 2 + op - 1) * NTILE + i + 4
                                    wait_apart(dve, "sorted", (n - 1) * 64 + done)
                                if op == 0:
                                    step = v.max(best[p][:, r, i, :], src[:, i, :])
                                else:
                                    step = v.match_replace(work[p][:, i, :], best[p][:, r, i, :], src[:, i, :], TAKEN)
                                step.then_inc(S("sorted"), 1)
                        if r == 1:
                            dve.wait_ge(S("qq_ready"), n)
                            v.tensor_reduce(q_n2[p][:], qq[p][:].rearrange("q (h e) -> q h e", h=NH), AX.X, ALU.add
                                            ).then_inc(S("q_n2_ready"), 1)
                    dve.wait_ge(S("q_norm_ready"), n)
                    chain[p].link(v.tensor_scalar(q_gate[p][:], q_norm[p][:], 0.2, 0.1, ALU.is_gt, ALU.mult))
                    chain[p].link(v.tensor_scalar(q_floor[p][:], q_norm[p][:], 1e-12, None, ALU.max))
                    chain[p].link(v.reciprocal(q_rec[p][:], q_floor[p][:]))
                    chain[p].link(v.tensor_tensor(heb_scale[p][:], q_gate[p][:], q_rec[p][:], ALU.mult))
                for p in (0, 1):
                    n = n0 + p
                    dve.wait_ge(S("infl_ready"), n)
                    dve.wait_ge(S("sorted"), n * 64)
                    v.scalar_tensor_tensor(kept[p][:], work[p], 1.5 * MASKED, infl[p][:], ALU.is_le, ALU.mult
                                           ).then_inc(S("kept_ready"), 1)
                for p in (0, 1):
                    n = n0 + p
                    dve.wait_ge(S("win_context"), n)
                    c = bank[5][:, 0:NH * (HE + 1)].rearrange("q (h e) -> q h e", h=NH)
                    chain[p].link(v.tensor_scalar(infl_sum[p][:], c[:, :, HE], 1e-8, None, ALU.add))
                    chain[p].link(v.tensor_tensor(heb_out[p][:].rearrange("q (h e) -> q h e", h=NH),
                                    bank[5][:, 256:256 + D].rearrange("q (h e) -> q h e", h=NH),
                                    heb_scale[p][:].rearrange("q (h e) -> q h e", e=1).broadcast_to([P, NH, HE]),
                                    ALU.mult))
                    chain[p].link(v.reciprocal(infl_rec[p][:], infl_sum[p][:]))
                    chain[p].link(v.tensor_tensor(context[p][:].rearrange("q (h e) -> q h e", h=NH), c[:, :, 0:HE],
                                    infl_rec[p][:].rearrange("q (h e) -> q h e", e=1).broadcast_to([P, NH, HE]),
                                    ALU.mult))
                    v.tensor_tensor(both[p][:], context[p][:], heb_out[p][:], ALU.add).then_inc(S("both_ready"), 1)
                    dve.wait_ge(S("both_ready"), n)
                    v.tensor_tensor(sparse[p][:], both[p][:], q_tok[p][:], ALU.mult).then_inc(S("sparse_ready"), 1)
                v.memset(h_max[:, 3:4], 0.0).then_inc(S("win_free"), 2)
                for p in (0, 1):
                    n = n0 + p
                    dve.wait_ge(S("decoded"), n)
                    dve.wait_ge(S("x3_kept"), B)
                    chain[p].link(v.tensor_tensor(y_sum[p][:], bank[6 + p][:, 0:D],
                                    x3_all[:, bass.ds(t * 2 + p, 1), :].rearrange("q b d -> q (b d)"), ALU.add
                                    ))
                    layernorm_stats(chain[p], y_sum[p][:])
                for p in (0, 1):
                    layernorm_apply(t * 4 + (3 * B + 1 + p), "x4_ready", p, y_sum[p][:], x4[p][:])
                for p in (0, 1):
                    dve.wait_ge(S("plain_scores"), n0 + p)
                    v.tensor_reduce(neg_max[p][:], bank[6 + p][:, 0:CTX], AX.X, ALU.max, negate=True
                                    ).then_inc(S("neg_max_ready"), 1)
                for p in (0, 1):
                    n = n0 + p
                    dve.wait_ge(S("pr_ready"), n)
                    chain[p].link(v.reciprocal(pr_rec[p][:], pr_sum[p][:]))
                for p in (0, 1):
                    n = n0 + p
                    dve.wait_ge(S("plain_out"), n)
                    chain[p].link(v.scalar_tensor_tensor(y_sum[p][:], bank[6 + p][:, 0:D], pr_rec[p][:], x4[p][:], ALU.mult, ALU.add
                                           ))
                    layernorm_stats(chain[p], y_sum[p][:])
                for p in (0, 1):
                    layernorm_apply(t * 4 + (3 * B + 3 + p), "x5_ready", p, y_sum[p][:], x5[p][:])

            def step_of(i):
                width = (FC, 1)[i]
                ws = w_step[:, 0:FC] if i == 0 else w_step[:, FC:FC + 1]
                bias = W("b1f") if i == 0 else W("b2f")
                dve.wait_ge(S(f"a_top_ready{i}"), 1)
                net.link(v.tensor_scalar(a_floor[i][:], a_top[i][:], 1e-8, None, ALU.max))
                net.link(v.tensor_scalar(a_step[i][:], a_floor[i][:], 1.0 / 255.0, None, ALU.mult))
                net.add(v.reciprocal(a_rec[i][:], a_step[i][:]))
                net.link(v.tensor_scalar(o_step[i][:], ws, a_step[i][:], None, ALU.mult))
                net.link(v.reciprocal(b_rec[i][:], o_step[i][:]))
                net.link(v.tensor_tensor(b_div[i][:], bias, b_rec[i][:], ALU.mult))
                net.link(v.tensor_scalar(b_int[i][:], b_div[i][:], ROUND, ROUND, ALU.add, ALU.subtract))
                v.tensor_tensor(b_q[i][:], b_int[i][:], o_step[i][:], ALU.mult
                                ).then_inc(S(("ff_coef_ready", "ff2_coef_ready")[i]), 1)

            dve.wait_ge(S("turned_copied"), turned("x5", PAIRS - 1, 1))
            v.tensor_reduce(a_max[0][:], x5T, AX.X, ALU.max).then_inc(S("a_max_ready0"), 1)
            step_of(0)
            net.link(v.tensor_scalar(zT, x5T, a_rec[0][:], 0.0, ALU.mult, ALU.max))
            net.link(v.tensor_scalar(ff_out, zT, 255.0, ROUND, ALU.min, ALU.add))
            v.tensor_scalar(xq, ff_out, ROUND, None, ALU.subtract).then_inc(S("xq_ready"), 1)
            for c in range(FC):
                for h in (0, 1):
                    i = 2 * c + h
                    dve.wait_ge(S("hid_ready"), i + 1)
                    v.tensor_reduce(h_max[:, i:i + 1], hid[:, c, h * 512:(h + 1) * 512], AX.X, ALU.max
                                    ).then_inc(S("h_max_ready"), 1)
            dve.wait_ge(S("h_max_ready"), 8)
            v.tensor_reduce(a_max[1][:], h_max[:], AX.X, ALU.max).then_inc(S("a_max_ready1"), 1)
            step_of(1)
            for c in range(FC):
                net.link(v.tensor_scalar(hid[:, c, :], hid[:, c, :], a_rec[1][:], 0.0, ALU.mult, ALU.max))
                net.link(v.tensor_scalar(hid[:, c, :], hid[:, c, :], 255.0, ROUND, ALU.min, ALU.add))
                v.tensor_scalar(hq[:, c, :], hid[:, c, :], ROUND, None, ALU.subtract).then_inc(S("hq_ready"), 1)
            for h in (0, 1):
                cols = slice(h * 512, (h + 1) * 512)
                dve.wait_ge(S("ff_out_ready"), h + 1)
                v.tensor_tensor(zT[:, cols], ff_out[:, cols], x5T[:, cols], ALU.add).then_inc(S("zT_ready"), 1)
            for b in range(B):
                dve.wait_ge(S("z_turned"), b // 4 + 1)
                v.bn_stats(fstats[:, b, :], bank[2 + b // 4][:, (b % 4) * D:(b % 4 + 1) * D]).then_inc(S("final_stats"), 1)
            for b in range(B):
                dve.wait_ge(S("final_stats"), b + 1)
                v.bn_aggr(fmv[:, b, :], fstats[:, b, :]).then_inc(S("final_mv"), 1)
            dve.wait_ge(S("final_mv"), B)
            v.tensor_scalar(fvar[:], fmv[:, :, 1], LN_EPS, None, ALU.add).then_inc(S("final_var"), 1)
            dve.wait_ge(S("final_rstd"), 1)
            for b in range(B):
                v.tensor_scalar(final[:, b, :], bank[2 + b // 4][:, (b % 4) * D:(b % 4 + 1) * D], fmv[:, b, 0:1],
                                frstd[:, b:b + 1], ALU.subtract, ALU.mult).then_inc(S("final_ready"), 1)


def kernel(**inputs):
    import numpy as np
    import concourse.bacc as bacc
    from concourse.bass_utils import run_bass_kernel_spmd

    a = {k: np.ascontiguousarray(v) for k, v in inputs.items()}
    f32 = np.float32
    head = np.arange(HEADS)
    padded = ((head // 4)[:, None] * P + 32 * (head % 4)[:, None] + np.arange(HD)[None, :]).reshape(-1)

    def pad_cols(w):
        out = np.zeros((w.shape[0], G * P), f32)
        out[:, padded] = w
        return out

    def pad_bias(vec):
        out = np.zeros(G * P, f32)
        out[padded] = vec
        return out.reshape(G, P).T

    def rows(array, n=P):
        array = np.asarray(array, f32).reshape(array.shape[0], -1) if array.ndim > 1 else array.reshape(1, -1)
        out = np.zeros((P, array.shape[1]), f32)
        out[:array.shape[0]] = array
        return out

    def packed(names, parts):
        return np.ascontiguousarray(np.concatenate([rows(parts[name]) for name, _ in names], axis=1))

    part = np.arange(P)
    r = part % 32
    rev = T - 1 - part
    parts_a = {
        "wq": pad_cols(a["L0_attn_Wq"].T), "wk": pad_cols(a["L0_attn_Wk"].T), "wv": a["L0_attn_Wv"].T,
        "max_col": (r == MAXROW).astype(f32)[:, None], "ident": np.eye(P, dtype=f32),
        "wq2": pad_cols(a["L0_xattn_Wq"]), "wk2": pad_cols(a["L0_xattn_Wk"]), "wv2": a["L0_xattn_Wv"],
        "bq2": pad_bias(a["L0_xattn_bq"]), "bk2": pad_bias(a["L0_xattn_bk"]), "bv2": a["L0_xattn_bv"],
        "wo": a["L0_xattn_Wo"], "bo": a["L0_xattn_bo"], "router": a["L0_ffn_w_router"],
    }
    nh = np.arange(NH)
    enc_q = a["L1_attn_encoder_query"].transpose(1, 0, 2)
    enc_v = a["L1_attn_encoder_value"].transpose(1, 0, 2)

    def doubled(w):
        w = w.reshape(w.shape[0], G2, 4, 1, HE)
        return np.broadcast_to(w, (w.shape[0], G2, 4, 2, HE)).reshape(w.shape[0], G2 * P)

    mn_w1 = np.zeros((G2, 4, 2, HE, HID), f32)
    mn_w1[:, :, 0] = a["L1_attn_mn_w1"].reshape(G2, 4, HE, HID)
    heb_u = np.zeros((4, 4, G2, 4, 32), f32)
    heb_v = np.zeros((4, 4, G2, 4, HE), f32)
    for h in nh:
        heb_u[h % 4, :, h // 4, h % 4, :HE] = a["L1_attn_hebbian_U"][h].T
        heb_v[h % 4, :, h // 4, h % 4, :] = a["L1_attn_hebbian_V"][h]
    col = np.arange(SEEN)[None, :]
    mask = np.where((col >= r[:, None]) & (col < r[:, None] + WIN), 0.0, MASKED).astype(f32)
    sig_w = np.where(rev % 8 == 0, 1.0 / T + 0.5 / (T // 8), 1.0 / T).astype(f32)
    parts_b = {
        "tri": (part[:, None] > part[None, :]).astype(f32),
        "iota_e": np.broadcast_to(np.arange(E, dtype=f32), (P, E)),
        "slot_e": np.broadcast_to(np.arange(E, dtype=f32) * CAP, (P, E)),
        "ffn_bias": np.broadcast_to(a["L0_ffn_bias"].reshape(1, D), (P, D)),
        "key_w": doubled(enc_q), "qv_w": np.concatenate([enc_q.reshape(D, D), enc_v.reshape(D, D)], axis=1),
        "mn_w1": mn_w1.reshape(G2, P, HID).transpose(1, 0, 2), "mn_b1": a["L1_attn_mn_b1"][:, None],
        "mn_w2": doubled(a["L1_attn_mn_w2"].reshape(HID, NH, HE)),
        "mn_b2": doubled(a["L1_attn_mn_b2"].reshape(1, NH, HE)).reshape(G2, P).T,
        "base_metric": doubled(a["L1_attn_base_metric"].reshape(1, NH, HE)).reshape(G2, P).T,
        "is_square": (r >= HE).astype(f32)[:, None], "sig_w": np.broadcast_to(sig_w, (P, T)),
        "heb_u": heb_u.reshape(16, G2 * P), "heb_v": heb_v.reshape(16, G2 * 64), "decoder": a["L1_attn_decoder"],
        "mask": mask, "w1f": a["L1_ffn_w1"].reshape(FC, P, D).transpose(1, 0, 2),
        "b1f": a["L1_ffn_b1"].reshape(FC, P).T, "w2f": a["L1_ffn_w2"], "b2f": a["L1_ffn_b2"][:, None],
    }
    x = a["x"][:, ::-1, :]
    arrays = {
        "x_rows": x, "x_cols": x.transpose(0, 2, 1), "ctx_rows": a["ctx_1024"], "ctx_cols": a["ctx_1024"].transpose(0, 2, 1),
        "pack_a": packed(PACK_A, parts_a), "pack_b": packed(PACK_B, parts_b),
        "w1": a["L0_ffn_w1"], "w2": a["L0_ffn_w2"].reshape(E, FC, P, D).transpose(0, 2, 1, 3),
    }
    arrays = {k: np.ascontiguousarray(v) for k, v in arrays.items()}
    nc = bacc.Bacc("TRN2", target_bir_lowering=False, num_devices=1)
    args = [nc.dram_tensor(k, v.shape, mybir.dt.from_np(v.dtype), kind="ExternalInput").ap() for k, v in arrays.items()]
    out = nc.dram_tensor("out", (B, T, D), F32, kind="ExternalOutput").ap()
    xb_dram = nc.dram_tensor("xb_dram", (SLOTS, D), F32, kind="Internal").ap()
    y_dram = nc.dram_tensor("y_dram", (SLOTS, D), F32, kind="Internal").ap()
    decoder_kernel(nc, *args, out, xb_dram, y_dram)
    result = run_bass_kernel_spmd(nc, [arrays], core_ids=[0])
    return np.ascontiguousarray(result.results[0]["out"][:, ::-1, :])
```

```python
from contextlib import ExitStack

import concourse.bass as bass
from concourse import mybir

F32 = mybir.dt.float32
BF16 = mybir.dt.bfloat16
U32 = mybir.dt.uint32
ALU = mybir.AluOpType
ACT = mybir.ActivationFunctionType
AX = mybir.AxisListType

P = 128
B, T, D = 8, 128, 128
TOK = B * T
CTX = 77
PAIRS = B // 2
HEADS, HD, G, J = 16, 8, 4, 4
PARTS = 3
MAXROW = PARTS * HD
LN_EPS = 1e-5
E, FF, CAP = 8, 512, 256
FC = FF // P
SLOTS = E * CAP
NH, HE, WIN, TOPK = 8, 16, 64, 32
G2 = NH // 4
HID = WIN
QUARTER = 32
SEEN = QUARTER + WIN
TX = T + WIN
NTILE = G2 * T // QUARTER
HALF = NTILE // 2 * SEEN
MASKED = -1e30
TAKEN = -2e30
ROUND = 12582912.0

PACK_A = [("wq", G * P), ("wk", G * P), ("wv", P), ("k_bias", 1), ("q_low", 1), ("k_low", 1), ("ident", P), ("wq2", G * P), ("wk2", G * P),
          ("wv2", P), ("bq2", G), ("bk2", G), ("bv2", P), ("wo", P), ("bo", P), ("router", E)]
PACK_B = [("tri", P), ("iota_e", E), ("slot_e", E), ("ffn_bias", P), ("key_w", G2 * P), ("qv_w", 2 * P),
          ("mn_w1", G2 * HID), ("mn_b1", 1), ("mn_w2", G2 * P), ("mn_b2", G2), ("base_metric", G2),
          ("is_square", 1), ("sig_w", P), ("heb_u", G2 * P), ("heb_v", G2 * 64), ("decoder", P),
          ("mask", SEEN), ("w1f", FF), ("b1f", FC), ("w2f", FF), ("b2f", 1)]


def columns(pack):
    at, out = 0, {}
    for name, width in pack:
        out[name] = (at, width)
        at += width
    return out, at


COLS_A, WIDTH_A = columns(PACK_A)
COLS_B, WIDTH_B = columns(PACK_B)


def decoder_kernel(nc, x_rows, x_cols, ctx_rows, ctx_cols, pack_a, pack_b, w1, w2, out, xb_dram, y_dram):
    with ExitStack() as stack:
        made = {}

        def S(name):
            if name not in made:
                made[name] = stack.enter_context(nc.semaphore(name))
            return made[name]

        def sb(name, shape, dt=F32):
            return stack.enter_context(nc.sbuf_tensor(name, shape, dt))

        bank = [stack.enter_context(nc.psum_tensor(f"bank{i}", [P, 512], F32)) for i in range(8)]

        wa = sb("wa", [P, WIDTH_A])
        wb = sb("wb", [P, WIDTH_B])

        def A(name, rows=P):
            at, width = COLS_A[name]
            return wa[0:rows, at:at + width]

        def W(name, rows=P):
            at, width = COLS_B[name]
            return wb[0:rows, at:at + width]

        ident = A("ident")
        hid = sb("hid", [P, FC, TOK])
        w_div = hid[:, 0, :].rearrange("p (i f) -> p i f", i=2)
        w_int = hid[:, 1, :].rearrange("p (i f) -> p i f", i=2)
        w_clip = hid[:, 2, :].rearrange("p (i f) -> p i f", i=2)
        sig_p = hid[:, 0:2, :].rearrange("p g (b t) -> p g b t", b=B)
        ones_row = sb("ones_row", [1, P])
        ones_bf = sb("ones_bf", [P, P], BF16)
        tri_bf = sb("tri_bf", [P, P], BF16)
        neg_half = sb("neg_half", [P, B])
        half = sb("half", [P, B])
        tiny = sb("tiny", [P, 1])
        x3T_all = sb("x3T_all", [P, TOK])
        zeros = x3T_all

        xT_in = [sb(f"xT_in{p}", [P, T]) for p in (0, 1)]
        x_in = [sb(f"x_in{p}", [P, D]) for p in (0, 1)]
        cT_in = [sb(f"cT_in{p}", [P, CTX]) for p in (0, 1)]
        qT = {a: [sb(f"{a}_qT{p}", [P, G, T], BF16) for p in (0, 1)] for a in ("self", "cross")}
        kT = {"self": [sb(f"self_kT{p}", [P, G, T], BF16) for p in (0, 1)],
              "cross": [sb(f"cross_kT{p}", [P, G, CTX], BF16) for p in (0, 1)]}
        q_high = {a: [sb(f"{a}_q_high{p}", [P, G, T], BF16) for p in (0, 1)] for a in ("self", "cross")}
        k_high = {"self": [sb(f"self_k_high{p}", [P, G, T], BF16) for p in (0, 1)],
                  "cross": [sb(f"cross_k_high{p}", [P, G, CTX], BF16) for p in (0, 1)]}
        q_full = [sb(f"q_full{p}", [P, G, T]) for p in (0, 1)]
        k_full = [sb(f"k_full{p}", [P, G, CTX]) for p in (0, 1)]
        v_high = {a: [sb(f"{a}_v_high{p}", [P, HEADS, HD + 1], BF16) for p in (0, 1)] for a in ("self", "cross")}
        v_low = {a: [sb(f"{a}_v_low{p}", [P, HEADS, HD + 1], BF16) for p in (0, 1)] for a in ("self", "cross")}
        maxes = {a: [sb(f"{a}_max{p}", [P, G, P], BF16) for p in (0, 1)] for a in ("self", "cross")}
        ident_bf = sb("ident_bf", [P, P], BF16)
        probs_all = sb("probs_all", [P, J * G * T])
        probs = [probs_all[:, j * G * T:(j + 1) * G * T].rearrange("p (g t) -> p g t", g=G) for j in range(J)]
        parts_all = sb("parts_all", [P, 2, J, G, T], BF16)
        p_high = [parts_all[:, 0, j] for j in range(J)]
        p_low = [parts_all[:, 1, j] for j in range(J)]
        rec = [sb(f"rec{p}", [P, HEADS]) for p in (0, 1)]
        attn = [sb(f"attn{p}", [P, D]) for p in (0, 1)]
        y_sum = [sb(f"y_sum{p}", [P, D]) for p in (0, 1)]
        stats = [sb(f"stats{p}", [P, 6]) for p in (0, 1)]
        mv = [sb(f"mv{p}", [P, 2]) for p in (0, 1)]
        var_eps = [sb(f"var_eps{p}", [P, 1]) for p in (0, 1)]
        rstd = [sb(f"rstd{p}", [P, 1]) for p in (0, 1)]
        x1 = [sb(f"x1_{p}", [P, D]) for p in (0, 1)]
        x1T = [sb(f"x1T{p}", [P, T]) for p in (0, 1)]
        a2T = [sb(f"a2T{p}", [P, T]) for p in (0, 1)]
        x2 = [sb(f"x2_{p}", [P, D]) for p in (0, 1)]
        x2T = [sb(f"x2T{p}", [P, T]) for p in (0, 1)]
        x2_all = sb("x2_all", [P, B, D])
        logits = sb("logits", [P, B, E])

        top8 = sb("top8", [P, B, 8])
        index8 = sb("index8", [P, B, 8], U32)
        index_f = sb("index_f", [P, B, 2])
        shifted = sb("shifted", [P, B, E])
        exps = sb("exps", [P, B, E])
        gap = sb("gap", [P, B])
        exp_gap = sb("exp_gap", [P, B])
        denom = sb("denom", [P, B])
        gate = sb("gate", [P, 2, B])
        onehot = [sb(f"onehot{k}", [P, B, E]) for k in (0, 1)]
        chosen = sb("chosen", [P, B, E], BF16)
        place = sb("place", [P, B, E])
        slot_of = sb("slot_of", [P, B, E])
        picked = [sb(f"picked{i}", [P, B, E]) for i in range(4)]
        place_k = sb("place_k", [P, 2, B])
        slot_k = sb("slot_k", [P, 2, B])
        fits = sb("fits", [P, 2, B])
        over = sb("over", [P, 2, B])
        put_f = sb("put_f", [P, 2, B])
        get_f = sb("get_f", [P, 2, B])
        put = sb("put", [P, 2, B], U32)
        get = sb("get", [P, 2, B], U32)
        gates = sb("gates", [P, 2, B])
        xb_in = [sb(f"xb_in{p}", [P, 2, D]) for p in (0, 1)]
        w1_in = [sb(f"w1_in{p}", [P, FF]) for p in (0, 1)]
        w2_in = [sb(f"w2_in{p}", [P, FC, D]) for p in (0, 1)]
        xbT = [sb(f"xbT{p}", [P, CAP]) for p in (0, 1)]
        hT = [sb(f"hT{p}", [P, FC, CAP]) for p in (0, 1)]
        yb = [sb(f"yb{p}", [P, 2, D]) for p in (0, 1)]
        got = [sb(f"got{k}", [P, B, D]) for k in (0, 1)]
        x2b = sb("x2b", [P, B, D])

        x3_all = sb("x3_all", [P, B, D])
        uT = sb("uT", [P, G2, B, T])
        sig = sb("sig", [P, G2, B])
        hidden = sb("hidden", [HID, B])
        pre = sb("pre", [P, G2])
        zm = sb("zm", [P, G2, B])
        zabs = sb("zabs", [P, G2, B])
        zexp = sb("zexp", [P, G2, B])
        zln = sb("zln", [P, G2, B])
        zpos = sb("zpos", [P, G2, B])
        metric = sb("metric", [P, G2, B])
        q_scale = sb("q_scale", [P, G2, B])
        q_bias = sb("q_bias", [P, G2, B])
        two_key = sb("two_key", [P, 1])
        not_square = sb("not_square", [P, 1])
        neg_square = sb("neg_square", [P, 1])
        heb = sb("heb", [P, G2, 64])
        k_all = sb("k_all", [P, G2, B, T])
        qs = [sb(f"qs{p}", [P, G2, T]) for p in (0, 1)]
        ks = [sb(f"ks{p}", [P, G2, TX]) for p in (0, 1)]
        x3T = [sb(f"x3T{p}", [P, TX]) for p in (0, 1)]
        q_tok = [sb(f"q_tok{p}", [P, D]) for p in (0, 1)]
        vw = [sb(f"vw{p}", [SEEN, 4, NH, HE + 1]) for p in (0, 1)]
        score = [probs_all[:, p * NTILE * SEEN:(p + 1) * NTILE * SEEN].rearrange("p (n w) -> p n w", w=SEEN) for p in (0, 1)]
        work = [hT[p][:].rearrange("p c s -> p (c s)")[:, 0:NTILE * SEEN].rearrange("p (n w) -> p n w", w=SEEN)
                for p in (0, 1)]
        best = [sb(f"best{p}", [P, TOPK // 8, NTILE, 8]) for p in (0, 1)]
        parts_f32 = parts_all[:].rearrange("p a j g t -> p (a j g t)").bitcast(F32)
        infl = [parts_f32[:, p * NTILE * SEEN:(p + 1) * NTILE * SEEN].rearrange("p (n w) -> p n w", w=SEEN) for p in (0, 1)]
        kept = [sb(f"kept{p}", [P, NTILE, SEEN]) for p in (0, 1)]
        keptT = hid[0:SEEN, 3, :].rearrange("p (n t) -> p n t", n=NTILE)
        heb_raw = [sb(f"heb_raw{p}", [P, D]) for p in (0, 1)]
        sparseT_all = hid[:, 2, :]
        qq = [sb(f"qq{p}", [P, D]) for p in (0, 1)]
        q_n2 = [sb(f"q_n2_{p}", [P, NH]) for p in (0, 1)]
        q_norm = [sb(f"q_norm{p}", [P, NH]) for p in (0, 1)]
        q_gate = [sb(f"q_gate{p}", [P, NH]) for p in (0, 1)]
        q_floor = [sb(f"q_floor{p}", [P, NH]) for p in (0, 1)]
        q_rec = [sb(f"q_rec{p}", [P, NH]) for p in (0, 1)]
        heb_scale = [sb(f"heb_scale{p}", [P, NH]) for p in (0, 1)]
        infl_sum = [sb(f"infl_sum{p}", [P, NH]) for p in (0, 1)]
        infl_rec = [sb(f"infl_rec{p}", [P, NH]) for p in (0, 1)]
        heb_out = [sb(f"heb_out{p}", [P, D]) for p in (0, 1)]
        context = [sb(f"context{p}", [P, D]) for p in (0, 1)]
        both = [sb(f"both{p}", [P, D]) for p in (0, 1)]
        sparse = [sb(f"sparse{p}", [P, D]) for p in (0, 1)]

        cT_all = sb("cT_all", [P, B, CTX])
        c_all = sb("c_all", [CTX, B, D])
        y4, x4_all = got[0], got[1]
        x4T_all = x2_all[:].rearrange("p b d -> p (b d)")
        neg_max = sb("neg_max", [P, B])
        pr_all = probs_all[:, 0:B * CTX].rearrange("p (b c) -> p b c", b=B)
        pr_sum = sb("pr_sum", [P, B])
        pr_rec = sb("pr_rec", [P, B])
        prT_all = hid[0:CTX, 3, :]
        y5 = got[0]
        x5_all = parts_f32[:, 0:TOK].rearrange("p (b d) -> p b d", b=B)
        x5T = x2b[:].rearrange("p b d -> p (b d)")
        stats4 = [sb(f"stats4_{h}", [P, 4, 6]) for h in (0, 1)]
        mv4 = [sb(f"mv4_{h}", [P, 4, 2]) for h in (0, 1)]
        var4 = [sb(f"var4_{h}", [P, 4]) for h in (0, 1)]
        rstd4 = [sb(f"rstd4_{h}", [P, 4]) for h in (0, 1)]

        w_abs = sb("w_abs", [P, FC + 1])
        w_floor = sb("w_floor", [P, FC + 1])
        w_step = sb("w_step", [P, FC + 1])
        w1q = sb("w1q", [P, FF], BF16)
        w2q = sb("w2q", [P, FC, P], BF16)
        w_rec = sb("w_rec", [P, FC + 1])
        a_max = [sb(f"a_max{i}", [P, 1]) for i in (0, 1)]
        a_top = [sb(f"a_top{i}", [P, 1]) for i in (0, 1)]
        a_floor = [sb(f"a_floor{i}", [P, 1]) for i in (0, 1)]
        a_step = [sb(f"a_step{i}", [P, 1]) for i in (0, 1)]
        a_rec = [sb(f"a_rec{i}", [P, 1]) for i in (0, 1)]
        b_rec = [sb(f"b_rec{i}", [P, (FC, 1)[i]]) for i in (0, 1)]
        o_step = [sb(f"o_step{i}", [P, (FC, 1)[i]]) for i in (0, 1)]
        b_div = [sb(f"b_div{i}", [P, (FC, 1)[i]]) for i in (0, 1)]
        b_int = [sb(f"b_int{i}", [P, (FC, 1)[i]]) for i in (0, 1)]
        b_q = [sb(f"b_q{i}", [P, (FC, 1)[i]]) for i in (0, 1)]
        xq = x3_all[:].rearrange("p b d -> p (b d)").bitcast(BF16)[:, 0:TOK]
        h_max = sb("h_max", [P, 8])
        hq = uT[:].rearrange("p g b t -> p (g b t)").bitcast(BF16).rearrange("p (c t) -> p c t", c=FC)
        ff_out = got[0][:].rearrange("p b d -> p (b d)")
        zT = got[1][:].rearrange("p b d -> p (b d)")
        final = x2_all

        block = stack.enter_context(nc.Block())

        SCALE = {"self": 1.0 / float(D) ** 0.5, "cross": 1.0 / float(HD) ** 0.5}
        KEYS = {"self": T, "cross": CTX}
        KINDS = ("self", "cross")
        MISC = (4, 5)
        WIDE = (6, 7)

        def wait_apart(engine, name, value):
            engine.wait_ge(S(name), value)
            engine.sem_inc(S("wait_passed"), 1)

        TURNS = {"x1": (0, 6, 0), "attn2": (0, 6, 1), "x2": (0, 6, 2)}

        LN4 = {"x3": 1, "x4": 3, "x5": 5, "final": 7}
        WIDE_TURNS = {"x3": 1, "x4": 3, "pr": 5, "x5": 7}
        QUADS = [slice(0, B // 2), slice(B // 2, B)]
        COLS4 = [slice(0, TOK // 2), slice(TOK // 2, TOK)]

        def turned(name, t, p):
            before, per, which = TURNS[name]
            return t * per + (before + 2 * which + p + 1)

        HIGH = {"self_q": (0, 2), "self_k": (1, 2), "self_v": (4, 1), "cross_k": (0, 1), "cross_v": (2, 1), "cross_q": (4, 1)}

        def high(name, t, p):
            first, stride = HIGH[name]
            return t * 6 + (first + stride * p + 1)

        @block.sync
        def _(sp):
            sp.dma_start(xT_in[0][:], x_cols[0]).then_inc(S("xT_loaded0"), 16)
            sp.dma_start(xT_in[1][:], x_cols[1]).then_inc(S("xT_loaded1"), 16)
            sp.dma_start(wa[:, 0:COLS_A["wq2"][0]], pack_a[:, 0:COLS_A["wq2"][0]]).then_inc(S("wa_loaded"), 16)
            for p in (0, 1):
                sp.dma_start(x_in[p][:], x_rows[p]).then_inc(S(f"x_loaded{p}"), 16)
                sp.dma_start(cT_in[p][:], ctx_cols[p]).then_inc(S(f"cT_loaded{p}"), 16)
            sp.dma_start(wa[:, COLS_A["wq2"][0]:WIDTH_A], pack_a[:, COLS_A["wq2"][0]:WIDTH_A]).then_inc(S("wa2_loaded"), 16)
            sp.dma_start(wb[:], pack_b).then_inc(S("wb_loaded"), 16)
            sp.dma_start(cT_all[:], ctx_cols.rearrange("b d c -> d b c")).then_inc(S("ctx_loaded"), 16)
            sp.dma_start(c_all[:], ctx_rows.rearrange("b c d -> c b d")).then_inc(S("ctx_loaded"), 16)
            sp.wait_ge(S("zeros_ready"), 1)
            for h in (0, 1):
                sp.dma_start(xb_dram[h * SLOTS // 2:(h + 1) * SLOTS // 2, :].rearrange("(p r) d -> p (r d)", p=P),
                             zeros[:]).then_inc(S("xb_zeroed"), 16)
            for p in (0, 1):
                sp.dma_start(w1_in[p][:], w1[p]).then_inc(S(f"w_loaded{p}"), 16)
                sp.dma_start(w2_in[p][:], w2[p]).then_inc(S(f"w_loaded{p}"), 16)
            with sp.Fori(0, PAIRS - 1) as t:
                for p in (0, 1):
                    n = t * 2 + p + 1
                    sp.wait_ge(S("self_v_done"), n)
                    sp.dma_start(xT_in[p][:], x_cols[bass.ds(t * 2 + (2 + p), 1)].rearrange("b d t -> (b d) t")
                                 ).then_inc(S(f"xT_loaded{p}"), 16)
                    sp.wait_ge(S("self_sum_done"), n)
                    sp.dma_start(x_in[p][:], x_rows[bass.ds(t * 2 + (2 + p), 1)].rearrange("b t d -> (b t) d")
                                 ).then_inc(S(f"x_loaded{p}"), 16)
                    sp.wait_ge(S("cross_v_done"), n)
                    sp.dma_start(cT_in[p][:], ctx_cols[bass.ds(t * 2 + (2 + p), 1)].rearrange("b d c -> (b d) c")
                                 ).then_inc(S(f"cT_loaded{p}"), 16)
            sp.wait_ge(S("scattered"), 16 * 2 * B)
            with sp.Fori(0, PAIRS) as t:
                for p in (0, 1):
                    e = t * 2 + p
                    sp.wait_ge(S("xb_free"), e + 1)
                    sp.dma_start(xb_in[p][:], xb_dram[bass.ds(e * CAP, CAP), :].rearrange("(h s) d -> s h d", h=2)
                                 ).then_inc(S(f"xb_loaded{p}"), 16)
                for p in (0, 1):
                    e = t * 2 + p
                    sp.wait_ge(S("yb_ready"), e + 1)
                    sp.dma_start(y_dram[bass.ds(e * CAP, CAP), :].rearrange("(h s) d -> s h d", h=2), yb[p][:]
                                 ).then_inc(S(f"y_stored{p}"), 16)
            sp.wait_ge(S("final_ready"), B)
            sp.dma_start(out.rearrange("b t d -> t b d"), final[:]).then_inc(S("out_stored"), 16)
            sp.wait_ge(S("out_stored"), 16)

        @block.gpsimd
        def _(pool):
            g = nc.gpsimd
            g.memset(neg_half[:], -0.5).then_inc(S("pool_consts"), 1)
            g.memset(half[:], 0.5).then_inc(S("pool_consts"), 1)
            g.memset(ones_row[:], 1.0).then_inc(S("pool_consts"), 1)
            g.memset(ones_bf[:], 1.0).then_inc(S("pool_consts"), 1)
            g.memset(tiny[:], 1e-8).then_inc(S("pool_consts"), 1)
            for a in KINDS:
                for p in (0, 1):
                    g.memset(maxes[a][p][:], 0.0).then_inc(S("pool_consts"), 1)
                    g.memset(v_high[a][p][:, :, HD:HD + 1], 1.0).then_inc(S("pool_consts"), 1)
                    g.memset(v_low[a][p][:, :, HD:HD + 1], 0.0).then_inc(S("pool_consts"), 1)
            for p in (0, 1):
                g.memset(vw[p][:, :, :, HE:HE + 1], 1.0).then_inc(S("pool_consts"), 1)
            g.memset(zeros[:], 0.0).then_inc(S("zeros_ready"), 1)

            def power(n, p):
                pool.wait_ge(S("ln_var"), n)
                g.tensor_tensor(rstd[p][:], var_eps[p][:], neg_half[:, 0:1], ALU.pow).then_inc(S("ln_rstd"), 1)

            def low_probs(a, m):
                K = KEYS[a]
                for j in range(J):
                    pool.wait_ge(S("p_high_ready"), (m - 1) * 4 + (j + 1))
                    g.tensor_tensor(p_low[j][0:K], probs[j][0:K], p_high[j][0:K], ALU.subtract
                                    ).then_inc(S("probs_ready"), 1)

            with pool.Fori(0, PAIRS) as t:
                for p in (0, 1):
                    wait_apart(pool, "cross_high", high("cross_k", t, p))
                    g.tensor_tensor(kT["cross"][p][:], k_full[p][:], k_high["cross"][p][:], ALU.subtract
                                    ).then_inc(S("cross_k_ready"), 1)
                for p in (0, 1):
                    low_probs("self", t * 4 + (1 + p))
                for p in (0, 1):
                    power(t * 4 + (1 + p), p)
                for p in (0, 1):
                    wait_apart(pool, "cross_high", high("cross_q", t, p))
                    g.tensor_tensor(qT["cross"][p][:], q_full[p][:], q_high["cross"][p][:], ALU.subtract
                                    ).then_inc(S("cross_q_ready"), 1)
                for p in (0, 1):
                    low_probs("cross", t * 4 + (3 + p))
                for p in (0, 1):
                    power(t * 4 + (3 + p), p)
                for p in (0, 1):
                    pool.wait_ge(S("x2_ready"), t * 2 + p + 1)
                    g.tensor_copy(x2_all[:, bass.ds(t * 2 + p, 1), :], x2[p][:].rearrange("q (b d) -> q b d", b=1)
                                  ).then_inc(S("x2_kept"), 1)

            pool.wait_ge(S("xb_zeroed"), 32)
            pool.wait_ge(S("put_ready"), 1)
            pool.wait_ge(S("x2_kept"), B)
            for b in range(B):
                for k in (0, 1):
                    g.indirect_dma_start(out=xb_dram, out_offset=bass.IndirectOffsetOnAxis(ap=put[:, k, b:b + 1], axis=0),
                                         in_=x2_all[:, b, :], in_offset=None, bounds_check=SLOTS - 1,
                                         oob_is_err=False).then_inc(S("scattered"), 16)
            pool.wait_ge(S("wb_loaded"), 16)
            g.tensor_tensor(x2b[:], x2_all[:], W("ffn_bias").rearrange("p (b d) -> p b d", b=1).broadcast_to([P, B, D]),
                            ALU.add).then_inc(S("x2b_ready"), 1)
            for p in (0, 1):
                pool.wait_ge(S(f"y_stored{p}"), 16 * PAIRS)
            pool.wait_ge(S("put_ready"), 1)
            for b in range(B):
                for k in (0, 1):
                    g.indirect_dma_start(out=got[k][:, b, :], out_offset=None, in_=y_dram,
                                         in_offset=bass.IndirectOffsetOnAxis(ap=get[:, k, b:b + 1], axis=0),
                                         bounds_check=SLOTS - 1, oob_is_err=False).then_inc(S(f"gathered{b // 4}"), 16)

            def power4(name):
                for h in (0, 1):
                    pool.wait_ge(S("ln4_var"), LN4[name] + h)
                    g.tensor_tensor(rstd4[h][:], var4[h][:], neg_half[:, 0:4], ALU.pow).then_inc(S("ln4_rstd"), 1)

            power4("x3")

            def fetch(u, p):
                b = u * 2 + p
                g.tensor_copy(x3T[p][:, 0:T], x3T_all[:, bass.ds(b * T, T)]).then_inc(S("x3T_here"), 1)
                g.tensor_copy(x3T[p][:, T:TX], x3T_all[:, bass.ds(b * T + (T - 1), 1)].broadcast_to([P, WIN])
                              ).then_inc(S("x3T_here"), 1)
                g.tensor_copy(ks[p][:, :, 0:T], k_all[:, :, bass.ds(b, 1), :].rearrange("q g b t -> q g (b t)")
                              ).then_inc(S("ks_here"), 1)
                g.tensor_copy(ks[p][:, :, T:TX], k_all[:, :, bass.ds(b, 1), T - 1:T]
                              .rearrange("q g b t -> q g (b t)").broadcast_to([P, G2, WIN])
                              ).then_inc(S("ks_here"), 1)

            def square_queries(u, p):
                pool.wait_ge(S("q_kept"), u * 4 + (2 * p + 1))
                g.tensor_tensor(qq[p][:], q_tok[p][:], q_tok[p][:], ALU.mult).then_inc(S("qq_ready"), 1)

            def distances(u, p):
                pool.wait_ge(S("sorted"), u * 128 + (p * 64 + NTILE))
                g.tensor_tensor(infl[p], best[p][:, 0, :, 0:1].broadcast_to([P, NTILE, SEEN]), score[p],
                                ALU.subtract).then_inc(S("dist2_ready"), 1)
                pool.wait_ge(S("q_n2_ready"), u * 2 + (p + 1))
                g.tensor_tensor(q_norm[p][:], q_n2[p][:], half[:, 0:NH], ALU.pow).then_inc(S("q_norm_ready"), 1)

            pool.wait_ge(S("k_all_ready"), 1)
            pool.wait_ge(S("wide_copied"), WIDE_TURNS["x3"] + 1)
            fetch(0, 0)
            square_queries(0, 0)
            distances(0, 0)
            fetch(0, 1)
            square_queries(0, 1)
            with pool.Fori(0, PAIRS - 1) as t:
                distances(t, 1)
                pool.wait_ge(S("win_scores"), t * 4 + 2)
                fetch(t + 1, 0)
                square_queries(t + 1, 0)
                distances(t + 1, 0)
                pool.wait_ge(S("win_scores"), t * 4 + 4)
                fetch(t + 1, 1)
                square_queries(t + 1, 1)
            distances(PAIRS - 1, 1)
            power4("x4")
            power4("x5")

            for i in (0, 1):
                pool.wait_ge(S(f"a_max_ready{i}"), 1)
                g.partition_all_reduce(a_top[i][:], a_max[i][:], P, bass.bass_isa.ReduceOp.max).then_inc(S(f"a_top_ready{i}"), 1)
            power4("final")

        @block.tensor
        def _(pe):
            mm = pe.matmul

            def project(a, what, n, p, src, dst_bank):
                w = A({"self": {"q": "wq", "k": "wk"}, "cross": {"q": "wq2", "k": "wk2"}}[a][what])
                width = src.shape[1]
                for gi in range(G):
                    last = mm(bank[dst_bank][:, gi * width:(gi + 1) * width], w[:, gi * P:(gi + 1) * P], src,
                              start=True, stop=True)
                last.then_inc(S(f"{a}_{what}_proj"), 1)

            def score_units(lhs, rhs, rows, width, name):
                for j0 in (0, 2):
                    for gi in range(G):
                        for j in (j0, j0 + 1):
                            last = mm(bank[j][0:rows, gi * width:(gi + 1) * width],
                                      lhs[32 * j:32 * j + 32, gi, :], rhs[32 * j:32 * j + 32, gi, :],
                                      start=True, stop=True)
                            if gi == G - 1:
                                last.then_inc(S(name), 1)

            def max_scores(a, n, m, p):
                pe.wait_ge(S(f"{a}_q_ready"), n)
                pe.wait_ge(S(f"{a}_k_ready"), n)
                if p == 1:
                    pe.wait_ge(S("max_ready"), (m - 1) * 4)
                score_units(qT[a][p], kT[a][p], T, KEYS[a], "scores")

            def turn_maxes(a, m, p):
                pe.wait_ge(S("max_ready"), m * 4)
                for gi in range(G):
                    last = mm(bank[WIDE[p]][:, gi * T:(gi + 1) * T], maxes[a][p][:, gi, :], ident_bf[:],
                              start=True, stop=True)
                last.then_inc(S("max_turned"), 1)

            def exp_scores(a, m, p, j0):
                K = KEYS[a]
                if j0 == 0:
                    pe.wait_ge(S("qm_ready"), m)
                for gi in range(G):
                    for j in (j0, j0 + 1):
                        last = mm(bank[j][0:K, gi * T:(gi + 1) * T], kT[a][p][32 * j:32 * j + 32, gi, :],
                                  qT[a][p][32 * j:32 * j + 32, gi, :], start=True, stop=True)
                        if gi == G - 1:
                            last.then_inc(S("scoresT"), 1)

            def weigh(a, n, m, p, j0):
                K = KEYS[a]
                for j in (j0, j0 + 1):
                    pe.wait_ge(S("probs_ready"), (m - 1) * 4 + (j + 1))
                    if j == 0:
                        pe.wait_ge(S(f"{a}_v_done"), n)
                    for gi in range(G):
                        h = 4 * gi + j
                        out_h = bank[WIDE[p]][:, h * (HD + 1):(h + 1) * (HD + 1)]
                        mm(out_h, p_high[j][0:K, gi, :], v_high[a][p][0:K, h, :], start=True, stop=False)
                        mm(out_h, p_high[j][0:K, gi, :], v_low[a][p][0:K, h, :], start=False, stop=False)
                        last = mm(out_h, p_low[j][0:K, gi, :], v_high[a][p][0:K, h, :], start=False, stop=True)
                    last.then_inc(S("weighed"), 1)

            def attend(a, n, m):
                pe.wait_ge(S("max_ready"), (m + 1) * 4)
                exp_scores(a, m, 0, 0)
                exp_scores(a, m, 0, 2)
                weigh(a, n, m, 0, 0)
                exp_scores(a, m + 1, 1, 0)
                weigh(a, n, m, 0, 2)
                exp_scores(a, m + 1, 1, 2)
                weigh(a, n + 1, m + 1, 1, 0)
                weigh(a, n + 1, m + 1, 1, 2)

            def turn(name, n, src, bank_no, rows=P):
                pe.wait_ge(S(f"{name}_ready"), n)
                pe.transpose(bank[bank_no][0:rows, 0:P], src, ident).then_inc(S("turned"), 1)

            pe.wait_ge(S("wa_loaded"), 16)
            pe.wait_ge(S("pool_consts"), 19)
            pe.wait_ge(S("ident_bf_ready"), 1)

            pe.wait_ge(S("w_clip_ready"), 1)
            for i in (0, 1):
                for c in range(FC):
                    last = pe.transpose(bank[i][:, c * P:(c + 1) * P], w_clip[:, i, c * P:(c + 1) * P], ident)
                last.then_inc(S("wq_turned"), 1)
            pe.wait_ge(S("wq_kept"), 2)

            with pe.Fori(0, PAIRS) as t:
                n0 = t * 2 + 1
                for p in (0, 1):
                    pe.wait_ge(S(f"xT_loaded{p}"), (t + 1) * 16)
                    project("self", "q", n0 + p, p, xT_in[p][:], MISC[p])
                    project("self", "k", n0 + p, p, xT_in[p][:], WIDE[p])
                for p in (0, 1):
                    pe.wait_ge(S("self_q_ready"), n0 + p)
                    mm(bank[MISC[p]][:, 0:D], xT_in[p][:], A("wv"), start=True, stop=True).then_inc(S("self_v_proj"), 1)
                for p in (0, 1):
                    max_scores("self", n0 + p, t * 4 + (1 + p), p)
                pe.wait_ge(S("wa2_loaded"), 16)
                for p in (0, 1):
                    pe.wait_ge(S("self_v_done"), n0 + p)
                    pe.wait_ge(S(f"cT_loaded{p}"), (t + 1) * 16)
                    project("cross", "k", n0 + p, p, cT_in[p][:], MISC[p])
                for p in (0, 1):
                    turn_maxes("self", t * 4 + (1 + p), p)
                attend("self", n0, t * 4 + 1)
                for p in (0, 1):
                    pe.wait_ge(S("cross_k_ready"), n0 + p)
                    mm(bank[MISC[p]][0:CTX, 0:D], cT_in[p][:], A("wv2"), start=True, stop=False)
                    mm(bank[MISC[p]][0:CTX, 0:D], ones_row[0:1, 0:CTX], A("bv2", 1), start=False, stop=True
                       ).then_inc(S("cross_v_proj"), 1)
                for p in (0, 1):
                    pe.wait_ge(S("cross_v_done"), n0 + p)
                    turn("x1", n0 + p, x1[p][:], MISC[p])
                for p in (0, 1):
                    pe.wait_ge(S("turned_copied"), turned("x1", t, p))
                    project("cross", "q", n0 + p, p, x1T[p][:], WIDE[p])
                for p in (0, 1):
                    max_scores("cross", n0 + p, t * 4 + (3 + p), p)
                for p in (0, 1):
                    turn_maxes("cross", t * 4 + (3 + p), p)
                attend("cross", n0, t * 4 + 3)
                for p in (0, 1):
                    turn("attn2", n0 + p, attn[p][:], MISC[p])
                for p in (0, 1):
                    pe.wait_ge(S("turned_copied"), turned("attn2", t, p))
                    mm(bank[MISC[p]][:, 0:D], a2T[p][:], A("wo"), start=True, stop=False)
                    mm(bank[MISC[p]][:, 0:D], ones_row[:], A("bo", 1), start=False, stop=True).then_inc(S("wo_done"), 1)
                for p in (0, 1):
                    turn("x2", n0 + p, x2[p][:], WIDE[p])
                for p in (0, 1):
                    pe.wait_ge(S("turned_copied"), turned("x2", t, p))
                    mm(bank[MISC[p]][:, 0:E], x2T[p][:], A("router"), start=True, stop=True).then_inc(S("routed"), 1)
                pe.wait_ge(S("logits_ready"), t * 2 + 2)

            pe.wait_ge(S("chosen_ready"), 1)
            pe.wait_ge(S("tri_ready"), 1)
            mm(bank[0][:, 0:B * E], tri_bf[:], chosen[:].rearrange("p b e -> p (b e)"), start=True, stop=False)
            for b in range(B - 1):
                later = B - 1 - b
                last = mm(bank[0][:, (b + 1) * E:B * E], ones_bf[:], chosen[:, b:b + 1, :].broadcast_to([P, later, E]),
                          start=False, stop=(b == B - 2))
            last.then_inc(S("places"), 1)

            pe.wait_ge(S("place_ready"), 1)
            with pe.Fori(0, PAIRS) as t:
                for p in (0, 1):
                    e1 = t * 2 + p + 1
                    pe.wait_ge(S(f"xb_loaded{p}"), (t + 1) * 16)
                    for h in (0, 1):
                        last = pe.transpose(bank[p][:, h * P:(h + 1) * P], xb_in[p][:, h, :], ident)
                    last.then_inc(S("xb_turned"), 1)
                for p in (0, 1):
                    e1 = t * 2 + p + 1
                    pe.wait_ge(S("xbT_ready"), e1)
                    pe.wait_ge(S(f"w_loaded{p}"), (t + 1) * 32)
                    for c in range(FC):
                        last = mm(bank[2 + 2 * p + c // 2][:, (c % 2) * CAP:(c % 2 + 1) * CAP],
                                  w1_in[p][:, c * P:(c + 1) * P], xbT[p][:], start=True, stop=True)
                        if c % 2:
                            last.then_inc(S("hidden_done"), 1)
                for p in (0, 1):
                    e1 = t * 2 + p + 1
                    pe.wait_ge(S("hT_ready"), e1 * 2)
                    for h in (0, 1):
                        for c in range(FC):
                            last = mm(bank[6 + p][:, h * D:(h + 1) * D], hT[p][:, c, h * P:(h + 1) * P],
                                      w2_in[p][:, c, :], start=(c == 0), stop=(c == FC - 1))
                    last.then_inc(S("y_done"), 1)

            def turn4(name, src_of, banks, rows=P):
                for h in (0, 1):
                    for i in range(4):
                        if i % 4 == 0:
                            pe.wait_ge(S(f"{name}_ready"), 4 * h + 4)
                        last = pe.transpose(bank[banks[h]][0:rows, i * P:(i + 1) * P], src_of(4 * h + i), ident)
                    last.then_inc(S("wide_turned"), 1)

            pe.wait_ge(S("yb_ready"), E)
            turn4("x3", lambda b: x3_all[:, b, :], (0, 1))

            pe.wait_ge(S("wide_copied"), WIDE_TURNS["x3"] + 1)
            for gi in range(G2):
                for h in (0, 1):
                    mm(bank[4 + 2 * gi + h][:], W("key_w")[:, gi * P:(gi + 1) * P], x3T_all[:, h * 512:(h + 1) * 512],
                       start=True, stop=True).then_inc(S("u_done"), 1)
            for gi in range(G2):
                last = mm(bank[2][:, gi * 64:(gi + 1) * 64], W("heb_u", 16)[:, gi * P:(gi + 1) * P],
                          W("heb_v", 16)[:, gi * 64:(gi + 1) * 64], start=True, stop=True)
            last.then_inc(S("heb_done"), 1)
            pe.wait_ge(S("sig_ready"), 1)
            for gi in range(G2):
                last = mm(bank[0][0:HID, 0:B], W("mn_w1")[:, gi * HID:(gi + 1) * HID], sig[:, gi, :],
                          start=(gi == 0), stop=(gi == G2 - 1))
            last.then_inc(S("mn_hidden"), 1)
            pe.wait_ge(S("mn_gelu"), 1)
            for gi in range(G2):
                last = mm(bank[1][:, gi * B:(gi + 1) * B], W("mn_w2", HID)[:, gi * P:(gi + 1) * P], hidden[:],
                          start=True, stop=True)
            last.then_inc(S("mn_mod"), 1)

            def window_scores(u, p, first=False):
                b = u * 2 + p
                pe.wait_ge(S("x3T_here"), b * 2 + 2)
                pe.wait_ge(S("ks_here"), b * 2 + 2)
                if not first:
                    pe.wait_ge(S("q_kept"), b * 2)
                mm(bank[7][:, 0:D], x3T[p][:, 0:T], W("qv_w")[:, 0:D], start=True, stop=True)
                for gi in range(G2):
                    last = mm(bank[7][:, D + gi * 64:D + (gi + 1) * 64], ks[p][:, gi, 0:T], heb[:, gi, :],
                              start=True, stop=True)
                last.then_inc(S("q_done"), 1)
                if not first:
                    pe.wait_ge(S("v_kept"), b)
                for q in range(4):
                    last = mm(bank[0][0:SEEN, q * D:(q + 1) * D], x3T[p][:, q * QUARTER:q * QUARTER + SEEN],
                              W("qv_w")[:, D:2 * D], start=True, stop=True)
                last.then_inc(S("v_done"), 1)
                if not first:
                    pe.wait_ge(S("score_ready"), b * 2)
                wait_apart(pe, "qs_ready", b * 2 + 2)
                for q in range(4):
                    for gi in range(G2):
                        at = (gi * 2 + q % 2) * SEEN
                        for j in range(4):
                            rows = slice(32 * j, 32 * j + 32)
                            last = mm(bank[1 + q // 2][rows, at:at + SEEN],
                                      qs[p][rows, gi, q * QUARTER:(q + 1) * QUARTER],
                                      ks[p][rows, gi, q * QUARTER:q * QUARTER + SEEN], start=True, stop=True)
                    if q % 2:
                        last.then_inc(S("win_scores"), 1)

            def window_context(u, p, first=False):
                b = u * 2 + p
                pe.wait_ge(S("kept_ready"), b + 1)
                for h in (0, 1):
                    for i in range(4):
                        last = pe.transpose(bank[3 + h][0:SEEN, i * P:(i + 1) * P], kept[p][:, 4 * h + i, :], ident)
                    last.then_inc(S("kept_turned"), 1)
                pe.wait_ge(S("keptT_ready"), b * 2 + 2)
                if not first:
                    pe.wait_ge(S("both_ready"), b)
                for q in range(4):
                    for h in range(NH):
                        gi, j = h // 4, h % 4
                        last = mm(bank[5][32 * q:32 * q + 32, h * (HE + 1):(h + 1) * (HE + 1)],
                                  keptT[:, q // 2 * 4 + gi * 2 + q % 2, 32 * j:32 * j + 32], vw[p][:, q, h, :],
                                  start=True, stop=True)
                last.then_inc(S("win_context"), 1)

            def turn_sparse(u):
                pe.wait_ge(S("sparse_ready"), u * 2 + 2)
                for p in (0, 1):
                    last = pe.transpose(bank[6][:, p * T:(p + 1) * T], sparse[p][:], ident)
                last.then_inc(S("sparse_turned"), 1)

            pe.wait_ge(S("heb_kept"), 1)
            window_scores(0, 0, first=True)
            window_scores(0, 1)
            window_context(0, 0, first=True)
            with pe.Fori(0, PAIRS - 1) as t:
                window_scores(t + 1, 0)
                window_context(t, 1)
                window_scores(t + 1, 1)
                turn_sparse(t)
                window_context(t + 1, 0)
                pe.wait_ge(S("sparse_copied"), t + 1)
            window_context(PAIRS - 1, 1)
            turn_sparse(PAIRS - 1)

            for h in (0, 1):
                pe.wait_ge(S("sparse_copied"), 2 * h + 2)
                for i in range(4):
                    b = 4 * h + i
                    last = mm(bank[h][:, i * D:(i + 1) * D], sparseT_all[:, b * T:(b + 1) * T], W("decoder"),
                              start=True, stop=True)
                last.then_inc(S("decoded"), 1)
            turn4("x4", lambda b: x4_all[:, b, :], (2, 3))
            pe.wait_ge(S("ctx_loaded"), 32)
            for h in (0, 1):
                pe.wait_ge(S("wide_copied"), WIDE_TURNS["x4"] + h)
                for i in range(4):
                    b = 4 * h + i
                    last = mm(bank[4 + h][:, i * CTX:(i + 1) * CTX], x4T_all[:, b * T:(b + 1) * T], cT_all[:, b, :],
                              start=True, stop=True)
                last.then_inc(S("plain_scores"), 1)
            turn4("pr", lambda b: pr_all[:, b, :], (6, 7), CTX)
            for h in (0, 1):
                pe.wait_ge(S("wide_copied"), WIDE_TURNS["pr"] + h)
                for i in range(4):
                    b = 4 * h + i
                    last = mm(bank[h][:, i * D:(i + 1) * D], prT_all[:, b * T:(b + 1) * T], c_all[:, b, :],
                              start=True, stop=True)
                last.then_inc(S("plain_out"), 1)
            turn4("x5", lambda b: x5_all[:, b, :], (2, 3))

            pe.wait_ge(S("xq_ready"), 1)
            pe.wait_ge(S("wide_copied"), WIDE_TURNS["x5"] + 1)
            for c in range(FC):
                for h in (0, 1):
                    mm(bank[2 * c + h][:], w1q[:, c * P:(c + 1) * P], xq[:, h * 512:(h + 1) * 512],
                       start=True, stop=True).then_inc(S("ff_hidden"), 1)
            for c in range(FC):
                pe.wait_ge(S("hq_ready"), c + 1)
                for h in (0, 1):
                    last = mm(bank[h][:], w2q[:, c, :], hq[:, c, h * 512:(h + 1) * 512],
                              start=(c == 0), stop=(c == FC - 1))
                    if c == FC - 1:
                        last.then_inc(S("ff_done"), 1)
            for h in (0, 1):
                pe.wait_ge(S("zT_ready"), h + 1)
                for i in range(4):
                    last = pe.transpose(bank[2 + h][:, i * D:(i + 1) * D], zT[:, (4 * h + i) * T:(4 * h + i + 1) * T], ident)
                last.then_inc(S("z_turned"), 1)

        @block.scalar
        def _(act):
            sc = nc.scalar

            def copy_turned(name, t, p, dst, bank_no, rows=P):
                act.wait_ge(S("turned"), turned(name, t, p))
                sc.activation(dst, bank[bank_no][0:rows, 0:P], ACT.Copy).then_inc(S("turned_copied"), 1)

            def exps_of(a, n, p, j0):
                K = KEYS[a]
                for j in (j0, j0 + 1):
                    act.wait_ge(S("scoresT"), (n - 1) * 4 + (j + 1))
                    if p == 1:
                        act.wait_ge(S("weighed"), (n - 2) * 4 + (j + 1))
                    sc.activation(probs_all[0:K, j * G * T:(j + 1) * G * T], bank[j][0:K, :], ACT.Exp,
                                  scale=SCALE[a]).then_inc(S("exp_ready"), 1)
                for j in (j0, j0 + 1):
                    act.wait_ge(S("exp_ready"), (n - 1) * 4 + (j + 1))
                    sc.activation(p_high[j][0:K], probs[j][0:K], ACT.Copy).then_inc(S("p_high_ready"), 1)

            act.wait_ge(S("wa_loaded"), 16)
            for i in (0, 1):
                act.wait_ge(S("wq_turned"), i + 1)
                dst = w1q[:] if i == 0 else w2q[:].rearrange("p c d -> p (c d)")
                sc.activation(dst, bank[i][:], ACT.Copy).then_inc(S("wq_kept"), 1)
            with act.Fori(0, PAIRS) as t:
                n0 = t * 2 + 1
                for p in (0, 1):
                    act.wait_ge(S("self_q_proj"), n0 + p)
                    sc.activation(q_high["self"][p][:].rearrange("q g t -> q (g t)"), bank[MISC[p]][:], ACT.Identity,
                                  scale=A("q_low")).then_inc(S("self_high"), 1)
                    act.wait_ge(S("self_k_proj"), n0 + p)
                    sc.activation(k_high["self"][p][:].rearrange("q g t -> q (g t)"), bank[WIDE[p]][:], ACT.Identity,
                                  bias=A("k_bias"), scale=A("k_low")).then_inc(S("self_high"), 1)
                for p in (0, 1):
                    act.wait_ge(S("self_v_proj"), n0 + p)
                    sc.activation(v_high["self"][p][:, :, 0:HD], bank[MISC[p]][:, 0:D].rearrange("q (h d) -> q h d", h=HEADS),
                                  ACT.Copy).then_inc(S("self_high"), 1)
                for p in (0, 1):
                    act.wait_ge(S("cross_k_full"), n0 + p)
                    sc.activation(k_high["cross"][p][:], k_full[p][:], ACT.Identity, bias=A("k_bias"), scale=A("k_low")).then_inc(S("cross_high"), 1)
                for p in (0, 1):
                    exps_of("self", t * 4 + (1 + p), p, 0)
                    exps_of("self", t * 4 + (1 + p), p, 2)
                for p in (0, 1):
                    act.wait_ge(S("cross_v_proj"), n0 + p)
                    sc.activation(v_high["cross"][p][0:CTX, :, 0:HD],
                                  bank[MISC[p]][0:CTX, 0:D].rearrange("q (h d) -> q h d", h=HEADS),
                                  ACT.Copy).then_inc(S("cross_high"), 1)
                for p in (0, 1):
                    copy_turned("x1", t, p, x1T[p][:], MISC[p])
                for p in (0, 1):
                    act.wait_ge(S("cross_q_full"), n0 + p)
                    sc.activation(q_high["cross"][p][:], q_full[p][:], ACT.Identity, scale=A("q_low")).then_inc(S("cross_high"), 1)
                for p in (0, 1):
                    exps_of("cross", t * 4 + (3 + p), p, 0)
                    exps_of("cross", t * 4 + (3 + p), p, 2)
                for p in (0, 1):
                    copy_turned("attn2", t, p, a2T[p][:], MISC[p])
                for p in (0, 1):
                    copy_turned("x2", t, p, x2T[p][:], WIDE[p])
                for p in (0, 1):
                    act.wait_ge(S("routed"), n0 + p)
                    sc.activation(logits[:, bass.ds(t * 2 + p, 1), :].rearrange("q b e -> q (b e)"),
                                  bank[MISC[p]][:, 0:E], ACT.Copy).then_inc(S("logits_ready"), 1)

            act.wait_ge(S("shifted_ready"), 2)
            sc.activation(exps[:], shifted[:], ACT.Exp).then_inc(S("exps_ready"), 1)
            sc.activation(exp_gap[:], gap[:], ACT.Exp).then_inc(S("exps_ready"), 1)

            def expert_pair(t, more):
                for p in (0, 1):
                    e1 = t * 2 + p + 1
                    act.wait_ge(S("xb_turned"), e1)
                    sc.activation(xbT[p][:], bank[p][:, 0:CAP], ACT.Copy).then_inc(S("xbT_ready"), 1)
                for p in (0, 1):
                    e1 = t * 2 + p + 1
                    for h in (0, 1):
                        act.wait_ge(S("hidden_done"), (e1 - 1) * 2 + (h + 1))
                        sc.activation(hT[p][:, 2 * h:2 * h + 2, :].rearrange("q c s -> q (c s)"), bank[2 + 2 * p + h][:],
                                      ACT.Gelu_apprx_tanh).then_inc(S("hT_ready"), 1)
                for p in (0, 1):
                    e1 = t * 2 + p + 1
                    if more:
                        act.wait_ge(S("y_done"), e1)
                        act.dma_start(w1_in[p][:], w1[bass.ds(t * 2 + (2 + p), 1)].rearrange("e d f -> (e d) f")
                                      ).then_inc(S(f"w_loaded{p}"), 16)
                        act.dma_start(w2_in[p][:], w2[bass.ds(t * 2 + (2 + p), 1)].rearrange("e f c d -> (e f) c d")
                                      ).then_inc(S(f"w_loaded{p}"), 16)

            with act.Fori(0, PAIRS - 1) as t:
                expert_pair(t, True)
            expert_pair(PAIRS - 1, False)

            def copy4(name, dst, banks, rows=P):
                for h in (0, 1):
                    act.wait_ge(S("wide_turned"), WIDE_TURNS[name] + h)
                    sc.activation(dst[:, COLS4[h]], bank[banks[h]][0:rows, :], ACT.Copy).then_inc(S("wide_copied"), 1)

            copy4("x3", x3T_all[:], (0, 1))
            for gi in range(G2):
                for h in (0, 1):
                    act.wait_ge(S("u_done"), gi * 2 + h + 1)
                    sc.activation(uT[:, gi, 4 * h:4 * h + 4, :].rearrange("q b t -> q (b t)"), bank[4 + 2 * gi + h][:],
                                  ACT.Relu).then_inc(S("uT_ready"), 1)
            act.wait_ge(S("heb_done"), 1)
            sc.activation(heb[:].rearrange("q g c -> q (g c)"), bank[2][:, 0:G2 * 64], ACT.Copy).then_inc(S("heb_kept"), 1)
            act.wait_ge(S("mn_hidden"), 1)
            sc.activation(hidden[:], bank[0][0:HID, 0:B], ACT.Gelu, bias=W("mn_b1", HID)).then_inc(S("mn_gelu"), 1)
            act.wait_ge(S("zabs_ready"), 1)
            sc.activation(zexp[:], zabs[:], ACT.Exp, scale=-1.0).then_inc(S("zexp_ready"), 1)
            act.wait_ge(S("zexp_ready"), 1)
            sc.activation(zln[:], zexp[:], ACT.Ln, bias=1.0).then_inc(S("zln_ready"), 1)

            act.wait_ge(S("q_coef_ready"), 2)

            def window_queries(u, p):
                b = u * 2 + p
                for gi in range(G2):
                    sc.activation(qs[p][:, gi, :], uT[:, gi, bass.ds(b, 1), :].rearrange("q b t -> q (b t)"),
                                  ACT.Identity, bias=q_bias[:, gi, bass.ds(b, 1)],
                                  scale=q_scale[:, gi, bass.ds(b, 1)]).then_inc(S("qs_ready"), 1)

            def keep_values(u, p):
                n = u * 2 + (p + 1)
                act.wait_ge(S("q_done"), n)
                sc.activation(q_tok[p][:], bank[7][:, 0:D], ACT.Relu).then_inc(S("q_kept"), 1)
                sc.activation(heb_raw[p][:], bank[7][:, D:2 * D], ACT.Copy).then_inc(S("q_kept"), 1)
                act.wait_ge(S("v_done"), n)
                sc.activation(vw[p][:, :, :, 0:HE], bank[0][0:SEEN, :].rearrange("q (s h e) -> q s h e", s=4, h=NH),
                              ACT.Relu).then_inc(S("v_kept"), 1)

            def influence(u, p):
                n = u * 2 + (p + 1)
                act.wait_ge(S("dist2_ready"), n)
                sc.activation(infl[p], infl[p], ACT.Sqrt, bias=tiny[:]).then_inc(S("dist_ready"), 1)
                act.wait_ge(S("dist_ready"), n)
                sc.activation(infl[p], infl[p], ACT.Exp, scale=-1.0).then_inc(S("infl_ready"), 1)

            def keep_weights(u, p):
                for h in (0, 1):
                    act.wait_ge(S("kept_turned"), u * 4 + (2 * p + h + 1))
                    sc.activation(keptT[:, 4 * h:4 * h + 4, :].rearrange("q n t -> q (n t)"), bank[3 + h][0:SEEN, :],
                                  ACT.Copy).then_inc(S("keptT_ready"), 1)

            window_queries(0, 0)
            keep_values(0, 0)
            influence(0, 0)
            window_queries(0, 1)
            keep_values(0, 1)
            keep_weights(0, 0)
            with act.Fori(0, PAIRS - 1) as t:
                influence(t, 1)
                window_queries(t + 1, 0)
                act.wait_ge(S("sparse_ready"), t * 2 + 1)
                keep_values(t + 1, 0)
                keep_weights(t, 1)
                influence(t + 1, 0)
                window_queries(t + 1, 1)
                act.wait_ge(S("sparse_ready"), t * 2 + 2)
                keep_values(t + 1, 1)
                act.wait_ge(S("sparse_turned"), t + 1)
                sc.activation(sparseT_all[:, bass.ds(t * 2 * T, 2 * T)], bank[6][:, 0:2 * T], ACT.Copy
                              ).then_inc(S("sparse_copied"), 1)
                keep_weights(t + 1, 0)
            influence(PAIRS - 1, 1)
            keep_weights(PAIRS - 1, 1)
            act.wait_ge(S("sparse_turned"), PAIRS)
            sc.activation(sparseT_all[:, (B - 2) * T:B * T], bank[6][:, 0:2 * T], ACT.Copy).then_inc(S("sparse_copied"), 1)

            copy4("x4", x4T_all, (2, 3))
            for b in range(B):
                act.wait_ge(S("neg_max_ready"), b // 4 + 1)
                sc.activation(pr_all[:, b, :], bank[4 + b // 4][:, b % 4 * CTX:(b % 4 + 1) * CTX], ACT.Exp,
                              bias=neg_max[:, b:b + 1], accum_out=pr_sum[:, b:b + 1]).then_inc(S("pr_ready"), 1)
            copy4("pr", prT_all, (6, 7), CTX)
            copy4("x5", x5T, (2, 3))

            act.wait_ge(S("ff_coef_ready"), 1)
            for c in range(FC):
                for h in (0, 1):
                    act.wait_ge(S("ff_hidden"), 2 * c + h + 1)
                    sc.activation(hid[:, c, h * 512:(h + 1) * 512], bank[2 * c + h][:], ACT.Relu, bias=b_q[0][:, c:c + 1],
                                  scale=o_step[0][:, c:c + 1]).then_inc(S("hid_ready"), 1)
            act.wait_ge(S("ff2_coef_ready"), 1)
            for h in (0, 1):
                act.wait_ge(S("ff_done"), h + 1)
                sc.activation(ff_out[:, h * 512:(h + 1) * 512], bank[h][:], ACT.Identity, bias=b_q[1][:],
                              scale=o_step[1][:]).then_inc(S("ff_out_ready"), 1)

        @block.vector
        def _(dve):
            v = nc.vector

            class Steps:

                def __init__(self, name, per=0):
                    self.name, self.per, self.n, self.t = name, per, 0, None

                def turn(self, t):
                    self.n, self.t = 0, t

                def add(self, instruction):
                    instruction.then_inc(S(self.name), 1)
                    self.n += 1

                def wait(self):
                    dve.wait_ge(S(self.name), self.n if self.t is None else self.t * self.per + self.n)

                def wait_apart(self):
                    wait_apart(dve, self.name, self.t * self.per + self.n)

                def link(self, instruction):
                    self.add(instruction)
                    self.wait()

            def layernorm_stats(chain, src):
                p = chain.parity
                chain.add(v.bn_stats(stats[p][:], src))
                chain.wait_apart()
                chain.link(v.bn_aggr(mv[p][:], stats[p][:]))
                v.tensor_scalar(var_eps[p][:], mv[p][:, 1:2], LN_EPS, None, ALU.add).then_inc(S("ln_var"), 1)

            def layernorm_apply(n, out_name, p, src, dst):
                dve.wait_ge(S("ln_rstd"), n)
                v.tensor_scalar(dst, src, mv[p][:, 0:1], rstd[p][:], ALU.subtract, ALU.mult).then_inc(S(out_name), 1)

            def chains(name, per):
                pair = [Steps(f"{name}{p}", per) for p in (0, 1)]
                for p in (0, 1):
                    pair[p].parity = p
                return pair

            def row_maxes(a, n, p):
                K = KEYS[a]
                for j in range(J):
                    dve.wait_ge(S("scores"), (n - 1) * 4 + (j + 1))
                    v.tensor_reduce(maxes[a][p][:, :, 32 * j + MAXROW], bank[j][:, 0:G * K].rearrange("q (g k) -> q g k", g=G),
                                    AX.X, ALU.max).then_inc(S("max_ready"), 1)

            def lower_queries(a, n, p):
                dve.wait_ge(S("max_turned"), n)
                qf = qT[a][p][:].rearrange("q g t -> q (g t)")
                v.tensor_tensor(qf, qf, bank[WIDE[p]][:], ALU.subtract).then_inc(S("qm_ready"), 1)

            def low_values(a, n, t, p, K):
                dve.wait_ge(S(f"{a}_high"), high(f"{a}_v", t, p))
                v.tensor_tensor(v_low[a][p][0:K, :, 0:HD], bank[MISC[p]][0:K, 0:D].rearrange("q (h d) -> q h d", h=HEADS),
                                v_high[a][p][0:K, :, 0:HD], ALU.subtract).then_inc(S(f"{a}_v_done"), 1)

            def normalise(a, m, p):
                dve.wait_ge(S("weighed"), m * 4)
                o = bank[WIDE[p]][:, 0:HEADS * (HD + 1)].rearrange("q (h c) -> q h c", h=HEADS)
                chain[p].link(v.reciprocal(rec[p][:], o[:, :, HD]))
                out_of = v.tensor_tensor(attn[p][:].rearrange("q (h d) -> q h d", h=HEADS), o[:, :, 0:HD],
                                rec[p][:].rearrange("q (h d) -> q h d", d=1).broadcast_to([P, HEADS, HD]), ALU.mult)
                if a == "self":
                    chain[p].link(out_of)
                else:
                    out_of.then_inc(S("attn2_ready"), 1)

            steps = Steps("step")
            dve.wait_ge(S("wb_loaded"), 16)
            dve.wait_ge(S("pool_consts"), 19)
            steps.add(v.tensor_reduce(w_abs[:, 0:FC], W("w1f").rearrange("p (c d) -> p c d", c=FC), AX.X, ALU.max,
                            apply_absolute_value=True))
            steps.add(v.tensor_reduce(w_abs[:, FC:FC + 1], W("w2f"), AX.X, ALU.max, apply_absolute_value=True
                            ))
            v.tensor_copy(tri_bf[:], W("tri")).then_inc(S("tri_ready"), 1)
            steps.add(v.tensor_scalar(two_key[:], W("is_square"), -2.0, 2.0, ALU.mult, ALU.add))
            steps.add(v.tensor_scalar(not_square[:], W("is_square"), -1.0, 1.0, ALU.mult, ALU.add))
            steps.add(v.tensor_scalar(neg_square[:], W("is_square"), -1.0, None, ALU.mult))
            dve.wait_ge(S("wa_loaded"), 16)
            v.tensor_copy(ident_bf[:], ident).then_inc(S("ident_bf_ready"), 1)
            dve.wait_ge(S("wa2_loaded"), 16)
            steps.wait()
            steps.link(v.tensor_scalar(w_floor[:], w_abs[:], 1e-8, None, ALU.max))
            steps.link(v.tensor_scalar(w_step[:], w_floor[:], 1.0 / 127.0, None, ALU.mult))
            steps.link(v.reciprocal(w_rec[:], w_step[:]))
            for i in range(FC + 1):
                src, dst = (W("w1f"), w_div[:, 0, :]) if i < FC else (W("w2f"), w_div[:, 1, :])
                cols = slice(i * P, (i + 1) * P) if i < FC else slice(0, FF)
                steps.add(v.tensor_scalar(dst[:, cols], src[:, cols], w_rec[:, i:i + 1], ROUND, ALU.mult, ALU.add))
            steps.wait()
            steps.link(v.tensor_scalar(w_int, w_div, ROUND, 127.0, ALU.subtract, ALU.min))
            v.tensor_scalar(w_clip, w_int, -128.0, None, ALU.max).then_inc(S("w_clip_ready"), 1)

            chain = chains("att_step", 8)
            with dve.Fori(0, PAIRS) as t:
                n0 = t * 2 + 1
                for p in (0, 1):
                    chain[p].turn(t)
                for p in (0, 1):
                    for which, high_of, out_of, dst_bank in (("q", q_high, qT, MISC), ("k", k_high, kT, WIDE)):
                        dve.wait_ge(S("self_high"), high(f"self_{which}", t, p))
                        v.tensor_tensor(out_of["self"][p][:].rearrange("q g t -> q (g t)"), bank[dst_bank[p]][:],
                                        high_of["self"][p][:].rearrange("q g t -> q (g t)"), ALU.subtract
                                        ).then_inc(S(f"self_{which}_ready"), 1)
                for p in (0, 1):
                    low_values("self", n0 + p, t, p, T)
                for p in (0, 1):
                    row_maxes("self", t * 4 + (1 + p), p)
                for p in (0, 1):
                    dve.wait_ge(S("cross_k_proj"), n0 + p)
                    v.tensor_tensor(k_full[p][:], bank[MISC[p]][:, 0:G * CTX].rearrange("q (g c) -> q g c", g=G),
                                    A("bk2").rearrange("q (g c) -> q g c", c=1).broadcast_to([P, G, CTX]), ALU.add
                                    ).then_inc(S("cross_k_full"), 1)
                for p in (0, 1):
                    lower_queries("self", t * 4 + (1 + p), p)
                for p in (0, 1):
                    normalise("self", t * 4 + (1 + p), p)
                    dve.wait_ge(S(f"x_loaded{p}"), (t + 1) * 16)
                    v.tensor_tensor(y_sum[p][:], attn[p][:], x_in[p][:], ALU.add).then_inc(S("self_sum_done"), 1)
                    dve.wait_ge(S("self_sum_done"), n0 + p)
                    layernorm_stats(chain[p], y_sum[p][:])
                for p in (0, 1):
                    low_values("cross", n0 + p, t, p, CTX)
                for p in (0, 1):
                    layernorm_apply(t * 4 + (1 + p), "x1_ready", p, y_sum[p][:], x1[p][:])
                for p in (0, 1):
                    dve.wait_ge(S("cross_q_proj"), n0 + p)
                    v.tensor_tensor(q_full[p][:], bank[WIDE[p]][:].rearrange("q (g c) -> q g c", g=G),
                                    A("bq2").rearrange("q (g c) -> q g c", c=1).broadcast_to([P, G, T]), ALU.add
                                    ).then_inc(S("cross_q_full"), 1)
                for p in (0, 1):
                    row_maxes("cross", t * 4 + (3 + p), p)
                for p in (0, 1):
                    lower_queries("cross", t * 4 + (3 + p), p)
                for p in (0, 1):
                    normalise("cross", t * 4 + (3 + p), p)
                for p in (0, 1):
                    dve.wait_ge(S("wo_done"), n0 + p)
                    chain[p].link(v.tensor_tensor(y_sum[p][:], bank[MISC[p]][:, 0:D], x1[p][:], ALU.add))
                    layernorm_stats(chain[p], y_sum[p][:])
                for p in (0, 1):
                    layernorm_apply(t * 4 + (3 + p), "x2_ready", p, y_sum[p][:], x2[p][:])

            dve.wait_ge(S("logits_ready"), B)
            for b in range(B):
                steps.add(v.max(top8[:, b, :], logits[:, b, :]))
            steps.wait()
            for b in range(B):
                steps.add(v.max_index(index8[:, b, :], top8[:, b, :], logits[:, b, :]))
            v.tensor_tensor(shifted[:], logits[:], top8[:, :, 0:1].broadcast_to([P, B, E]), ALU.subtract
                            ).then_inc(S("shifted_ready"), 1)
            v.tensor_tensor(gap[:], top8[:, :, 1], top8[:, :, 0], ALU.subtract).then_inc(S("shifted_ready"), 1)
            steps.wait()
            steps.link(v.tensor_copy(index_f[:], index8[:, :, 0:2]))
            for k in (0, 1):
                steps.add(v.tensor_tensor(onehot[k][:], W("iota_e").rearrange("p (b e) -> p b e", b=1).broadcast_to([P, B, E]),
                                index_f[:, :, k:k + 1].broadcast_to([P, B, E]), ALU.is_equal))
            steps.wait()
            v.tensor_tensor(chosen[:], onehot[0][:], onehot[1][:], ALU.add).then_inc(S("chosen_ready"), 1)
            dve.wait_ge(S("exps_ready"), 2)
            steps.link(v.tensor_reduce(denom[:], exps[:], AX.X, ALU.add))
            steps.add(v.reciprocal(gate[:, 0, :], denom[:]))
            steps.wait()
            steps.add(v.tensor_tensor(gate[:, 1, :], gate[:, 0, :], exp_gap[:], ALU.mult))
            dve.wait_ge(S("places"), 1)
            places = bank[0][:, 0:B * E].rearrange("p (b e) -> p b e", b=B)
            v.tensor_copy(place[:], places).then_inc(S("place_ready"), 1)
            dve.wait_ge(S("place_ready"), 1)
            steps.link(v.tensor_tensor(slot_of[:], place[:], W("slot_e").rearrange("p (b e) -> p b e", b=1).broadcast_to([P, B, E]),
                            ALU.add))
            for k in (0, 1):
                steps.add(v.tensor_tensor(picked[k][:], onehot[k][:], place[:], ALU.mult))
                steps.add(v.tensor_tensor(picked[2 + k][:], onehot[k][:], slot_of[:], ALU.mult))
            steps.wait()
            for k in (0, 1):
                steps.add(v.tensor_reduce(place_k[:, k, :], picked[k][:], AX.X, ALU.add))
                steps.add(v.tensor_reduce(slot_k[:, k, :], picked[2 + k][:], AX.X, ALU.add))
            steps.wait()
            steps.add(v.tensor_scalar(over[:], place_k[:], float(CAP), 2.0 * SLOTS, ALU.is_ge, ALU.mult))
            steps.add(v.tensor_scalar(fits[:], place_k[:], float(CAP), None, ALU.is_lt))
            steps.add(v.tensor_scalar(get_f[:], slot_k[:], float(SLOTS - 1), None, ALU.min))
            steps.wait()
            steps.link(v.tensor_tensor(put_f[:], slot_k[:], over[:], ALU.add))
            v.tensor_copy(put[:], put_f[:]).then_inc(S("put_ready"), 1)
            v.tensor_copy(get[:], get_f[:]).then_inc(S("put_ready"), 1)
            steps.wait()
            v.tensor_tensor(gates[:], gate[:], fits[:], ALU.mult).then_inc(S("gates_ready"), 1)

            dve.wait_ge(S("place_ready"), 1)
            v.memset(h_max[:, 0:2], 0.0).then_inc(S("xb_free"), 2)
            with dve.Fori(0, PAIRS) as t:
                for p in (0, 1):
                    e1 = t * 2 + p + 1
                    dve.wait_ge(S("xbT_ready"), e1)
                    v.memset(h_max[:, p:p + 1], 0.0).then_inc(S("xb_free"), 1)
                for p in (0, 1):
                    e1 = t * 2 + p + 1
                    dve.wait_ge(S("y_done"), e1)
                    v.tensor_copy(yb[p][:].rearrange("q h d -> q (h d)"), bank[6 + p][:, 0:2 * D]).then_inc(S("yb_ready"), 1)

            dve.wait_ge(S("gates_ready"), 1)
            dve.wait_ge(S("x2b_ready"), 1)
            def layernorm4_stats(h, y):
                for i in range(4):
                    steps.add(v.bn_stats(stats4[h][:, i, :], y(4 * h + i)))
                steps.wait()
                for i in range(4):
                    steps.add(v.bn_aggr(mv4[h][:, i, :], stats4[h][:, i, :]))
                steps.wait()
                v.tensor_scalar(var4[h][:], mv4[h][:, :, 1], LN_EPS, None, ALU.add).then_inc(S("ln4_var"), 1)

            def layernorm4_apply(name, h, y, out):
                dve.wait_ge(S("ln4_rstd"), LN4[name] + h)
                for i in range(4):
                    b = 4 * h + i
                    v.tensor_scalar(out(b), y(b), mv4[h][:, i, 0:1], rstd4[h][:, i:i + 1], ALU.subtract, ALU.mult
                                    ).then_inc(S(f"{name}_ready"), 1)

            for h in (0, 1):
                dve.wait_ge(S(f"gathered{h}"), 16 * 2 * 4)
                for k, before in ((0, x2b), (1, got[0])):
                    for b in range(4 * h, 4 * h + 4):
                        steps.add(v.scalar_tensor_tensor(got[k][:, b, :], got[k][:, b, :], gates[:, k, b:b + 1],
                                                        before[:, b, :], ALU.mult, ALU.add))
                    steps.wait()
                layernorm4_stats(h, lambda b: got[1][:, b, :])
            for h in (0, 1):
                layernorm4_apply("x3", h, lambda b: got[1][:, b, :], lambda b: x3_all[:, b, :])

            for gi in range(G2):
                dve.wait_ge(S("uT_ready"), 2 * gi + 2)
                steps.link(v.tensor_tensor(sig_p[:, gi], uT[:, gi], W("sig_w").rearrange("p (b t) -> p b t", b=1).broadcast_to([P, B, T]),
                                ALU.mult))
                v.tensor_reduce(sig[:, gi, :], sig_p[:, gi], AX.X, ALU.add).then_inc(S("sig_half"), 1)
            dve.wait_ge(S("sig_half"), 2)
            v.scalar_tensor_tensor(pre[:], W("mn_b2"), 0.1, W("base_metric"), ALU.mult, ALU.add).then_inc(S("sig_ready"), 1)
            steps.wait()
            for gi in range(G2):
                steps.link(v.tensor_scalar(sig_p[:, gi], uT[:, gi], W("is_square"), not_square[:], ALU.mult, ALU.add
                                ))
                v.tensor_tensor(k_all[:, gi], uT[:, gi], sig_p[:, gi], ALU.mult).then_inc(S("k_half"), 1)
            dve.wait_ge(S("k_half"), 2)
            dve.wait_ge(S("mn_mod"), 1)
            mod = bank[1][:, 0:G2 * B].rearrange("p (g b) -> p g b", g=G2)
            steps.link(v.scalar_tensor_tensor(zm[:], mod, 0.1, pre[:].rearrange("p (g b) -> p g b", b=1).broadcast_to([P, G2, B]),
                                   ALU.mult, ALU.add))
            v.scalar_tensor_tensor(zabs[:], zm[:], -1.0, zm[:], ALU.mult, ALU.max).then_inc(S("zabs_ready"), 1)
            steps.link(v.tensor_scalar(zpos[:], zm[:], 0.0, None, ALU.max))
            dve.wait_ge(S("zln_ready"), 1)
            steps.link(v.tensor_tensor(metric[:], zpos[:], zln[:], ALU.add))
            v.tensor_scalar(q_scale[:], metric[:], two_key[:], None, ALU.mult).then_inc(S("q_coef_ready"), 1)
            v.tensor_scalar(q_bias[:], metric[:], neg_square[:], None, ALU.mult).then_inc(S("q_coef_ready"), 1)
            v.memset(h_max[:, 0:1], 0.0).then_inc(S("k_all_ready"), 1)
            chain = chains("win_step", 8)
            mask = W("mask").rearrange("p (n w) -> p n w", n=1).broadcast_to([P, 4, SEEN])

            def keep_scores(u, p):
                for h in (0, 1):
                    dve.wait_ge(S("win_scores"), u * 4 + (2 * p + h + 1))
                    v.tensor_tensor(score[p][:, 4 * h:4 * h + 4, :],
                                    bank[1 + h][:, 0:HALF].rearrange("q (n w) -> q n w", w=SEEN), mask, ALU.add
                                    ).then_inc(S("score_ready"), 1)

            def weights(u, p, meanwhile=None):
                n = u * 2 + (p + 1)
                wait_apart(dve, "score_ready", u * 4 + (2 * p + 2))
                for r in range(TOPK // 8):
                    for op in (0, 1):
                        for i in range(NTILE):
                            src = score[p] if r == 0 else work[p]
                            if i % 4 == 0 and r + op > 0:
                                done = (r * 2 + op - 1) * NTILE + i + 4
                                wait_apart(dve, "sorted", u * 128 + (p * 64 + done))
                            if op == 0:
                                step = v.max(best[p][:, r, i, :], src[:, i, :])
                            else:
                                step = v.match_replace(work[p][:, i, :], best[p][:, r, i, :], src[:, i, :], TAKEN)
                            step.then_inc(S("sorted"), 1)
                    if r == 0:
                        dve.wait_ge(S("qq_ready"), n)
                        v.tensor_reduce(q_n2[p][:], qq[p][:].rearrange("q (h e) -> q h e", h=NH), AX.X, ALU.add
                                        ).then_inc(S("q_n2_ready"), 1)
                    if r == 1 and meanwhile is not None:
                        meanwhile()
                dve.wait_ge(S("infl_ready"), n)
                dve.wait_ge(S("sorted"), u * 128 + (p * 64 + 64))
                v.scalar_tensor_tensor(kept[p][:], work[p], 1.5 * MASKED, infl[p], ALU.is_le, ALU.mult
                                       ).then_inc(S("kept_ready"), 1)

            def contexts(u, p):
                n = u * 2 + (p + 1)
                chain[p].turn(u)
                dve.wait_ge(S("q_norm_ready"), n)
                chain[p].add(v.tensor_scalar(q_gate[p][:], q_norm[p][:], 0.2, 0.1, ALU.is_gt, ALU.mult))
                chain[p].link(v.tensor_scalar(q_floor[p][:], q_norm[p][:], 1e-12, None, ALU.max))
                chain[p].link(v.reciprocal(q_rec[p][:], q_floor[p][:]))
                chain[p].link(v.tensor_tensor(heb_scale[p][:], q_gate[p][:], q_rec[p][:], ALU.mult))
                dve.wait_ge(S("win_context"), n)
                c = bank[5][:, 0:NH * (HE + 1)].rearrange("q (h e) -> q h e", h=NH)
                chain[p].add(v.tensor_scalar(infl_sum[p][:], c[:, :, HE], 1e-8, None, ALU.add))
                dve.wait_ge(S("q_kept"), u * 4 + (2 * p + 2))
                chain[p].link(v.tensor_tensor(heb_out[p][:].rearrange("q (h e) -> q h e", h=NH),
                                              heb_raw[p][:].rearrange("q (h e) -> q h e", h=NH),
                                              heb_scale[p][:].rearrange("q (h e) -> q h e", e=1).broadcast_to([P, NH, HE]),
                                              ALU.mult))
                chain[p].link(v.reciprocal(infl_rec[p][:], infl_sum[p][:]))
                chain[p].link(v.tensor_tensor(context[p][:].rearrange("q (h e) -> q h e", h=NH), c[:, :, 0:HE],
                                              infl_rec[p][:].rearrange("q (h e) -> q h e", e=1).broadcast_to([P, NH, HE]),
                                              ALU.mult))
                v.tensor_tensor(both[p][:], context[p][:], heb_out[p][:], ALU.add).then_inc(S("both_ready"), 1)
                dve.wait_ge(S("both_ready"), n)
                v.tensor_tensor(sparse[p][:], both[p][:], q_tok[p][:], ALU.mult).then_inc(S("sparse_ready"), 1)

            keep_scores(0, 0)
            weights(0, 0)
            keep_scores(0, 1)
            with dve.Fori(0, PAIRS - 1) as t:
                weights(t, 1, meanwhile=lambda: contexts(t, 0))
                keep_scores(t + 1, 0)
                weights(t + 1, 0, meanwhile=lambda: contexts(t, 1))
                keep_scores(t + 1, 1)
                dve.wait_ge(S("sparse_turned"), t + 1)
            weights(PAIRS - 1, 1, meanwhile=lambda: contexts(PAIRS - 1, 0))
            contexts(PAIRS - 1, 1)

            def four(tensor, h):
                return tensor[:, QUADS[h], :]

            for h in (0, 1):
                dve.wait_ge(S("decoded"), h + 1)
                steps.link(v.tensor_tensor(four(y4, h), bank[h][:].rearrange("p (b d) -> p b d", b=4), four(x3_all, h),
                                          ALU.add))
                layernorm4_stats(h, lambda b: y4[:, b, :])
            for h in (0, 1):
                layernorm4_apply("x4", h, lambda b: y4[:, b, :], lambda b: x4_all[:, b, :])
            for h in (0, 1):
                dve.wait_ge(S("plain_scores"), h + 1)
                v.tensor_reduce(neg_max[:, QUADS[h]], bank[4 + h][:, 0:4 * CTX].rearrange("p (b c) -> p b c", b=4),
                                AX.X, ALU.max, negate=True).then_inc(S("neg_max_ready"), 1)
            for h in (0, 1):
                dve.wait_ge(S("pr_ready"), 4 * h + 4)
                steps.add(v.reciprocal(pr_rec[:, QUADS[h]], pr_sum[:, QUADS[h]]))
            steps.wait()
            for h in (0, 1):
                dve.wait_ge(S("plain_out"), h + 1)
                for i in range(4):
                    b = 4 * h + i
                    steps.add(v.scalar_tensor_tensor(y5[:, b, :], bank[h][:, i * D:(i + 1) * D], pr_rec[:, b:b + 1],
                                                    x4_all[:, b, :], ALU.mult, ALU.add))
                steps.wait()
                layernorm4_stats(h, lambda b: y5[:, b, :])
            for h in (0, 1):
                layernorm4_apply("x5", h, lambda b: y5[:, b, :], lambda b: x5_all[:, b, :])

            def step_of(i):
                width = (FC, 1)[i]
                ws = w_step[:, 0:FC] if i == 0 else w_step[:, FC:FC + 1]
                bias = W("b1f") if i == 0 else W("b2f")
                dve.wait_ge(S(f"a_top_ready{i}"), 1)
                steps.link(v.tensor_scalar(a_floor[i][:], a_top[i][:], 1e-8, None, ALU.max))
                steps.link(v.tensor_scalar(a_step[i][:], a_floor[i][:], 1.0 / 255.0, None, ALU.mult))
                steps.add(v.reciprocal(a_rec[i][:], a_step[i][:]))
                steps.link(v.tensor_scalar(o_step[i][:], ws, a_step[i][:], None, ALU.mult))
                steps.link(v.reciprocal(b_rec[i][:], o_step[i][:]))
                steps.link(v.tensor_tensor(b_div[i][:], bias, b_rec[i][:], ALU.mult))
                steps.link(v.tensor_scalar(b_int[i][:], b_div[i][:], ROUND, ROUND, ALU.add, ALU.subtract))
                v.tensor_tensor(b_q[i][:], b_int[i][:], o_step[i][:], ALU.mult
                                ).then_inc(S(("ff_coef_ready", "ff2_coef_ready")[i]), 1)

            dve.wait_ge(S("wide_copied"), WIDE_TURNS["x5"] + 1)
            v.tensor_reduce(a_max[0][:], x5T, AX.X, ALU.max).then_inc(S("a_max_ready0"), 1)
            step_of(0)
            steps.link(v.tensor_scalar(zT, x5T, a_rec[0][:], 0.0, ALU.mult, ALU.max))
            steps.link(v.tensor_scalar(ff_out, zT, 255.0, ROUND, ALU.min, ALU.add))
            v.tensor_scalar(xq, ff_out, ROUND, None, ALU.subtract).then_inc(S("xq_ready"), 1)
            for c in range(FC):
                for h in (0, 1):
                    i = 2 * c + h
                    dve.wait_ge(S("hid_ready"), i + 1)
                    v.tensor_reduce(h_max[:, i:i + 1], hid[:, c, h * 512:(h + 1) * 512], AX.X, ALU.max
                                    ).then_inc(S("h_max_ready"), 1)
            dve.wait_ge(S("h_max_ready"), 8)
            v.tensor_reduce(a_max[1][:], h_max[:], AX.X, ALU.max).then_inc(S("a_max_ready1"), 1)
            step_of(1)
            for c in range(FC):
                steps.link(v.tensor_scalar(hid[:, c, :], hid[:, c, :], a_rec[1][:], 0.0, ALU.mult, ALU.max))
                steps.link(v.tensor_scalar(hid[:, c, :], hid[:, c, :], 255.0, ROUND, ALU.min, ALU.add))
                v.tensor_scalar(hq[:, c, :], hid[:, c, :], ROUND, None, ALU.subtract).then_inc(S("hq_ready"), 1)
            for h in (0, 1):
                cols = slice(h * 512, (h + 1) * 512)
                dve.wait_ge(S("ff_out_ready"), h + 1)
                v.tensor_tensor(zT[:, cols], ff_out[:, cols], x5T[:, cols], ALU.add).then_inc(S("zT_ready"), 1)
            def z(b):
                return bank[2 + b // 4][:, (b % 4) * D:(b % 4 + 1) * D]

            for h in (0, 1):
                dve.wait_ge(S("z_turned"), h + 1)
                layernorm4_stats(h, z)
            for h in (0, 1):
                layernorm4_apply("final", h, z, lambda b: final[:, b, :])


def kernel(**inputs):
    import numpy as np
    import concourse.bacc as bacc
    from concourse.bass_utils import run_bass_kernel_spmd

    a = {k: np.ascontiguousarray(v) for k, v in inputs.items()}
    f32 = np.float32
    head = np.arange(HEADS)
    padded = [((head // 4)[:, None] * P + 32 * (head % 4)[:, None] + c * HD + np.arange(HD)[None, :]).reshape(-1)
              for c in range(PARTS)]

    def pad_cols(w):
        out = np.zeros((w.shape[0], G * P), f32)
        for at in padded:
            out[:, at] = w
        return out

    def pad_bias(vec):
        out = np.zeros(G * P, f32)
        for at in padded:
            out[at] = vec
        return out.reshape(G, P).T

    def rows(array, n=P):
        array = np.asarray(array, f32).reshape(array.shape[0], -1) if array.ndim > 1 else array.reshape(1, -1)
        out = np.zeros((P, array.shape[1]), f32)
        out[:array.shape[0]] = array
        return out

    def packed(names, parts):
        return np.ascontiguousarray(np.concatenate([rows(parts[name]) for name, _ in names], axis=1))

    part = np.arange(P)
    r = part % 32
    rev = T - 1 - part
    parts_a = {
        "wq": pad_cols(a["L0_attn_Wq"].T), "wk": pad_cols(a["L0_attn_Wk"].T), "wv": a["L0_attn_Wv"].T,
        "k_bias": -(r == MAXROW).astype(f32)[:, None], "ident": np.eye(P, dtype=f32),
        "q_low": ((r >= 2 * HD) & (r < MAXROW)).astype(f32)[:, None],
        "k_low": ((r >= HD) & (r < 2 * HD)).astype(f32)[:, None],
        "wq2": pad_cols(a["L0_xattn_Wq"]), "wk2": pad_cols(a["L0_xattn_Wk"]), "wv2": a["L0_xattn_Wv"],
        "bq2": pad_bias(a["L0_xattn_bq"]), "bk2": pad_bias(a["L0_xattn_bk"]), "bv2": a["L0_xattn_bv"],
        "wo": a["L0_xattn_Wo"], "bo": a["L0_xattn_bo"], "router": a["L0_ffn_w_router"],
    }
    nh = np.arange(NH)
    enc_q = a["L1_attn_encoder_query"].transpose(1, 0, 2)
    enc_v = a["L1_attn_encoder_value"].transpose(1, 0, 2)

    def doubled(w):
        w = w.reshape(w.shape[0], G2, 4, 1, HE)
        return np.broadcast_to(w, (w.shape[0], G2, 4, 2, HE)).reshape(w.shape[0], G2 * P)

    mn_w1 = np.zeros((G2, 4, 2, HE, HID), f32)
    mn_w1[:, :, 0] = a["L1_attn_mn_w1"].reshape(G2, 4, HE, HID)
    heb_u = np.zeros((4, 4, G2, 4, 32), f32)
    heb_v = np.zeros((4, 4, G2, 4, HE), f32)
    for h in nh:
        heb_u[h % 4, :, h // 4, h % 4, :HE] = a["L1_attn_hebbian_U"][h].T
        heb_v[h % 4, :, h // 4, h % 4, :] = a["L1_attn_hebbian_V"][h]
    col = np.arange(SEEN)[None, :]
    mask = np.where((col >= r[:, None]) & (col < r[:, None] + WIN), 0.0, MASKED).astype(f32)
    sig_w = np.where(rev % 8 == 0, 1.0 / T + 0.5 / (T // 8), 1.0 / T).astype(f32)
    parts_b = {
        "tri": (part[:, None] > part[None, :]).astype(f32),
        "iota_e": np.broadcast_to(np.arange(E, dtype=f32), (P, E)),
        "slot_e": np.broadcast_to(np.arange(E, dtype=f32) * CAP, (P, E)),
        "ffn_bias": np.broadcast_to(a["L0_ffn_bias"].reshape(1, D), (P, D)),
        "key_w": doubled(enc_q), "qv_w": np.concatenate([enc_q.reshape(D, D), enc_v.reshape(D, D)], axis=1),
        "mn_w1": mn_w1.reshape(G2, P, HID).transpose(1, 0, 2), "mn_b1": a["L1_attn_mn_b1"][:, None],
        "mn_w2": doubled(a["L1_attn_mn_w2"].reshape(HID, NH, HE)),
        "mn_b2": doubled(a["L1_attn_mn_b2"].reshape(1, NH, HE)).reshape(G2, P).T,
        "base_metric": doubled(a["L1_attn_base_metric"].reshape(1, NH, HE)).reshape(G2, P).T,
        "is_square": (r >= HE).astype(f32)[:, None], "sig_w": np.broadcast_to(sig_w, (P, T)),
        "heb_u": heb_u.reshape(16, G2 * P), "heb_v": heb_v.reshape(16, G2 * 64), "decoder": a["L1_attn_decoder"],
        "mask": mask, "w1f": a["L1_ffn_w1"].reshape(FC, P, D).transpose(1, 0, 2),
        "b1f": a["L1_ffn_b1"].reshape(FC, P).T, "w2f": a["L1_ffn_w2"], "b2f": a["L1_ffn_b2"][:, None],
    }
    x = a["x"][:, ::-1, :]
    arrays = {
        "x_rows": x, "x_cols": x.transpose(0, 2, 1), "ctx_rows": a["ctx_1024"], "ctx_cols": a["ctx_1024"].transpose(0, 2, 1),
        "pack_a": packed(PACK_A, parts_a), "pack_b": packed(PACK_B, parts_b),
        "w1": a["L0_ffn_w1"], "w2": a["L0_ffn_w2"].reshape(E, FC, P, D).transpose(0, 2, 1, 3),
    }
    arrays = {k: np.ascontiguousarray(v) for k, v in arrays.items()}
    nc = bacc.Bacc("TRN2", target_bir_lowering=False, num_devices=1)
    args = [nc.dram_tensor(k, v.shape, mybir.dt.from_np(v.dtype), kind="ExternalInput").ap() for k, v in arrays.items()]
    out = nc.dram_tensor("out", (B, T, D), F32, kind="ExternalOutput").ap()
    xb_dram = nc.dram_tensor("xb_dram", (SLOTS, D), F32, kind="Internal").ap()
    y_dram = nc.dram_tensor("y_dram", (SLOTS, D), F32, kind="Internal").ap()
    decoder_kernel(nc, *args, out, xb_dram, y_dram)
    result = run_bass_kernel_spmd(nc, [arrays], core_ids=[0])
    return np.ascontiguousarray(result.results[0]["out"][:, ::-1, :])
```

```python
from contextlib import ExitStack

import concourse.bass as bass
from concourse import mybir

F32 = mybir.dt.float32
BF16 = mybir.dt.bfloat16
U32 = mybir.dt.uint32
ALU = mybir.AluOpType
ACT = mybir.ActivationFunctionType
AX = mybir.AxisListType

P = 128
B, T, D = 8, 128, 128
TOK = B * T
CTX = 77
PAIRS = B // 2
HEADS, HD, G, J = 16, 8, 4, 4
PARTS = 3
MAXROW = PARTS * HD
LN_EPS = 1e-5
E, FF, CAP = 8, 512, 256
FC = FF // P
SLOTS = E * CAP
NH, HE, WIN, TOPK = 8, 16, 64, 32
G2 = NH // 4
HID = WIN
QUARTER = 32
SEEN = QUARTER + WIN
TX = T + WIN
NTILE = G2 * T // QUARTER
HALF = NTILE // 2 * SEEN
MASKED = -1e30
TAKEN = -2e30
ROUND = 12582912.0

PACK_A = [("wq", G * P), ("wk", G * P), ("wv", P), ("k_bias", 1), ("q_low", 1), ("k_low", 1), ("ident", P),
          ("wq2", G * P), ("wk2", G * P),
          ("wv2", P), ("bq2", G), ("bk2", G), ("bv2", P), ("wo", P), ("bo", P), ("router", E)]
PACK_B = [("tri", P), ("iota_e", E), ("slot_e", E), ("ffn_bias", P), ("key_w", G2 * P), ("qv_w", 2 * P),
          ("mn_w1", G2 * HID), ("mn_b1", 1), ("mn_w2", G2 * P), ("mn_b2", G2), ("base_metric", G2),
          ("is_square", 1), ("heb_u", G2 * P), ("heb_v", G2 * 64), ("decoder", P),
          ("mask", SEEN), ("w1f", FF), ("b1f", FC), ("w2f", FF), ("b2f", 1)]


def columns(pack):
    at, out = 0, {}
    for name, width in pack:
        out[name] = (at, width)
        at += width
    return out, at


COLS_A, WIDTH_A = columns(PACK_A)
COLS_B, WIDTH_B = columns(PACK_B)


def decoder_kernel(nc, x_rows, x_cols, ctx_rows, ctx_cols, pack_a, pack_b, w1, w2, out, xb_dram, y_dram):
    with ExitStack() as stack:
        made = {}

        def S(name):
            if name not in made:
                made[name] = stack.enter_context(nc.semaphore(name))
            return made[name]

        def sb(name, shape, dt=F32):
            return stack.enter_context(nc.sbuf_tensor(name, shape, dt))

        bank = [stack.enter_context(nc.psum_tensor(f"bank{i}", [P, 512], F32)) for i in range(8)]

        wa = sb("wa", [P, WIDTH_A])
        wb = sb("wb", [P, WIDTH_B])

        def A(name, rows=P):
            at, width = COLS_A[name]
            return wa[0:rows, at:at + width]

        def W(name, rows=P):
            at, width = COLS_B[name]
            return wb[0:rows, at:at + width]

        ident = A("ident")
        hid = sb("hid", [P, FC, TOK])
        w_div = hid[:, 0, :].rearrange("p (i f) -> p i f", i=2)
        w_int = hid[:, 1, :].rearrange("p (i f) -> p i f", i=2)
        w_clip = hid[:, 2, :].rearrange("p (i f) -> p i f", i=2)
        sig_p = hid[:, 0:2, :].rearrange("p g (b t) -> p g b t", b=B)
        ones_row = sb("ones_row", [1, P])
        ones_bf = sb("ones_bf", [P, P], BF16)
        tri_bf = sb("tri_bf", [P, P], BF16)
        neg_half = sb("neg_half", [P, B])
        half = sb("half", [P, B])
        neg_one = sb("neg_one", [P, B])
        tiny = sb("tiny", [P, 1])
        x3T_all = sb("x3T_all", [P, TOK])
        zeros = x3T_all

        xT_in = [sb(f"xT_in{p}", [P, T]) for p in (0, 1)]
        x_in = [sb(f"x_in{p}", [P, D]) for p in (0, 1)]
        cT_in = [sb(f"cT_in{p}", [P, CTX]) for p in (0, 1)]
        qT = {a: [sb(f"{a}_qT{p}", [P, G, T], BF16) for p in (0, 1)] for a in ("self", "cross")}
        kT = {"self": [sb(f"self_kT{p}", [P, G, T], BF16) for p in (0, 1)],
              "cross": [sb(f"cross_kT{p}", [P, G, CTX], BF16) for p in (0, 1)]}
        q_high = {a: [sb(f"{a}_q_high{p}", [P, G, T], BF16) for p in (0, 1)] for a in ("self", "cross")}
        k_high = {"self": [sb(f"self_k_high{p}", [P, G, T], BF16) for p in (0, 1)],
                  "cross": [sb(f"cross_k_high{p}", [P, G, CTX], BF16) for p in (0, 1)]}
        q_full = [sb(f"q_full{p}", [P, G, T]) for p in (0, 1)]
        k_full = [sb(f"k_full{p}", [P, G, CTX]) for p in (0, 1)]
        v_high = {a: [sb(f"{a}_v_high{p}", [P, HEADS, HD + 1], BF16) for p in (0, 1)] for a in ("self", "cross")}
        v_low = {a: [sb(f"{a}_v_low{p}", [P, HEADS, HD + 1], BF16) for p in (0, 1)] for a in ("self", "cross")}
        maxes = {a: [sb(f"{a}_max{p}", [P, G, P], BF16) for p in (0, 1)] for a in ("self", "cross")}
        ident_bf = sb("ident_bf", [P, P], BF16)
        mask_bf = sb("mask_bf", [P, SEEN], BF16)
        probs_all = sb("probs_all", [P, J * G * T])
        probs = [probs_all[:, j * G * T:(j + 1) * G * T].rearrange("p (g t) -> p g t", g=G) for j in range(J)]
        parts_all = sb("parts_all", [P, 2, J, G, T], BF16)
        p_high = [parts_all[:, 0, j] for j in range(J)]
        p_low = [parts_all[:, 1, j] for j in range(J)]
        got = [sb(f"got{k}", [P, B, D]) for k in (0, 1)]
        rec = {a: [sb(f"{a}_rec{p}", [P, HEADS]) for p in (0, 1)] for a in ("self", "cross")}
        attn = {"self": [sb(f"attn{p}", [P, D]) for p in (0, 1)], "cross": [got[0][:, p, :] for p in (0, 1)]}
        y_sum = {"self": [sb(f"y_sum{p}", [P, D]) for p in (0, 1)], "cross": [got[0][:, 2 + p, :] for p in (0, 1)]}
        stats = {a: [sb(f"{a}_stats{p}", [P, 6]) for p in (0, 1)] for a in ("self", "cross")}
        mv = {a: [sb(f"{a}_mv{p}", [P, 2]) for p in (0, 1)] for a in ("self", "cross")}
        var_eps = {a: [sb(f"{a}_var_eps{p}", [P, 1]) for p in (0, 1)] for a in ("self", "cross")}
        rstd = {a: [sb(f"{a}_rstd{p}", [P, 1]) for p in (0, 1)] for a in ("self", "cross")}
        x1 = [sb(f"x1_{p}", [P, D]) for p in (0, 1)]
        x1T = [sb(f"x1T{p}", [P, T]) for p in (0, 1)]
        a2T = [sb(f"a2T{p}", [P, T]) for p in (0, 1)]
        x2 = [sb(f"x2_{p}", [P, D]) for p in (0, 1)]
        x2T_all = hid[:, 3, :]
        x2_all = sb("x2_all", [P, B, D])
        logits = sb("logits", [P, B, E])

        top8 = sb("top8", [P, B, 8])
        index8 = sb("index8", [P, B, 8], U32)
        index_f = sb("index_f", [P, B, 2])
        shifted = sb("shifted", [P, B, E])
        exps = sb("exps", [P, B, E])
        gap = sb("gap", [P, B])
        exp_gap = sb("exp_gap", [P, B])
        denom = sb("denom", [P, B])
        gate = sb("gate", [P, 2, B])
        onehot = [sb(f"onehot{k}", [P, B, E]) for k in (0, 1)]
        chosen = sb("chosen", [P, B, E], BF16)
        place = sb("place", [P, B, E])
        slot_of = sb("slot_of", [P, B, E])
        picked = [sb(f"picked{i}", [P, B, E]) for i in range(4)]
        place_k = sb("place_k", [P, 2, B])
        slot_k = sb("slot_k", [P, 2, B])
        fits = sb("fits", [P, 2, B])
        over = sb("over", [P, 2, B])
        put_f = sb("put_f", [P, 2, B])
        get_f = sb("get_f", [P, 2, B])
        put = sb("put", [P, 2, B], U32)
        get = sb("get", [P, 2, B], U32)
        gates = sb("gates", [P, 2, B])
        xb_in = [sb(f"xb_in{p}", [P, 2, D]) for p in (0, 1)]
        w1_in = [sb(f"w1_in{p}", [P, FF]) for p in (0, 1)]
        w2_in = [sb(f"w2_in{p}", [P, FC, D]) for p in (0, 1)]
        xbT = [sb(f"xbT{p}", [P, CAP]) for p in (0, 1)]
        hT = [sb(f"hT{p}", [P, FC, CAP]) for p in (0, 1)]
        yb = [sb(f"yb{p}", [P, 2, D]) for p in (0, 1)]
        x2b = sb("x2b", [P, B, D])

        x3_all = sb("x3_all", [P, B, D])
        uT = sb("uT", [P, G2, B, T])
        sum_all = sb("sum_all", [P, G2, B])
        sum_eighth = sb("sum_eighth", [P, G2, B])
        sum_both = sb("sum_both", [P, G2, B])
        sig = sb("sig", [P, G2, B])
        hidden = sb("hidden", [HID, B])
        pre = sb("pre", [P, G2])
        zm = sb("zm", [P, G2, B])
        zabs = sb("zabs", [P, G2, B])
        zexp = sb("zexp", [P, G2, B])
        zln = sb("zln", [P, G2, B])
        zpos = sb("zpos", [P, G2, B])
        metric = sb("metric", [P, G2, B])
        q_scale = sb("q_scale", [P, G2, B])
        q_bias = sb("q_bias", [P, G2, B])
        two_key = sb("two_key", [P, 1])
        not_square = sb("not_square", [P, 1])
        neg_square = sb("neg_square", [P, 1])
        heb = sb("heb", [P, G2, 64])
        k_all = sb("k_all", [P, G2, B, T])
        qs = [sb(f"qs{p}", [P, G2, T]) for p in (0, 1)]
        ks = [sb(f"ks{p}", [P, G2, TX]) for p in (0, 1)]
        x3T = [sb(f"x3T{p}", [P, TX]) for p in (0, 1)]
        q_tok = [sb(f"q_tok{p}", [P, D]) for p in (0, 1)]
        vw = [sb(f"vw{p}", [SEEN, 4, NH, HE + 1]) for p in (0, 1)]
        score = [probs_all[:, p * NTILE * SEEN:(p + 1) * NTILE * SEEN].rearrange("p (n w) -> p n w", w=SEEN) for p in (0, 1)]
        work = [hT[p][:].rearrange("p c s -> p (c s)")[:, 0:NTILE * SEEN].rearrange("p (n w) -> p n w", w=SEEN)
                for p in (0, 1)]
        best = [sb(f"best{p}", [P, TOPK // 8, NTILE, 8]) for p in (0, 1)]
        parts_f32 = parts_all[:].rearrange("p a j g t -> p (a j g t)").bitcast(F32)
        infl = [parts_f32[:, p * NTILE * SEEN:(p + 1) * NTILE * SEEN].rearrange("p (n w) -> p n w", w=SEEN) for p in (0, 1)]
        kept = [sb(f"kept{p}", [P, NTILE, SEEN]) for p in (0, 1)]
        keptT = hid[0:SEEN, 3, :].rearrange("p (n t) -> p n t", n=NTILE)
        heb_raw = [sb(f"heb_raw{p}", [P, D]) for p in (0, 1)]
        sparseT_all = hid[:, 2, :]
        qq = [sb(f"qq{p}", [P, D]) for p in (0, 1)]
        q_n2 = [sb(f"q_n2_{p}", [P, NH]) for p in (0, 1)]
        q_norm = [sb(f"q_norm{p}", [P, NH]) for p in (0, 1)]
        q_gate = [sb(f"q_gate{p}", [P, NH]) for p in (0, 1)]
        q_floor = [sb(f"q_floor{p}", [P, NH]) for p in (0, 1)]
        q_rec = [sb(f"q_rec{p}", [P, NH]) for p in (0, 1)]
        heb_scale = [sb(f"heb_scale{p}", [P, NH]) for p in (0, 1)]
        infl_sum = [sb(f"infl_sum{p}", [P, NH]) for p in (0, 1)]
        infl_rec = [sb(f"infl_rec{p}", [P, NH]) for p in (0, 1)]
        heb_out = [sb(f"heb_out{p}", [P, D]) for p in (0, 1)]
        context = [sb(f"context{p}", [P, D]) for p in (0, 1)]
        both = [sb(f"both{p}", [P, D]) for p in (0, 1)]
        sparse = [sb(f"sparse{p}", [P, D]) for p in (0, 1)]

        cT_all = sb("cT_all", [P, B, CTX])
        c_all = sb("c_all", [CTX, B, D])
        y4, x4_all = got[0], got[1]
        x4T_all = x2_all[:].rearrange("p b d -> p (b d)")
        neg_max = sb("neg_max", [P, B])
        pr_all = probs_all[:, 0:B * CTX].rearrange("p (b c) -> p b c", b=B)
        pr_sum = sb("pr_sum", [P, B])
        pr_rec = sb("pr_rec", [P, B])
        prT_all = hid[0:CTX, 3, :]
        y5 = got[0]
        x5_all = parts_f32[:, 0:TOK].rearrange("p (b d) -> p b d", b=B)
        x5T = x2b[:].rearrange("p b d -> p (b d)")
        stats4 = [sb(f"stats4_{h}", [P, 4, 6]) for h in (0, 1)]
        mv4 = [sb(f"mv4_{h}", [P, 4, 2]) for h in (0, 1)]
        var4 = [sb(f"var4_{h}", [P, 4]) for h in (0, 1)]
        rstd4 = [sb(f"rstd4_{h}", [P, 4]) for h in (0, 1)]

        w_abs = sb("w_abs", [P, FC + 1])
        w_floor = sb("w_floor", [P, FC + 1])
        w_step = sb("w_step", [P, FC + 1])
        w1q = sb("w1q", [P, FF], BF16)
        w2q = sb("w2q", [P, FC, P], BF16)
        w_rec = sb("w_rec", [P, FC + 1])
        a_max = [sb(f"a_max{i}", [P, 1]) for i in (0, 1)]
        a_top = [sb(f"a_top{i}", [P, 1]) for i in (0, 1)]
        a_floor = [sb(f"a_floor{i}", [P, 1]) for i in (0, 1)]
        a_step = [sb(f"a_step{i}", [P, 1]) for i in (0, 1)]
        a_rec = [sb(f"a_rec{i}", [P, 1]) for i in (0, 1)]
        b_rec = [sb(f"b_rec{i}", [P, (FC, 1)[i]]) for i in (0, 1)]
        o_step = [sb(f"o_step{i}", [P, (FC, 1)[i]]) for i in (0, 1)]
        b_div = [sb(f"b_div{i}", [P, (FC, 1)[i]]) for i in (0, 1)]
        b_int = [sb(f"b_int{i}", [P, (FC, 1)[i]]) for i in (0, 1)]
        b_q = [sb(f"b_q{i}", [P, (FC, 1)[i]]) for i in (0, 1)]
        xq = x3_all[:].rearrange("p b d -> p (b d)").bitcast(BF16)[:, 0:TOK]
        h_max = sb("h_max", [P, 8])
        hq = uT[:].rearrange("p g b t -> p (g b t)").bitcast(BF16).rearrange("p (c t) -> p c t", c=FC)
        ff_out = got[0][:].rearrange("p b d -> p (b d)")
        zT = got[1][:].rearrange("p b d -> p (b d)")
        final = x2_all

        block = stack.enter_context(nc.Block())

        SCALE = {"self": 1.0 / float(D) ** 0.5, "cross": 1.0 / float(HD) ** 0.5}
        KEYS = {"self": T, "cross": CTX}
        KINDS = ("self", "cross")
        OWN = {"self": (4, 5), "cross": (6, 7)}
        SELF_KEYS = (6, 7)

        def wait_apart(engine, name, value):
            engine.wait_ge(S(name), value)
            engine.sem_inc(S("wait_passed"), 1)

        TURNS = {"x1": (0, 4, 0), "attn2": (0, 4, 1)}

        LN4 = {"x3": 1, "x4": 3, "x5": 5, "final": 7}
        WIDE_TURNS = {"x2": 1, "x3": 3, "x4": 5, "pr": 7, "x5": 9}
        GATHERS = [range(0, B // 2), range(B // 2, B - 2), range(B - 2, B)]

        def gathered_with(b):
            return [b in group for group in GATHERS].index(True)

        QUADS = [slice(0, B // 2), slice(B // 2, B)]
        COLS4 = [slice(0, TOK // 2), slice(TOK // 2, TOK)]

        def turned(name, t, p):
            before, per, which = TURNS[name]
            return t * per + (before + 2 * which + p + 1)

        HIGH = {"self": {"q": (2, 1), "k": (0, 1), "v": (4, 1)}, "cross": {"q": (0, 1), "k": (2, 1), "v": (4, 1)}}

        def high(a, what, u, p):
            first, stride = HIGH[a][what]
            return u * 6 + (first + stride * p + 1)

        class Share:

            def __init__(self, a, u, scored, attended, beside=0):
                self.a, self.u, self.s0, self.a0, self.beside = a, u, scored, attended, beside

            def n(self, p):
                return self.u * 2 + (p + 1)

            def scored(self, p):
                return self.s0 + p

            def attended(self, p):
                return self.a0 + p

            def lowered(self, p):
                return self.a0 + (p + self.beside)

        def rounds(engine, round_of):
            round_of(Share("self", 0, 1, 1), None)
            with engine.Fori(0, PAIRS - 1) as t:
                round_of(Share("self", t + 1, t * 4 + 3, t * 4 + 5),
                         Share("cross", t, t * 4 + 5, t * 4 + 3, beside=1))
            round_of(None, Share("cross", PAIRS - 1, 4 * PAIRS - 1, 4 * PAIRS - 1))

        @block.sync
        def _(sp):
            sp.dma_start(xT_in[0][:], x_cols[0]).then_inc(S("xT_loaded0"), 16)
            sp.dma_start(xT_in[1][:], x_cols[1]).then_inc(S("xT_loaded1"), 16)
            sp.dma_start(wa[:, 0:COLS_A["wq2"][0]], pack_a[:, 0:COLS_A["wq2"][0]]).then_inc(S("wa_loaded"), 16)
            for p in (0, 1):
                sp.dma_start(x_in[p][:], x_rows[p]).then_inc(S(f"x_loaded{p}"), 16)
                sp.dma_start(cT_in[p][:], ctx_cols[p]).then_inc(S(f"cT_loaded{p}"), 16)
            sp.dma_start(wa[:, COLS_A["wq2"][0]:WIDTH_A], pack_a[:, COLS_A["wq2"][0]:WIDTH_A]).then_inc(S("wa2_loaded"), 16)
            sp.dma_start(wb[:], pack_b).then_inc(S("wb_loaded"), 16)
            sp.dma_start(cT_all[:], ctx_cols.rearrange("b d c -> d b c")).then_inc(S("ctx_loaded"), 16)
            sp.dma_start(c_all[:], ctx_rows.rearrange("b c d -> c b d")).then_inc(S("ctx_loaded"), 16)
            sp.wait_ge(S("zeros_ready"), 1)
            for h in (0, 1):
                sp.dma_start(xb_dram[h * SLOTS // 2:(h + 1) * SLOTS // 2, :].rearrange("(p r) d -> p (r d)", p=P),
                             zeros[:]).then_inc(S("xb_zeroed"), 16)
            for p in (0, 1):
                sp.dma_start(w1_in[p][:], w1[p]).then_inc(S(f"w1_loaded{p}"), 16)
                sp.dma_start(w2_in[p][:], w2[p]).then_inc(S(f"w2_loaded{p}"), 16)
            with sp.Fori(0, PAIRS - 1) as t:
                for p in (0, 1):
                    sp.wait_ge(S("self_v_done"), t * 2 + p + 1)
                    sp.dma_start(xT_in[p][:], x_cols[bass.ds(t * 2 + (2 + p), 1)].rearrange("b d t -> (b d) t")
                                 ).then_inc(S(f"xT_loaded{p}"), 16)
                for p in (0, 1):
                    sp.wait_ge(S("self_sum_done"), t * 2 + p + 1)
                    sp.dma_start(x_in[p][:], x_rows[bass.ds(t * 2 + (2 + p), 1)].rearrange("b t d -> (b t) d")
                                 ).then_inc(S(f"x_loaded{p}"), 16)
                for p in (0, 1):
                    sp.wait_ge(S("cross_v_done"), t * 2 + p + 1)
                    sp.dma_start(cT_in[p][:], ctx_cols[bass.ds(t * 2 + (2 + p), 1)].rearrange("b d c -> (b d) c")
                                 ).then_inc(S(f"cT_loaded{p}"), 16)
            sp.wait_ge(S("scattered"), 16 * 2 * B)
            def load_rows(t, p):
                sp.dma_start(xb_in[p][:], xb_dram[bass.ds((t * 2 + p) * CAP, CAP), :].rearrange("(h s) d -> s h d", h=2)
                             ).then_inc(S(f"xb_loaded{p}"), 16)

            def store_results(t, p):
                sp.wait_ge(S("yb_ready"), t * 2 + (p + 1))
                sp.dma_start(y_dram[bass.ds((t * 2 + p) * CAP, CAP), :].rearrange("(h s) d -> s h d", h=2), yb[p][:]
                             ).then_inc(S(f"y_stored{p}"), 16)

            for p in (0, 1):
                load_rows(0, p)
            for p in (0, 1):
                sp.wait_ge(S("xb_turned"), p + 1)
                load_rows(1, p)
            with sp.Fori(0, PAIRS - 2) as t:
                for p in (0, 1):
                    sp.wait_ge(S("xb_turned"), t * 2 + (p + 3))
                    load_rows(t + 2, p)
                for p in (0, 1):
                    store_results(t, p)
            for t in (PAIRS - 2, PAIRS - 1):
                for p in (0, 1):
                    store_results(t, p)
            for h in (0, 1):
                sp.wait_ge(S("final_ready"), 4 * h + 4)
                sp.dma_start(out[4 * h:4 * h + 4].rearrange("b t d -> t b d"), final[:, 4 * h:4 * h + 4, :]
                             ).then_inc(S("out_stored"), 16)
            sp.wait_ge(S("out_stored"), 32)

        @block.gpsimd
        def _(pool):
            g = nc.gpsimd
            g.memset(neg_half[:], -0.5).then_inc(S("pool_consts"), 1)
            g.memset(half[:], 0.5).then_inc(S("pool_consts"), 1)
            g.memset(neg_one[:], -1.0).then_inc(S("pool_consts"), 1)
            g.memset(ones_row[:], 1.0).then_inc(S("pool_consts"), 1)
            g.memset(ones_bf[:], 1.0).then_inc(S("pool_consts"), 1)
            g.memset(tiny[:], 1e-8).then_inc(S("pool_consts"), 1)
            for a in KINDS:
                for p in (0, 1):
                    g.memset(maxes[a][p][:], 0.0).then_inc(S("pool_consts"), 1)
                    g.memset(v_high[a][p][:, :, HD:HD + 1], 1.0).then_inc(S("pool_consts"), 1)
                    g.memset(v_low[a][p][:, :, HD:HD + 1], 0.0).then_inc(S("pool_consts"), 1)
            for p in (0, 1):
                g.memset(vw[p][:, :, :, HE:HE + 1], 1.0).then_inc(S("pool_consts"), 1)
            g.memset(zeros[:], 0.0).then_inc(S("zeros_ready"), 1)

            def power(share, p):
                pool.wait_ge(S("ln_var"), share.attended(p))
                g.tensor_tensor(rstd[share.a][p][:], var_eps[share.a][p][:], neg_half[:, 0:1], ALU.pow
                                ).then_inc(S("ln_rstd"), 1)

            def low_probs(share, p):
                K = KEYS[share.a]
                for j in (0, 1):
                    pool.wait_ge(S("p_high_ready"), (share.attended(p) - 1) * 2 + (j + 1))
                    g.tensor_tensor(p_low[j][0:K], probs[j][0:K], p_high[j][0:K], ALU.subtract
                                    ).then_inc(S("probs01_ready"), 1)

            def attention_round(s, c):
                if c:
                    for what, parts, full, taken in (("q", qT, q_full, q_high), ("k", kT, k_full, k_high)):
                        for p in (0, 1):
                            wait_apart(pool, "cross_high", high("cross", what, c.u, p))
                            g.tensor_tensor(parts["cross"][p][:], full[p][:], taken["cross"][p][:], ALU.subtract
                                            ).then_inc(S(f"cross_{what}_ready"), 1)
                for share in (c, s):
                    if share:
                        low_probs(share, 0)
                        low_probs(share, 1)
                for share in (c, s):
                    if share:
                        power(share, 0)
                        power(share, 1)
                if c:
                    for p in (0, 1):
                        pool.wait_ge(S("x2_ready"), c.n(p))
                        g.tensor_copy(x2_all[:, bass.ds(c.u * 2 + p, 1), :], x2[p][:].rearrange("q (b d) -> q b d", b=1)
                                      ).then_inc(S("x2_kept"), 1)

            rounds(pool, attention_round)

            pool.wait_ge(S("xb_zeroed"), 32)
            pool.wait_ge(S("put_ready"), 1)
            pool.wait_ge(S("x2_kept"), B)
            for b in range(B):
                for k in (0, 1):
                    g.indirect_dma_start(out=xb_dram, out_offset=bass.IndirectOffsetOnAxis(ap=put[:, k, b:b + 1], axis=0),
                                         in_=x2_all[:, b, :], in_offset=None, bounds_check=SLOTS - 1,
                                         oob_is_err=False).then_inc(S("scattered"), 16)
            pool.wait_ge(S("wb_loaded"), 16)
            g.tensor_tensor(x2b[:], x2_all[:], W("ffn_bias").rearrange("p (b d) -> p b d", b=1).broadcast_to([P, B, D]),
                            ALU.add).then_inc(S("x2b_ready"), 1)
            def power4(name, halves=(0, 1)):
                for h in halves:
                    pool.wait_ge(S("ln4_var"), LN4[name] + h)
                    g.tensor_tensor(rstd4[h][:], var4[h][:], neg_half[:, 0:4], ALU.pow).then_inc(S("ln4_rstd"), 1)

            for p in (0, 1):
                pool.wait_ge(S(f"y_stored{p}"), 16 * PAIRS)
            pool.wait_ge(S("put_ready"), 1)
            for b in range(B):
                for k in (0, 1):
                    g.indirect_dma_start(out=got[k][:, b, :], out_offset=None, in_=y_dram,
                                         in_offset=bass.IndirectOffsetOnAxis(ap=get[:, k, b:b + 1], axis=0),
                                         bounds_check=SLOTS - 1, oob_is_err=False
                                         ).then_inc(S(f"gathered{gathered_with(b)}"), 16)
                if b == B - 2:
                    power4("x3", halves=(0,))

            def fetch_rows(u, p):
                b = u * 2 + p
                g.tensor_copy(x3T[p][:, 0:T], x3T_all[:, bass.ds(b * T, T)]).then_inc(S("x3T_here"), 1)
                g.tensor_copy(x3T[p][:, T:TX], x3T_all[:, bass.ds(b * T + (T - 1), 1)].broadcast_to([P, WIN])
                              ).then_inc(S("x3T_here"), 1)

            def fetch_keys(u, p):
                b = u * 2 + p
                g.tensor_copy(ks[p][:, :, 0:T], k_all[:, :, bass.ds(b, 1), :].rearrange("q g b t -> q g (b t)")
                              ).then_inc(S("ks_here"), 1)
                g.tensor_copy(ks[p][:, :, T:TX], k_all[:, :, bass.ds(b, 1), T - 1:T]
                              .rearrange("q g b t -> q g (b t)").broadcast_to([P, G2, WIN])
                              ).then_inc(S("ks_here"), 1)

            power4("x3", halves=(1,))
            pool.wait_ge(S("wide_copied"), WIDE_TURNS["x3"])
            fetch_rows(0, 0)
            fetch_rows(0, 1)

            def key_half(h):
                rows, quad = sig_p[:, 1, QUADS[h]], QUADS[h]
                pool.wait_ge(S("uT_ready"), h * G2 + 2)
                g.tensor_scalar(rows, uT[:, 1, quad], W("is_square"), not_square[:], ALU.mult, ALU.add
                                ).then_inc(S("square_rows"), 1)
                pool.wait_ge(S("square_rows"), 2 * h + 1)
                g.tensor_tensor(k_all[:, 1, quad], uT[:, 1, quad], rows, ALU.mult).then_inc(S("square_rows"), 1)

            key_half(0)
            pool.wait_ge(S("square_rows"), 2)
            pool.wait_ge(S("k_half"), 1)
            fetch_keys(0, 0)
            fetch_keys(0, 1)
            key_half(1)
            pool.wait_ge(S("square_rows"), 4)
            pool.wait_ge(S("k_half"), 2)

            def square_queries(u, p):
                pool.wait_ge(S("q_kept"), u * 4 + (2 * p + 1))
                g.tensor_tensor(qq[p][:], q_tok[p][:], q_tok[p][:], ALU.mult).then_inc(S("qq_ready"), 1)

            def distances(u, p):
                pool.wait_ge(S("sorted"), u * 128 + (p * 64 + NTILE))
                g.tensor_tensor(infl[p], best[p][:, 0, :, 0:1].broadcast_to([P, NTILE, SEEN]), score[p],
                                ALU.subtract).then_inc(S("dist2_ready"), 1)

            def hebbian(u, p):
                n = u * 2 + (p + 1)

                def link(instruction, i):
                    instruction.then_inc(S("hebbian_step"), 1)
                    wait_apart(pool, "hebbian_step", u * 10 + (5 * p + i))

                pool.wait_ge(S("q_n2_ready"), n)
                link(g.tensor_tensor(q_norm[p][:], q_n2[p][:], half[:, 0:NH], ALU.pow), 1)
                link(g.tensor_scalar(q_gate[p][:], q_norm[p][:], 0.2, 0.1, ALU.is_gt, ALU.mult), 2)
                link(g.tensor_scalar(q_floor[p][:], q_norm[p][:], 1e-12, None, ALU.max), 3)
                link(g.tensor_tensor(q_rec[p][:], q_floor[p][:], neg_one[:, 0:NH], ALU.pow), 4)
                link(g.tensor_tensor(heb_scale[p][:], q_gate[p][:], q_rec[p][:], ALU.mult), 5)
                pool.wait_ge(S("q_kept"), u * 4 + (2 * p + 2))
                g.tensor_tensor(heb_out[p][:].rearrange("q (h e) -> q h e", h=NH),
                                heb_raw[p][:].rearrange("q (h e) -> q h e", h=NH),
                                heb_scale[p][:].rearrange("q (h e) -> q h e", e=1).broadcast_to([P, NH, HE]),
                                ALU.mult).then_inc(S("heb_out_ready"), 1)

            def result(u, p):
                n = u * 2 + (p + 1)
                pool.wait_ge(S("context_ready"), n)
                pool.wait_ge(S("heb_out_ready"), n)
                g.tensor_tensor(both[p][:], context[p][:], heb_out[p][:], ALU.add).then_inc(S("both_ready"), 1)
                pool.wait_ge(S("both_ready"), n)
                g.tensor_tensor(sparse[p][:], both[p][:], q_tok[p][:], ALU.mult).then_inc(S("sparse_ready"), 1)

            square_queries(0, 0)
            distances(0, 0)
            hebbian(0, 0)
            with pool.Fori(0, PAIRS - 1) as t:
                pool.wait_ge(S("win_scores"), t * 4 + 2)
                fetch_rows(t + 1, 0)
                fetch_keys(t + 1, 0)
                square_queries(t, 1)
                distances(t, 1)
                hebbian(t, 1)
                result(t, 0)
                pool.wait_ge(S("win_scores"), t * 4 + 4)
                fetch_rows(t + 1, 1)
                fetch_keys(t + 1, 1)
                square_queries(t + 1, 0)
                distances(t + 1, 0)
                hebbian(t + 1, 0)
                result(t, 1)
                pool.wait_ge(S("sparse_turned"), t + 1)
            square_queries(PAIRS - 1, 1)
            distances(PAIRS - 1, 1)
            hebbian(PAIRS - 1, 1)
            result(PAIRS - 1, 0)
            power4("x4", halves=(0,))
            result(PAIRS - 1, 1)
            power4("x4", halves=(1,))
            power4("x5")

            for i in (0, 1):
                pool.wait_ge(S(f"a_max_ready{i}"), 1)
                g.partition_all_reduce(a_top[i][:], a_max[i][:], P, bass.bass_isa.ReduceOp.max
                                       ).then_inc(S(f"a_top_ready{i}"), 1)
            power4("final")

        @block.tensor
        def _(pe):
            mm = pe.matmul

            def project(share, what, p):
                a = share.a
                w = A({"self": {"q": "wq", "k": "wk"}, "cross": {"q": "wq2", "k": "wk2"}}[a][what])
                src = xT_in[p] if a == "self" else (x1T if what == "q" else cT_in)[p]
                width = src.shape[1]
                if a == "self" and what == "k":
                    pe.wait_ge(S(f"xT_loaded{p}"), (share.u + 1) * 16)
                if a == "cross" and what == "q":
                    pe.wait_ge(S("turned_copied"), turned("x1", share.u, p))
                dst_bank = OWN[a][p]
                if a == "self" and what == "k":
                    dst_bank = SELF_KEYS[p]
                if a == "cross" and what == "k":
                    pe.wait_ge(S("cross_q_full"), share.n(p))
                if a == "cross" and what == "k":
                    pe.wait_ge(S(f"cT_loaded{p}"), (share.u + 1) * 16)
                for gi in range(G):
                    last = mm(bank[dst_bank][:, gi * width:(gi + 1) * width], w[:, gi * P:(gi + 1) * P], src[:],
                              start=True, stop=True)
                last.then_inc(S(f"{a}_{what}_proj"), 1)

            def project_values(share, p):
                a = share.a
                dst = bank[OWN[a][p]][0:KEYS[a], 0:D]
                pe.wait_ge(S("self_q_ready" if a == "self" else "cross_k_full"), share.n(p))
                if a == "self":
                    mm(dst, xT_in[p][:], A("wv"), start=True, stop=True).then_inc(S("self_v_proj"), 1)
                else:
                    mm(dst, cT_in[p][:], A("wv2"), start=True, stop=False)
                    mm(dst, ones_row[0:1, 0:CTX], A("bv2", 1), start=False, stop=True).then_inc(S("cross_v_proj"), 1)

            def max_scores(share, p, first):
                a = share.a
                pe.wait_ge(S(f"{a}_q_ready"), share.n(p))
                pe.wait_ge(S(f"{a}_k_ready"), share.n(p))
                if not first:
                    pe.wait_ge(S("max_ready"), (share.scored(p) - 1) * 4)
                width = KEYS[a]
                for j0 in (0, 2):
                    for gi in range(G):
                        for j in (j0, j0 + 1):
                            rows = slice(32 * j, 32 * j + 32)
                            last = mm(bank[j][:, gi * width:(gi + 1) * width], qT[a][p][rows, gi, :],
                                      kT[a][p][rows, gi, :], start=True, stop=True)
                            if gi == G - 1:
                                last.then_inc(S("scores"), 1)

            def turn_maxes(share, p):
                a = share.a
                pe.wait_ge(S("max_ready"), share.scored(p) * 4)
                pe.wait_ge(S(f"{a}_v_done"), share.n(p))
                for gi in range(G):
                    last = mm(bank[OWN[a][p]][:, gi * T:(gi + 1) * T], maxes[a][p][:, gi, :], ident_bf[:],
                              start=True, stop=True)
                last.then_inc(S("max_turned"), 1)

            def exp_scores(share, p, j0, first=False):
                K = KEYS[share.a]
                if not first:
                    pe.wait_ge(S("exp_ready"), (share.attended(p) - 2) * 4 + (j0 + 2))
                if j0 == 0:
                    pe.wait_ge(S("qm_ready"), share.lowered(p))
                for gi in range(G):
                    for j in (j0, j0 + 1):
                        rows = slice(32 * j, 32 * j + 32)
                        last = mm(bank[j][0:K, gi * T:(gi + 1) * T], kT[share.a][p][rows, gi, :],
                                  qT[share.a][p][rows, gi, :], start=True, stop=True)
                        if gi == G - 1:
                            last.then_inc(S("scoresT"), 1)

            def weigh(share, p, j0):
                a, K = share.a, KEYS[share.a]
                for j in (j0, j0 + 1):
                    pe.wait_ge(S("probs01_ready" if j0 == 0 else "probs23_ready"),
                               (share.attended(p) - 1) * 2 + (j - j0 + 1))
                    for gi in range(G):
                        h = 4 * gi + j
                        out_h = bank[OWN[a][p]][:, h * (HD + 1):(h + 1) * (HD + 1)]
                        mm(out_h, p_high[j][0:K, gi, :], v_high[a][p][0:K, h, :], start=True, stop=False)
                        mm(out_h, p_high[j][0:K, gi, :], v_low[a][p][0:K, h, :], start=False, stop=False)
                        last = mm(out_h, p_low[j][0:K, gi, :], v_high[a][p][0:K, h, :], start=False, stop=True)
                    last.then_inc(S("weighed"), 1)

            def turn(name, n, src, bank_no, rows=P):
                pe.wait_ge(S(f"{name}_ready"), n)
                pe.transpose(bank[bank_no][0:rows, 0:P], src, ident).then_inc(S("turned"), 1)

            def output_projection(c, p):
                own = bank[OWN["cross"][p]][:, 0:D]
                pe.wait_ge(S("turned_copied"), turned("attn2", c.u, p))
                mm(own, a2T[p][:], A("wo"), start=True, stop=False)
                mm(own, ones_row[:], A("bo", 1), start=False, stop=True).then_inc(S("wo_done"), 1)

            def attention_round(s, c):
                both = s and c
                if s:
                    for p in (0, 1):
                        project(s, "k", p)
                    for p in (0, 1):
                        if c:
                            pe.wait_ge(S("self_sum_done"), s.n(p) - 2)
                        project(s, "q", p)
                if s:
                    max_scores(s, 0, first=True)
                if c:
                    for p in (0, 1):
                        if s:
                            pe.wait_ge(S("self_k_ready"), s.n(p))
                        turn("x1", c.n(p), x1[p][:], OWN["cross"][p])
                    project(c, "q", 0)
                    project(c, "q", 1)
                if s:
                    project_values(s, 0)
                    project_values(s, 1)
                    max_scores(s, 1, first=False)
                if c:
                    project(c, "k", 0)
                    project(c, "k", 1)
                    project_values(c, 0)
                    project_values(c, 1)
                for p in (0, 1):
                    if s:
                        turn_maxes(s, p)
                    if c:
                        max_scores(c, p, first=(p == 0 and not s))
                if c:
                    turn_maxes(c, 0)
                    turn_maxes(c, 1)
                units = [(share, p) for share in (c, s) if share for p in (0, 1)]
                last_scored = c if c else s
                pe.wait_ge(S("max_ready"), last_scored.scored(1) * 4)
                exp_scores(*units[0], 0, first=True)
                exp_scores(*units[0], 2, first=True)
                for i, unit in enumerate(units):
                    if i + 1 < len(units):
                        exp_scores(*units[i + 1], 0)
                        exp_scores(*units[i + 1], 2)
                    if both and i == 2:
                        turn("attn2", c.n(1), attn["cross"][1], OWN["cross"][1])
                    weigh(*unit, 0)
                    weigh(*unit, 2)
                    if both and i == 1:
                        turn("attn2", c.n(0), attn["cross"][0], OWN["cross"][0])
                    if both and i == 2:
                        output_projection(c, 0)
                        output_projection(c, 1)
                if both:
                    pe.wait_ge(S("cross_sum_done"), c.n(1))
                if c and not s:
                    for p in (0, 1):
                        turn("attn2", c.n(p), attn["cross"][p], OWN["cross"][p])
                    for p in (0, 1):
                        output_projection(c, p)

            pe.wait_ge(S("wa_loaded"), 16)
            pe.wait_ge(S("pool_consts"), 20)
            pe.wait_ge(S("ident_bf_ready"), 1)
            pe.wait_ge(S("wa2_loaded"), 16)
            rounds(pe, attention_round)

            def turn4(name, src_of, banks, rows=P, halves=(0, 1)):
                for h in halves:
                    for i in range(4):
                        if i % 4 == 0:
                            pe.wait_ge(S(f"{name}_ready" if name != "x2" else "x2_kept"), 4 * h + 4)
                        last = pe.transpose(bank[banks[h]][0:rows, i * P:(i + 1) * P], src_of(4 * h + i), ident)
                    last.then_inc(S("wide_turned"), 1)

            for h in (0, 1):
                turn4("x2", lambda b: x2_all[:, b, :], (0, 1), halves=(h,))
                pe.wait_ge(S("wide_copied"), WIDE_TURNS["x2"] + h)
                for b in range(4 * h, 4 * h + 4):
                    last = mm(bank[2][:, b * E:(b + 1) * E], x2T_all[:, b * T:(b + 1) * T], A("router"),
                              start=True, stop=True)
            last.then_inc(S("routed"), 1)

            pe.wait_ge(S("chosen_ready"), 1)
            pe.wait_ge(S("tri_ready"), 1)
            mm(bank[0][:, 0:B * E], tri_bf[:], chosen[:].rearrange("p b e -> p (b e)"), start=True, stop=False)
            for b in range(B - 1):
                later = B - 1 - b
                last = mm(bank[0][:, (b + 1) * E:B * E], ones_bf[:], chosen[:, b:b + 1, :].broadcast_to([P, later, E]),
                          start=False, stop=(b == B - 2))
            last.then_inc(S("places"), 1)

            pe.wait_ge(S("place_ready"), 1)
            def turn_rows(t):
                for p in (0, 1):
                    pe.wait_ge(S(f"xb_loaded{p}"), t * 16 + 16)
                    for h in (0, 1):
                        last = pe.transpose(bank[p][:, h * P:(h + 1) * P], xb_in[p][:, h, :], ident)
                    last.then_inc(S("xb_turned"), 1)

            def expert_hidden(t):
                for p in (0, 1):
                    pe.wait_ge(S("xbT_ready"), t * 2 + (p + 1))
                    pe.wait_ge(S(f"w1_loaded{p}"), t * 16 + 16)
                    for c in range(FC):
                        last = mm(bank[2 + 2 * p + c // 2][:, (c % 2) * CAP:(c % 2 + 1) * CAP],
                                  w1_in[p][:, c * P:(c + 1) * P], xbT[p][:], start=True, stop=True)
                        if c % 2:
                            last.then_inc(S("hidden_done"), 1)

            def expert_result(t):
                for p in (0, 1):
                    pe.wait_ge(S("hT_ready"), t * 4 + (2 * p + 2))
                    pe.wait_ge(S(f"w2_loaded{p}"), t * 16 + 16)
                    for h in (0, 1):
                        for c in range(FC):
                            last = mm(bank[6 + p][:, h * D:(h + 1) * D], hT[p][:, c, h * P:(h + 1) * P],
                                      w2_in[p][:, c, :], start=(c == 0), stop=(c == FC - 1))
                    last.then_inc(S("y_done"), 1)

            turn_rows(0)
            expert_hidden(0)
            with pe.Fori(0, PAIRS - 1) as t:
                turn_rows(t + 1)
                expert_result(t)
                expert_hidden(t + 1)
                pe.wait_ge(S("yb_ready"), t * 2 + 2)
            expert_result(PAIRS - 1)

            pe.wait_ge(S("yb_ready"), E)
            pe.wait_ge(S("w_clip_ready"), 1)
            for i in (0, 1):
                for c in range(FC):
                    last = pe.transpose(bank[2 + i][:, c * P:(c + 1) * P], w_clip[:, i, c * P:(c + 1) * P], ident)
                last.then_inc(S("wq_turned"), 1)

            for h in (0, 1):
                turn4("x3", lambda b: x3_all[:, b, :], (0, 1), halves=(h,))
                pe.wait_ge(S("wide_copied"), WIDE_TURNS["x3"] + h)
                for gi in range(G2):
                    mm(bank[4 + 2 * gi + h][:], W("key_w")[:, gi * P:(gi + 1) * P], x3T_all[:, COLS4[h]],
                       start=True, stop=True).then_inc(S("u_done"), 1)
            pe.wait_ge(S("wq_kept"), 2)
            for gi in range(G2):
                last = mm(bank[2][:, gi * 64:(gi + 1) * 64], W("heb_u", 16)[:, gi * P:(gi + 1) * P],
                          W("heb_v", 16)[:, gi * 64:(gi + 1) * 64], start=True, stop=True)
            last.then_inc(S("heb_done"), 1)
            pe.wait_ge(S("sig_ready"), 1)
            for gi in range(G2):
                last = mm(bank[0][0:HID, 0:B], W("mn_w1")[:, gi * HID:(gi + 1) * HID], sig[:, gi, :],
                          start=(gi == 0), stop=(gi == G2 - 1))
            last.then_inc(S("mn_hidden"), 1)
            pe.wait_ge(S("mn_gelu"), 1)
            for gi in range(G2):
                last = mm(bank[1][:, gi * B:(gi + 1) * B], W("mn_w2", HID)[:, gi * P:(gi + 1) * P], hidden[:],
                          start=True, stop=True)
            last.then_inc(S("mn_mod"), 1)

            def window_scores(u, p, first=False):
                b = u * 2 + p
                pe.wait_ge(S("x3T_here"), b * 2 + 2)
                if not first:
                    pe.wait_ge(S("v_kept"), b)
                for q in range(4):
                    last = mm(bank[0][0:SEEN, q * D:(q + 1) * D], x3T[p][:, q * QUARTER:q * QUARTER + SEEN],
                              W("qv_w")[:, D:2 * D], start=True, stop=True)
                last.then_inc(S("v_done"), 1)
                pe.wait_ge(S("ks_here"), b * 2 + 2)
                if not first:
                    pe.wait_ge(S("q_kept"), b * 2)
                mm(bank[7][:, 0:D], x3T[p][:, 0:T], W("qv_w")[:, 0:D], start=True, stop=True)
                for gi in range(G2):
                    last = mm(bank[7][:, D + gi * 64:D + (gi + 1) * 64], ks[p][:, gi, 0:T], heb[:, gi, :],
                              start=True, stop=True)
                last.then_inc(S("q_done"), 1)
                if not first:
                    pe.wait_ge(S("score_ready"), b * 2)
                wait_apart(pe, "qs_ready", b * 2 + 2)
                for q in range(4):
                    if q % 2 == 0:
                        mm(bank[1 + q // 2][:, 0:HALF], ident_bf[:],
                           mask_bf[:].rearrange("p (n w) -> p n w", n=1).broadcast_to([P, 4, SEEN]),
                           start=True, stop=False)
                    for gi in range(G2):
                        at = (gi * 2 + q % 2) * SEEN
                        for j in range(4):
                            rows = slice(32 * j, 32 * j + 32)
                            last = mm(bank[1 + q // 2][rows, at:at + SEEN],
                                      qs[p][rows, gi, q * QUARTER:(q + 1) * QUARTER],
                                      ks[p][rows, gi, q * QUARTER:q * QUARTER + SEEN], start=False,
                                      stop=(q % 2 == 1 and gi == G2 - 1))
                    if q % 2:
                        last.then_inc(S("win_scores"), 1)

            def window_context(u, p, first=False):
                b = u * 2 + p
                pe.wait_ge(S("kept_ready"), b + 1)
                for h in (0, 1):
                    for i in range(4):
                        last = pe.transpose(bank[3 + h][0:SEEN, i * P:(i + 1) * P], kept[p][:, 4 * h + i, :], ident)
                    last.then_inc(S("kept_turned"), 1)
                pe.wait_ge(S("keptT_ready"), b * 2 + 2)
                if not first:
                    pe.wait_ge(S("context_ready"), b)
                for q in range(4):
                    for h in range(NH):
                        gi, j = h // 4, h % 4
                        last = mm(bank[5][32 * q:32 * q + 32, h * (HE + 1):(h + 1) * (HE + 1)],
                                  keptT[:, q // 2 * 4 + gi * 2 + q % 2, 32 * j:32 * j + 32], vw[p][:, q, h, :],
                                  start=True, stop=True)
                last.then_inc(S("win_context"), 1)

            def turn_sparse(u):
                pe.wait_ge(S("sparse_ready"), u * 2 + 2)
                for p in (0, 1):
                    last = pe.transpose(bank[6][:, p * T:(p + 1) * T], sparse[p][:], ident)
                last.then_inc(S("sparse_turned"), 1)

            pe.wait_ge(S("heb_kept"), 1)
            pe.wait_ge(S("ident_bf_ready"), 2)
            window_scores(0, 0, first=True)
            window_scores(0, 1)
            window_context(0, 0, first=True)
            with pe.Fori(0, PAIRS - 1) as t:
                window_scores(t + 1, 0)
                window_context(t, 1)
                window_scores(t + 1, 1)
                turn_sparse(t)
                window_context(t + 1, 0)
                pe.wait_ge(S("sparse_copied"), t + 1)

            def decode(h):
                pe.wait_ge(S("sparse_copied"), 2 * h + 2)
                for i in range(4):
                    b = 4 * h + i
                    last = mm(bank[h][:, i * D:(i + 1) * D], sparseT_all[:, b * T:(b + 1) * T], W("decoder"),
                              start=True, stop=True)
                last.then_inc(S("decoded"), 1)

            def plain_scores(h):
                pe.wait_ge(S("wide_copied"), WIDE_TURNS["x4"] + h)
                for i in range(4):
                    b = 4 * h + i
                    last = mm(bank[4 + h][:, i * CTX:(i + 1) * CTX], x4T_all[:, b * T:(b + 1) * T], cT_all[:, b, :],
                              start=True, stop=True)
                last.then_inc(S("plain_scores"), 1)

            def plain_context(h):
                pe.wait_ge(S("wide_copied"), WIDE_TURNS["pr"] + h)
                for i in range(4):
                    b = 4 * h + i
                    last = mm(bank[h][:, i * D:(i + 1) * D], prT_all[:, b * T:(b + 1) * T], c_all[:, b, :],
                              start=True, stop=True)
                last.then_inc(S("plain_out"), 1)

            def turn_x4(h):
                turn4("x4", lambda b: x4_all[:, b, :], (2, 3), halves=(h,))

            def turn_pr(h):
                turn4("pr", lambda b: pr_all[:, b, :], (6, 7), CTX, halves=(h,))

            pe.wait_ge(S("v_kept"), B)
            decode(0)
            window_context(PAIRS - 1, 1)
            turn_x4(0)
            turn_sparse(PAIRS - 1)
            decode(1)
            pe.wait_ge(S("ctx_loaded"), 32)
            plain_scores(0)
            turn_x4(1)
            turn_pr(0)
            plain_scores(1)
            plain_context(0)
            turn_pr(1)
            plain_context(1)
            turn4("x5", lambda b: x5_all[:, b, :], (2, 3))

            pe.wait_ge(S("wide_copied"), WIDE_TURNS["x5"] + 1)
            for c in range(FC):
                for h in (0, 1):
                    if c == 0:
                        pe.wait_ge(S("xq_ready"), h + 1)
                    mm(bank[2 * c + h][:], w1q[:, c * P:(c + 1) * P], xq[:, h * 512:(h + 1) * 512],
                       start=True, stop=True).then_inc(S("ff_hidden"), 1)
            for c in range(FC):
                pe.wait_ge(S("hq_ready"), c + 1)
                for h in (0, 1):
                    last = mm(bank[h][:], w2q[:, c, :], hq[:, c, h * 512:(h + 1) * 512],
                              start=(c == 0), stop=(c == FC - 1))
                    if c == FC - 1:
                        last.then_inc(S("ff_done"), 1)
            for h in (0, 1):
                pe.wait_ge(S("zT_ready"), h + 1)
                for i in range(4):
                    last = pe.transpose(bank[2 + h][:, i * D:(i + 1) * D], zT[:, (4 * h + i) * T:(4 * h + i + 1) * T], ident)
                last.then_inc(S("z_turned"), 1)

        @block.scalar
        def _(act):
            sc = nc.scalar

            def copy_turned(name, t, p, dst, bank_no, rows=P):
                act.wait_ge(S("turned"), turned(name, t, p))
                sc.activation(dst, bank[bank_no][0:rows, 0:P], ACT.Copy).then_inc(S("turned_copied"), 1)

            def keep_high(share, what, p):
                a, n = share.a, share.n(p)
                dst = (q_high if what == "q" else k_high)[a][p]
                if a == "self":
                    act.wait_ge(S(f"self_{what}_proj"), n)
                    src_bank = OWN[a][p] if what == "q" else SELF_KEYS[p]
                    src, dst = bank[src_bank][:], dst[:].rearrange("q g t -> q (g t)")
                else:
                    act.wait_ge(S(f"cross_{what}_full"), n)
                    src, dst = (q_full if what == "q" else k_full)[p][:], dst[:]
                if what == "q":
                    ins = sc.activation(dst, src, ACT.Identity, scale=A("q_low"))
                else:
                    ins = sc.activation(dst, src, ACT.Identity, bias=A("k_bias"), scale=A("k_low"))
                ins.then_inc(S(f"{a}_high"), 1)

            def keep_high_values(share, p):
                a, K = share.a, KEYS[share.a]
                act.wait_ge(S(f"{a}_v_proj"), share.n(p))
                sc.activation(v_high[a][p][0:K, :, 0:HD], bank[OWN[a][p]][0:K, 0:D].rearrange("q (h d) -> q h d", h=HEADS),
                              ACT.Copy).then_inc(S(f"{a}_high"), 1)

            def exps_of(share, p, first):
                K, m = KEYS[share.a], share.attended(p)
                for j0 in (0, 2):
                    for j in (j0, j0 + 1):
                        act.wait_ge(S("scoresT"), (m - 1) * 4 + (j + 1))
                        if not first:
                            act.wait_ge(S("probs01_ready" if j < 2 else "probs23_ready"), (m - 2) * 2 + (j - j0 + 1))
                        sc.activation(probs_all[0:K, j * G * T:(j + 1) * G * T], bank[j][0:K, :], ACT.Exp,
                                      scale=SCALE[share.a]).then_inc(S("exp_ready"), 1)
                    if j0 == 0:
                        for j in (0, 1):
                            act.wait_ge(S("exp_ready"), (m - 1) * 4 + (j + 1))
                            if not first:
                                act.wait_ge(S("weighed"), (m - 2) * 4 + (j + 1))
                            sc.activation(p_high[j][0:K], probs[j][0:K], ACT.Copy).then_inc(S("p_high_ready"), 1)

            def attention_round(s, c):
                if s:
                    for what in ("k", "q"):
                        for p in (0, 1):
                            keep_high(s, what, p)
                if c:
                    for p in (0, 1):
                        copy_turned("x1", c.u, p, x1T[p][:], OWN["cross"][p])
                if c:
                    keep_high(c, "q", 0)
                    keep_high(c, "q", 1)
                if s:
                    keep_high_values(s, 0)
                    keep_high_values(s, 1)
                if c:
                    for p in (0, 1):
                        keep_high(c, "k", p)
                    for p in (0, 1):
                        keep_high_values(c, p)
                units = [(share, p) for share in (c, s) if share for p in (0, 1)]
                for i, unit in enumerate(units):
                    exps_of(*unit, first=(i == 0 and not c))
                    if s and c and i == 2:
                        for p in (0, 1):
                            copy_turned("attn2", c.u, p, a2T[p][:], OWN["cross"][p])
                if c:
                    for p in (0, 1):
                        if not s:
                            copy_turned("attn2", c.u, p, a2T[p][:], OWN["cross"][p])

            act.wait_ge(S("wa_loaded"), 16)
            rounds(act, attention_round)

            def copy4(name, dst, banks, rows=P, halves=(0, 1)):
                for h in halves:
                    act.wait_ge(S("wide_turned"), WIDE_TURNS[name] + h)
                    sc.activation(dst[:, COLS4[h]], bank[banks[h]][0:rows, :], ACT.Copy).then_inc(S("wide_copied"), 1)

            copy4("x2", x2T_all, (0, 1))
            act.wait_ge(S("shifted_ready"), 2)
            sc.activation(exps[:], shifted[:], ACT.Exp).then_inc(S("exps_ready"), 1)
            sc.activation(exp_gap[:], gap[:], ACT.Exp).then_inc(S("exps_ready"), 1)

            def expert_pair(t, more):
                for p in (0, 1):
                    e1 = t * 2 + p + 1
                    for h in (0, 1):
                        act.wait_ge(S("hidden_done"), (e1 - 1) * 2 + (h + 1))
                        sc.activation(hT[p][:, 2 * h:2 * h + 2, :].rearrange("q c s -> q (c s)"), bank[2 + 2 * p + h][:],
                                      ACT.Gelu_apprx_tanh).then_inc(S("hT_ready"), 1)
                    if more:
                        act.dma_start(w1_in[p][:], w1[bass.ds(t * 2 + (2 + p), 1)].rearrange("e d f -> (e d) f")
                                      ).then_inc(S(f"w1_loaded{p}"), 16)
                for p in (0, 1):
                    if more:
                        act.wait_ge(S("y_done"), t * 2 + p + 1)
                        act.dma_start(w2_in[p][:], w2[bass.ds(t * 2 + (2 + p), 1)].rearrange("e f c d -> (e f) c d")
                                      ).then_inc(S(f"w2_loaded{p}"), 16)

            with act.Fori(0, PAIRS - 1) as t:
                expert_pair(t, True)
            expert_pair(PAIRS - 1, False)

            for i in (0, 1):
                act.wait_ge(S("wq_turned"), i + 1)
                dst = w1q[:] if i == 0 else w2q[:].rearrange("p c d -> p (c d)")
                sc.activation(dst, bank[2 + i][:], ACT.Copy).then_inc(S("wq_kept"), 1)
            for h in (0, 1):
                copy4("x3", x3T_all[:], (0, 1), halves=(h,))
                for gi in range(G2):
                    act.wait_ge(S("u_done"), h * G2 + gi + 1)
                    sc.activation(uT[:, gi, 4 * h:4 * h + 4, :].rearrange("q b t -> q (b t)"), bank[4 + 2 * gi + h][:],
                                  ACT.Relu).then_inc(S("uT_ready"), 1)
            act.wait_ge(S("heb_done"), 1)
            sc.activation(heb[:].rearrange("q g c -> q (g c)"), bank[2][:, 0:G2 * 64], ACT.Copy).then_inc(S("heb_kept"), 1)
            act.wait_ge(S("mn_hidden"), 1)
            sc.activation(hidden[:], bank[0][0:HID, 0:B], ACT.Gelu, bias=W("mn_b1", HID)).then_inc(S("mn_gelu"), 1)
            act.wait_ge(S("zabs_ready"), 1)
            sc.activation(zexp[:], zabs[:], ACT.Exp, scale=-1.0).then_inc(S("zexp_ready"), 1)
            act.wait_ge(S("zexp_ready"), 1)
            sc.activation(zln[:], zexp[:], ACT.Ln, bias=1.0).then_inc(S("zln_ready"), 1)

            act.wait_ge(S("q_coef_ready"), 2)

            def window_queries(u, p):
                b = u * 2 + p
                for gi in range(G2):
                    sc.activation(qs[p][:, gi, :], uT[:, gi, bass.ds(b, 1), :].rearrange("q b t -> q (b t)"),
                                  ACT.Identity, bias=q_bias[:, gi, bass.ds(b, 1)],
                                  scale=q_scale[:, gi, bass.ds(b, 1)]).then_inc(S("qs_ready"), 1)

            def keep_scores(u, p):
                for h in (0, 1):
                    act.wait_ge(S("win_scores"), u * 4 + (2 * p + h + 1))
                    sc.activation(score[p][:, 4 * h:4 * h + 4, :].rearrange("q n w -> q (n w)"), bank[1 + h][:, 0:HALF],
                                  ACT.Copy).then_inc(S("score_ready"), 1)

            def keep_values(u, p):
                n = u * 2 + (p + 1)
                act.wait_ge(S("q_done"), n)
                sc.activation(q_tok[p][:], bank[7][:, 0:D], ACT.Relu).then_inc(S("q_kept"), 1)
                sc.activation(heb_raw[p][:], bank[7][:, D:2 * D], ACT.Copy).then_inc(S("q_kept"), 1)
                act.wait_ge(S("v_done"), n)
                sc.activation(vw[p][:, :, :, 0:HE], bank[0][0:SEEN, :].rearrange("q (s h e) -> q s h e", s=4, h=NH),
                              ACT.Relu).then_inc(S("v_kept"), 1)

            def influence(u, p):
                n = u * 2 + (p + 1)
                act.wait_ge(S("dist2_ready"), n)
                sc.activation(infl[p], infl[p], ACT.Sqrt, bias=tiny[:]).then_inc(S("dist_ready"), 1)
                act.wait_ge(S("dist_ready"), n)
                sc.activation(infl[p], infl[p], ACT.Exp, scale=-1.0).then_inc(S("infl_ready"), 1)

            def keep_weights(u, p):
                for h in (0, 1):
                    act.wait_ge(S("kept_turned"), u * 4 + (2 * p + h + 1))
                    sc.activation(keptT[:, 4 * h:4 * h + 4, :].rearrange("q n t -> q (n t)"), bank[3 + h][0:SEEN, :],
                                  ACT.Copy).then_inc(S("keptT_ready"), 1)

            window_queries(0, 0)
            window_queries(0, 1)
            keep_scores(0, 0)
            keep_values(0, 0)
            influence(0, 0)
            keep_scores(0, 1)
            keep_values(0, 1)
            keep_weights(0, 0)
            with act.Fori(0, PAIRS - 1) as t:
                window_queries(t + 1, 0)
                window_queries(t + 1, 1)
                influence(t, 1)
                keep_scores(t + 1, 0)
                act.wait_ge(S("sparse_ready"), t * 2 + 1)
                keep_values(t + 1, 0)
                keep_weights(t, 1)
                influence(t + 1, 0)
                keep_scores(t + 1, 1)
                act.wait_ge(S("sparse_ready"), t * 2 + 2)
                keep_values(t + 1, 1)
                act.wait_ge(S("sparse_turned"), t + 1)
                sc.activation(sparseT_all[:, bass.ds(t * 2 * T, 2 * T)], bank[6][:, 0:2 * T], ACT.Copy
                              ).then_inc(S("sparse_copied"), 1)
                keep_weights(t + 1, 0)
            influence(PAIRS - 1, 1)
            keep_weights(PAIRS - 1, 1)
            copy4("x4", x4T_all, (2, 3), halves=(0,))
            act.wait_ge(S("sparse_turned"), PAIRS)
            sc.activation(sparseT_all[:, (B - 2) * T:B * T], bank[6][:, 0:2 * T], ACT.Copy).then_inc(S("sparse_copied"), 1)

            def plain_probs(h):
                act.wait_ge(S("neg_max_ready"), h + 1)
                for i in range(4):
                    b = 4 * h + i
                    sc.activation(pr_all[:, b, :], bank[4 + h][:, i * CTX:(i + 1) * CTX], ACT.Exp,
                                  bias=neg_max[:, b:b + 1], accum_out=pr_sum[:, b:b + 1]).then_inc(S("pr_ready"), 1)

            plain_probs(0)
            copy4("x4", x4T_all, (2, 3), halves=(1,))
            copy4("pr", prT_all, (6, 7), CTX, halves=(0,))
            plain_probs(1)
            copy4("pr", prT_all, (6, 7), CTX, halves=(1,))
            copy4("x5", x5T, (2, 3))

            act.wait_ge(S("ff_coef_ready"), 1)
            for c in range(FC):
                for h in (0, 1):
                    act.wait_ge(S("ff_hidden"), 2 * c + h + 1)
                    sc.activation(hid[:, c, h * 512:(h + 1) * 512], bank[2 * c + h][:], ACT.Relu, bias=b_q[0][:, c:c + 1],
                                  scale=o_step[0][:, c:c + 1]).then_inc(S("hid_ready"), 1)
            act.wait_ge(S("h_rec_ready"), 1)
            for c in range(1, FC):
                sc.activation(hid[:, c, :], hid[:, c, :], ACT.Relu, scale=a_rec[1][:]).then_inc(S("hid_ready"), 1)
            act.wait_ge(S("ff_coef_ready"), 2)
            for h in (0, 1):
                act.wait_ge(S("ff_done"), h + 1)
                sc.activation(ff_out[:, h * 512:(h + 1) * 512], bank[h][:], ACT.Identity, bias=b_q[1][:],
                              scale=o_step[1][:]).then_inc(S("ff_out_ready"), 1)

        @block.vector
        def _(dve):
            v = nc.vector

            class Steps:

                def __init__(self, name, per=0):
                    self.name, self.per, self.n, self.t = name, per, 0, None

                def turn(self, t):
                    self.n, self.t = 0, t

                def add(self, instruction):
                    instruction.then_inc(S(self.name), 1)
                    self.n += 1

                def wait(self):
                    dve.wait_ge(S(self.name), self.n if self.t is None else self.t * self.per + self.n)

                def wait_apart(self):
                    wait_apart(dve, self.name, self.t * self.per + self.n)

                def link(self, instruction):
                    self.add(instruction)
                    self.wait()

            def layernorm_apply(share, p):
                a = share.a
                dst, name = (x1, "x1_ready") if a == "self" else (x2, "x2_ready")
                dve.wait_ge(S("ln_rstd"), share.attended(p))
                v.tensor_scalar(dst[p][:], y_sum[a][p][:], mv[a][p][:, 0:1], rstd[a][p][:], ALU.subtract, ALU.mult
                                ).then_inc(S(name), 1)

            def split_self(s, what, p):
                parts, taken = (qT, q_high) if what == "q" else (kT, k_high)
                dve.wait_ge(S("self_high"), high("self", what, s.u, p))
                src_bank = OWN["self"][p] if what == "q" else SELF_KEYS[p]
                v.tensor_tensor(parts["self"][p][:].rearrange("q g t -> q (g t)"), bank[src_bank][:],
                                taken["self"][p][:].rearrange("q g t -> q (g t)"), ALU.subtract
                                ).then_inc(S(f"self_{what}_ready"), 1)

            def add_bias(c, what, p):
                full, bias, width = (q_full, "bq2", T) if what == "q" else (k_full, "bk2", CTX)
                dve.wait_ge(S(f"cross_{what}_proj"), c.n(p))
                v.tensor_tensor(full[p][:], bank[OWN["cross"][p]][:, 0:G * width].rearrange("q (g c) -> q g c", g=G),
                                A(bias).rearrange("q (g c) -> q g c", c=1).broadcast_to([P, G, width]), ALU.add
                                ).then_inc(S(f"cross_{what}_full"), 1)

            def low_values(share, p):
                a, K = share.a, KEYS[share.a]
                dve.wait_ge(S(f"{a}_high"), high(a, "v", share.u, p))
                v.tensor_tensor(v_low[a][p][0:K, :, 0:HD], bank[OWN[a][p]][0:K, 0:D].rearrange("q (h d) -> q h d", h=HEADS),
                                v_high[a][p][0:K, :, 0:HD], ALU.subtract).then_inc(S(f"{a}_v_done"), 1)

            def row_maxes(share, p):
                a, K = share.a, KEYS[share.a]
                for j in range(J):
                    dve.wait_ge(S("scores"), (share.scored(p) - 1) * 4 + (j + 1))
                    v.tensor_reduce(maxes[a][p][:, :, 32 * j + MAXROW],
                                    bank[j][:, 0:G * K].rearrange("q (g k) -> q g k", g=G), AX.X, ALU.max
                                    ).then_inc(S("max_ready"), 1)

            def lower_queries(share, p):
                dve.wait_ge(S("max_turned"), share.scored(p))
                qf = qT[share.a][p][:].rearrange("q g t -> q (g t)")
                v.tensor_tensor(qf, qf, bank[OWN[share.a][p]][:], ALU.subtract).then_inc(S("qm_ready"), 1)

            def split_probs(share, p, first=False):
                K, m = KEYS[share.a], share.attended(p)
                for j in (2, 3):
                    dve.wait_ge(S("exp_ready"), (m - 1) * 4 + (j + 1))
                    if not first:
                        dve.wait_ge(S("weighed"), (m - 2) * 4 + (j + 1))
                    v.tensor_copy(p_high[j][0:K], probs[j][0:K]).then_inc(S("p_high23_ready"), 1)
                for j in (2, 3):
                    dve.wait_ge(S("p_high23_ready"), (m - 1) * 2 + (j - 1))
                    v.tensor_tensor(p_low[j][0:K], probs[j][0:K], p_high[j][0:K], ALU.subtract
                                    ).then_inc(S("probs23_ready"), 1)

            def reciprocals(share):
                a = share.a
                chain[a].turn(share.u)
                for p in (0, 1):
                    dve.wait_ge(S("weighed"), share.attended(p) * 4)
                    chain[a].add(v.reciprocal(rec[a][p][:], weighted(a, p)[:, :, HD]))

            def weighted(a, p):
                return bank[OWN[a][p]][:, 0:HEADS * (HD + 1)].rearrange("q (h c) -> q h c", h=HEADS)

            def divided(a, p):
                return v.tensor_tensor(attn[a][p][:].rearrange("q (h d) -> q h d", h=HEADS), weighted(a, p)[:, :, 0:HD],
                                       rec[a][p][:].rearrange("q (h d) -> q h d", d=1).broadcast_to([P, HEADS, HD]),
                                       ALU.mult)

            def normalise_cross(c):
                reciprocals(c)
                chain["cross"].wait()
                for p in (0, 1):
                    divided("cross", p).then_inc(S("attn2_ready"), 1)

            def normalise_self():
                chain["self"].wait()
                for p in (0, 1):
                    chain["self"].add(divided("self", p))

            def self_sum(s):
                chain["self"].wait()
                for p in (0, 1):
                    dve.wait_ge(S(f"x_loaded{p}"), (s.u + 1) * 16)
                    v.tensor_tensor(y_sum["self"][p][:], attn["self"][p][:], x_in[p][:], ALU.add
                                    ).then_inc(S("self_sum_done"), 1)

            def cross_sum(c):
                for p in (0, 1):
                    dve.wait_ge(S("wo_done"), c.n(p))
                    v.tensor_tensor(y_sum["cross"][p][:], bank[OWN["cross"][p]][:, 0:D], x1[p][:], ALU.add
                                    ).then_inc(S("cross_sum_done"), 1)

            def row_stats(share):
                a = share.a
                for p in (0, 1):
                    dve.wait_ge(S(f"{a}_sum_done"), share.n(p))
                    chain[a].add(v.bn_stats(stats[a][p][:], y_sum[a][p][:]))

            def row_mean_var(share):
                a = share.a
                chain[a].wait_apart()
                for p in (0, 1):
                    chain[a].add(v.bn_aggr(mv[a][p][:], stats[a][p][:]))

            def row_var_eps(share):
                a = share.a
                chain[a].wait()
                for p in (0, 1):
                    v.tensor_scalar(var_eps[a][p][:], mv[a][p][:, 1:2], LN_EPS, None, ALU.add).then_inc(S("ln_var"), 1)

            def attention_round(s, c):
                if s:
                    for what in ("k", "q"):
                        for p in (0, 1):
                            split_self(s, what, p)
                    row_maxes(s, 0)
                if c:
                    add_bias(c, "q", 0)
                    add_bias(c, "q", 1)
                if s:
                    row_maxes(s, 1)
                if c:
                    add_bias(c, "k", 0)
                    add_bias(c, "k", 1)
                if s:
                    low_values(s, 0)
                    low_values(s, 1)
                if c:
                    low_values(c, 0)
                    low_values(c, 1)
                    row_maxes(c, 0)
                if s:
                    lower_queries(s, 0)
                if c:
                    row_maxes(c, 1)
                    lower_queries(c, 0)
                    lower_queries(c, 1)
                if s:
                    lower_queries(s, 1)
                if s and c:
                    split_probs(c, 0)
                    split_probs(c, 1)
                    normalise_cross(c)
                    split_probs(s, 0)
                    split_probs(s, 1)
                    cross_sum(c)
                    reciprocals(s)
                    row_stats(c)
                    normalise_self()
                    row_mean_var(c)
                    self_sum(s)
                    row_var_eps(c)
                    row_stats(s)
                    row_mean_var(s)
                    row_var_eps(s)
                    layernorm_apply(c, 0)
                    layernorm_apply(c, 1)
                    layernorm_apply(s, 0)
                    layernorm_apply(s, 1)
                elif s:
                    split_probs(s, 0, first=True)
                    split_probs(s, 1)
                    reciprocals(s)
                    normalise_self()
                    self_sum(s)
                    row_stats(s)
                    row_mean_var(s)
                    row_var_eps(s)
                    layernorm_apply(s, 0)
                    layernorm_apply(s, 1)
                else:
                    split_probs(c, 0)
                    split_probs(c, 1)
                    normalise_cross(c)
                    cross_sum(c)
                    row_stats(c)
                    row_mean_var(c)
                    row_var_eps(c)
                    layernorm_apply(c, 0)
                    layernorm_apply(c, 1)

            steps = Steps("step")
            dve.wait_ge(S("wa_loaded"), 16)
            v.tensor_copy(ident_bf[:], ident).then_inc(S("ident_bf_ready"), 1)
            dve.wait_ge(S("wa2_loaded"), 16)
            dve.wait_ge(S("pool_consts"), 20)
            chain = {"self": Steps("self_step", 8), "cross": Steps("cross_step", 6)}
            rounds(dve, attention_round)

            dve.wait_ge(S("wb_loaded"), 16)
            v.tensor_copy(mask_bf[:], W("mask")).then_inc(S("ident_bf_ready"), 1)
            v.tensor_copy(tri_bf[:], W("tri")).then_inc(S("tri_ready"), 1)

            dve.wait_ge(S("routed"), 1)
            steps.link(v.tensor_copy(logits[:].rearrange("p b e -> p (b e)"), bank[2][:, 0:B * E]))
            for b in range(B):
                steps.add(v.max(top8[:, b, :], logits[:, b, :]))
            steps.wait()
            for b in range(B):
                steps.add(v.max_index(index8[:, b, :], top8[:, b, :], logits[:, b, :]))
            v.tensor_tensor(shifted[:], logits[:], top8[:, :, 0:1].broadcast_to([P, B, E]), ALU.subtract
                            ).then_inc(S("shifted_ready"), 1)
            v.tensor_tensor(gap[:], top8[:, :, 1], top8[:, :, 0], ALU.subtract).then_inc(S("shifted_ready"), 1)
            steps.wait()
            steps.link(v.tensor_copy(index_f[:], index8[:, :, 0:2]))
            for k in (0, 1):
                steps.add(v.tensor_tensor(onehot[k][:],
                                          W("iota_e").rearrange("p (b e) -> p b e", b=1).broadcast_to([P, B, E]),
                                index_f[:, :, k:k + 1].broadcast_to([P, B, E]), ALU.is_equal))
            steps.wait()
            v.tensor_tensor(chosen[:], onehot[0][:], onehot[1][:], ALU.add).then_inc(S("chosen_ready"), 1)
            dve.wait_ge(S("exps_ready"), 2)
            steps.link(v.tensor_reduce(denom[:], exps[:], AX.X, ALU.add))
            steps.add(v.reciprocal(gate[:, 0, :], denom[:]))
            steps.wait()
            steps.add(v.tensor_tensor(gate[:, 1, :], gate[:, 0, :], exp_gap[:], ALU.mult))
            dve.wait_ge(S("places"), 1)
            places = bank[0][:, 0:B * E].rearrange("p (b e) -> p b e", b=B)
            v.tensor_copy(place[:], places).then_inc(S("place_ready"), 1)
            dve.wait_ge(S("place_ready"), 1)
            steps.link(v.tensor_tensor(slot_of[:], place[:],
                                       W("slot_e").rearrange("p (b e) -> p b e", b=1).broadcast_to([P, B, E]),
                            ALU.add))
            for k in (0, 1):
                steps.add(v.tensor_tensor(picked[k][:], onehot[k][:], place[:], ALU.mult))
                steps.add(v.tensor_tensor(picked[2 + k][:], onehot[k][:], slot_of[:], ALU.mult))
            steps.wait()
            for k in (0, 1):
                steps.add(v.tensor_reduce(place_k[:, k, :], picked[k][:], AX.X, ALU.add))
                steps.add(v.tensor_reduce(slot_k[:, k, :], picked[2 + k][:], AX.X, ALU.add))
            steps.wait()
            steps.add(v.tensor_scalar(over[:], place_k[:], float(CAP), 2.0 * SLOTS, ALU.is_ge, ALU.mult))
            steps.add(v.tensor_scalar(fits[:], place_k[:], float(CAP), None, ALU.is_lt))
            steps.add(v.tensor_scalar(get_f[:], slot_k[:], float(SLOTS - 1), None, ALU.min))
            steps.wait()
            steps.link(v.tensor_tensor(put_f[:], slot_k[:], over[:], ALU.add))
            v.tensor_copy(put[:], put_f[:]).then_inc(S("put_ready"), 1)
            v.tensor_copy(get[:], get_f[:]).then_inc(S("put_ready"), 1)
            steps.wait()
            v.tensor_tensor(gates[:], gate[:], fits[:], ALU.mult).then_inc(S("gates_ready"), 1)

            steps.add(v.tensor_reduce(w_abs[:, 0:FC], W("w1f").rearrange("p (c d) -> p c d", c=FC), AX.X, ALU.max,
                            apply_absolute_value=True))
            steps.add(v.tensor_reduce(w_abs[:, FC:FC + 1], W("w2f"), AX.X, ALU.max, apply_absolute_value=True))
            steps.add(v.tensor_scalar(two_key[:], W("is_square"), -2.0, 2.0, ALU.mult, ALU.add))
            steps.add(v.tensor_scalar(not_square[:], W("is_square"), -1.0, 1.0, ALU.mult, ALU.add))
            steps.add(v.tensor_scalar(neg_square[:], W("is_square"), -1.0, None, ALU.mult))
            steps.wait()
            steps.link(v.tensor_scalar(w_floor[:], w_abs[:], 1e-8, None, ALU.max))
            steps.link(v.tensor_scalar(w_step[:], w_floor[:], 1.0 / 127.0, None, ALU.mult))
            steps.link(v.reciprocal(w_rec[:], w_step[:]))
            for i in range(FC + 1):
                src, dst = (W("w1f"), w_div[:, 0, :]) if i < FC else (W("w2f"), w_div[:, 1, :])
                cols = slice(i * P, (i + 1) * P) if i < FC else slice(0, FF)
                steps.add(v.tensor_scalar(dst[:, cols], src[:, cols], w_rec[:, i:i + 1], ROUND, ALU.mult, ALU.add))
            steps.wait()
            steps.link(v.tensor_scalar(w_int, w_div, ROUND, 127.0, ALU.subtract, ALU.min))
            v.tensor_scalar(w_clip, w_int, -128.0, None, ALU.max).then_inc(S("w_clip_ready"), 1)

            def keep_rows(t):
                for p in (0, 1):
                    dve.wait_ge(S("xb_turned"), t * 2 + (p + 1))
                    v.tensor_copy(xbT[p][:], bank[p][:, 0:CAP]).then_inc(S("xbT_ready"), 1)

            def keep_results(t):
                for p in (0, 1):
                    dve.wait_ge(S("y_done"), t * 2 + (p + 1))
                    v.tensor_copy(yb[p][:].rearrange("q h d -> q (h d)"), bank[6 + p][:, 0:2 * D]).then_inc(S("yb_ready"), 1)

            keep_rows(0)
            with dve.Fori(0, PAIRS - 1) as t:
                keep_rows(t + 1)
                keep_results(t)
                for p in (0, 1):
                    dve.wait_ge(S(f"y_stored{p}"), t * 16 + 16)
            keep_results(PAIRS - 1)

            dve.wait_ge(S("gates_ready"), 1)
            dve.wait_ge(S("x2b_ready"), 1)
            def layernorm4_stats(h, y):
                for i in range(4):
                    steps.add(v.bn_stats(stats4[h][:, i, :], y(4 * h + i)))
                steps.wait()
                for i in range(4):
                    steps.add(v.bn_aggr(mv4[h][:, i, :], stats4[h][:, i, :]))
                steps.wait()
                v.tensor_scalar(var4[h][:], mv4[h][:, :, 1], LN_EPS, None, ALU.add).then_inc(S("ln4_var"), 1)

            def layernorm4_apply(name, h, y, out):
                dve.wait_ge(S("ln4_rstd"), LN4[name] + h)
                for i in range(4):
                    b = 4 * h + i
                    v.tensor_scalar(out(b), y(b), mv4[h][:, i, 0:1], rstd4[h][:, i:i + 1], ALU.subtract, ALU.mult
                                    ).then_inc(S(f"{name}_ready"), 1)

            def add_experts(batches):
                for k, before in ((0, x2b), (1, got[0])):
                    for b in batches:
                        steps.add(v.scalar_tensor_tensor(got[k][:, b, :], got[k][:, b, :], gates[:, k, b:b + 1],
                                                        before[:, b, :], ALU.mult, ALU.add))
                    steps.wait()

            for i, batches in enumerate(GATHERS):
                dve.wait_ge(S(f"gathered{i}"), 16 * 2 * len(batches))
                add_experts(batches)
                if i == 0:
                    layernorm4_stats(0, lambda b: got[1][:, b, :])
                if i == 1:
                    layernorm4_apply("x3", 0, lambda b: got[1][:, b, :], lambda b: x3_all[:, b, :])
            layernorm4_stats(1, lambda b: got[1][:, b, :])

            def sums(h):
                for gi in range(G2):
                    dve.wait_ge(S("uT_ready"), h * G2 + gi + 1)
                    steps.add(v.tensor_reduce(sum_all[:, gi, QUADS[h]], uT[:, gi, QUADS[h]], AX.X, ALU.add))
                    steps.add(v.tensor_reduce(sum_eighth[:, gi, QUADS[h]], uT[:, gi, QUADS[h], 7:T:8], AX.X, ALU.add))

            def key_half(h):
                rows, quad = sig_p[:, 0, QUADS[h]], QUADS[h]
                steps.link(v.tensor_scalar(rows, uT[:, 0, quad], W("is_square"), not_square[:], ALU.mult, ALU.add))
                v.tensor_tensor(k_all[:, 0, quad], uT[:, 0, quad], rows, ALU.mult).then_inc(S("k_half"), 1)

            sums(0)
            layernorm4_apply("x3", 1, lambda b: got[1][:, b, :], lambda b: x3_all[:, b, :])
            key_half(0)
            sums(1)
            steps.wait()
            steps.link(v.scalar_tensor_tensor(sum_both[:], sum_eighth[:], 0.5 * 8, sum_all[:], ALU.mult, ALU.add))
            v.tensor_scalar(sig[:], sum_both[:], 1.0 / T, None, ALU.mult).then_inc(S("sig_ready"), 1)
            steps.add(v.scalar_tensor_tensor(pre[:], W("mn_b2"), 0.1, W("base_metric"), ALU.mult, ALU.add))
            key_half(1)
            dve.wait_ge(S("mn_mod"), 1)
            mod = bank[1][:, 0:G2 * B].rearrange("p (g b) -> p g b", g=G2)
            steps.link(v.scalar_tensor_tensor(zm[:], mod, 0.1,
                                              pre[:].rearrange("p (g b) -> p g b", b=1).broadcast_to([P, G2, B]),
                                   ALU.mult, ALU.add))
            v.scalar_tensor_tensor(zabs[:], zm[:], -1.0, zm[:], ALU.mult, ALU.max).then_inc(S("zabs_ready"), 1)
            steps.link(v.tensor_scalar(zpos[:], zm[:], 0.0, None, ALU.max))
            dve.wait_ge(S("zln_ready"), 1)
            steps.link(v.tensor_tensor(metric[:], zpos[:], zln[:], ALU.add))
            v.tensor_scalar(q_scale[:], metric[:], two_key[:], None, ALU.mult).then_inc(S("q_coef_ready"), 1)
            v.tensor_scalar(q_bias[:], metric[:], neg_square[:], None, ALU.mult).then_inc(S("q_coef_ready"), 1)
            chain = Steps("win_step", 4)

            def weights(u, p, meanwhile=None):
                n = u * 2 + (p + 1)
                for r in range(TOPK // 8):
                    for op in (0, 1):
                        for i in range(NTILE):
                            src = score[p] if r == 0 else work[p]
                            if i % 4 == 0 and r + op == 0:
                                wait_apart(dve, "score_ready", u * 4 + (2 * p + i // 4 + 1))
                            if i % 4 == 0 and r + op > 0:
                                done = (r * 2 + op - 1) * NTILE + i + 4
                                wait_apart(dve, "sorted", u * 128 + (p * 64 + done))
                            if op == 0:
                                step = v.max(best[p][:, r, i, :], src[:, i, :])
                            else:
                                step = v.match_replace(work[p][:, i, :], best[p][:, r, i, :], src[:, i, :], TAKEN)
                            step.then_inc(S("sorted"), 1)
                    if r == 0:
                        dve.wait_ge(S("qq_ready"), n)
                        v.tensor_reduce(q_n2[p][:], qq[p][:].rearrange("q (h e) -> q h e", h=NH), AX.X, ALU.add
                                        ).then_inc(S("q_n2_ready"), 1)
                    if r == 1 and meanwhile is not None:
                        meanwhile()
                dve.wait_ge(S("infl_ready"), n)
                dve.wait_ge(S("sorted"), u * 128 + (p * 64 + 64))
                v.scalar_tensor_tensor(kept[p][:], work[p], 1.5 * MASKED, infl[p], ALU.is_le, ALU.mult
                                       ).then_inc(S("kept_ready"), 1)

            def contexts(u, p):
                n = u * 2 + (p + 1)
                if p == 0:
                    chain.turn(u)
                dve.wait_ge(S("win_context"), n)
                c = bank[5][:, 0:NH * (HE + 1)].rearrange("q (h e) -> q h e", h=NH)
                chain.link(v.tensor_scalar(infl_sum[p][:], c[:, :, HE], 1e-8, None, ALU.add))
                chain.link(v.reciprocal(infl_rec[p][:], infl_sum[p][:]))
                v.tensor_tensor(context[p][:].rearrange("q (h e) -> q h e", h=NH), c[:, :, 0:HE],
                                infl_rec[p][:].rearrange("q (h e) -> q h e", e=1).broadcast_to([P, NH, HE]),
                                ALU.mult).then_inc(S("context_ready"), 1)

            weights(0, 0)
            with dve.Fori(0, PAIRS - 1) as t:
                weights(t, 1, meanwhile=lambda: contexts(t, 0))
                weights(t + 1, 0, meanwhile=lambda: contexts(t, 1))
            weights(PAIRS - 1, 1, meanwhile=lambda: contexts(PAIRS - 1, 0))

            def four(tensor, h):
                return tensor[:, QUADS[h], :]

            def decoder_stats(h):
                dve.wait_ge(S("decoded"), h + 1)
                steps.link(v.tensor_tensor(four(y4, h), bank[h][:].rearrange("p (b d) -> p b d", b=4), four(x3_all, h),
                                          ALU.add))
                layernorm4_stats(h, lambda b: y4[:, b, :])

            def decoder_norm(h):
                layernorm4_apply("x4", h, lambda b: y4[:, b, :], lambda b: x4_all[:, b, :])

            def plain_maxima(h):
                dve.wait_ge(S("plain_scores"), h + 1)
                v.tensor_reduce(neg_max[:, QUADS[h]], bank[4 + h][:, 0:4 * CTX].rearrange("p (b c) -> p b c", b=4),
                                AX.X, ALU.max, negate=True).then_inc(S("neg_max_ready"), 1)

            def plain_stats(h):
                dve.wait_ge(S("pr_ready"), 4 * h + 4)
                steps.link(v.reciprocal(pr_rec[:, QUADS[h]], pr_sum[:, QUADS[h]]))
                dve.wait_ge(S("plain_out"), h + 1)
                for i in range(4):
                    b = 4 * h + i
                    steps.add(v.scalar_tensor_tensor(y5[:, b, :], bank[h][:, i * D:(i + 1) * D], pr_rec[:, b:b + 1],
                                                    x4_all[:, b, :], ALU.mult, ALU.add))
                steps.wait()
                layernorm4_stats(h, lambda b: y5[:, b, :])

            decoder_stats(0)
            decoder_norm(0)
            contexts(PAIRS - 1, 1)
            decoder_stats(1)
            plain_maxima(0)
            decoder_norm(1)
            plain_maxima(1)
            plain_stats(0)
            plain_stats(1)
            for h in (0, 1):
                layernorm4_apply("x5", h, lambda b: y5[:, b, :], lambda b: x5_all[:, b, :])

            def step_of(i):
                dve.wait_ge(S(f"a_top_ready{i}"), 1)
                steps.link(v.tensor_scalar(a_floor[i][:], a_top[i][:], 1e-8, None, ALU.max))
                steps.link(v.tensor_scalar(a_step[i][:], a_floor[i][:], 1.0 / 255.0, None, ALU.mult))

            def bias_of(i):
                ws = w_step[:, 0:FC] if i == 0 else w_step[:, FC:FC + 1]
                bias = W("b1f") if i == 0 else W("b2f")
                steps.link(v.tensor_scalar(o_step[i][:], ws, a_step[i][:], None, ALU.mult))
                steps.link(v.reciprocal(b_rec[i][:], o_step[i][:]))
                steps.link(v.tensor_tensor(b_div[i][:], bias, b_rec[i][:], ALU.mult))
                steps.link(v.tensor_scalar(b_int[i][:], b_div[i][:], ROUND, ROUND, ALU.add, ALU.subtract))
                v.tensor_tensor(b_q[i][:], b_int[i][:], o_step[i][:], ALU.mult
                                ).then_inc(S("ff_coef_ready"), 1)

            dve.wait_ge(S("wide_copied"), WIDE_TURNS["x5"] + 1)
            v.tensor_reduce(a_max[0][:], x5T, AX.X, ALU.max).then_inc(S("a_max_ready0"), 1)
            step_of(0)
            steps.link(v.reciprocal(a_rec[0][:], a_step[0][:]))
            for h in (0, 1):
                steps.add(v.tensor_scalar(zT[:, COLS4[h]], x5T[:, COLS4[h]], a_rec[0][:], 0.0, ALU.mult, ALU.max))
            steps.wait()
            for h in (0, 1):
                steps.add(v.tensor_scalar(ff_out[:, COLS4[h]], zT[:, COLS4[h]], 255.0, ROUND, ALU.min, ALU.add))
            steps.wait()
            for h in (0, 1):
                v.tensor_scalar(xq[:, COLS4[h]], ff_out[:, COLS4[h]], ROUND, None, ALU.subtract).then_inc(S("xq_ready"), 1)
            bias_of(0)
            for c in range(FC):
                for h in (0, 1):
                    i = 2 * c + h
                    dve.wait_ge(S("hid_ready"), i + 1)
                    v.tensor_reduce(h_max[:, i:i + 1], hid[:, c, h * 512:(h + 1) * 512], AX.X, ALU.max
                                    ).then_inc(S("h_max_ready"), 1)
            dve.wait_ge(S("h_max_ready"), 8)
            v.tensor_reduce(a_max[1][:], h_max[:], AX.X, ALU.max).then_inc(S("a_max_ready1"), 1)
            step_of(1)
            v.reciprocal(a_rec[1][:], a_step[1][:]).then_inc(S("h_rec_ready"), 1)
            dve.wait_ge(S("h_rec_ready"), 1)
            steps.add(v.tensor_scalar(hid[:, 0, :], hid[:, 0, :], a_rec[1][:], 0.0, ALU.mult, ALU.max))
            bias_of(1)
            for c in range(FC):
                if c > 0:
                    dve.wait_ge(S("hid_ready"), 2 * FC + c)
                steps.link(v.tensor_scalar(hid[:, c, :], hid[:, c, :], 255.0, ROUND, ALU.min, ALU.add))
                v.tensor_scalar(hq[:, c, :], hid[:, c, :], ROUND, None, ALU.subtract).then_inc(S("hq_ready"), 1)
            for h in (0, 1):
                cols = slice(h * 512, (h + 1) * 512)
                dve.wait_ge(S("ff_out_ready"), h + 1)
                v.tensor_tensor(zT[:, cols], ff_out[:, cols], x5T[:, cols], ALU.add).then_inc(S("zT_ready"), 1)
            def z(b):
                return bank[2 + b // 4][:, (b % 4) * D:(b % 4 + 1) * D]

            for h in (0, 1):
                dve.wait_ge(S("z_turned"), h + 1)
                layernorm4_stats(h, z)
            for h in (0, 1):
                layernorm4_apply("final", h, z, lambda b: final[:, b, :])


def kernel(**inputs):
    import numpy as np
    import concourse.bacc as bacc
    from concourse.bass_utils import run_bass_kernel_spmd

    a = {k: np.ascontiguousarray(v) for k, v in inputs.items()}
    f32 = np.float32
    head = np.arange(HEADS)
    padded = [((head // 4)[:, None] * P + 32 * (head % 4)[:, None] + c * HD + np.arange(HD)[None, :]).reshape(-1)
              for c in range(PARTS)]

    def pad_cols(w):
        out = np.zeros((w.shape[0], G * P), f32)
        for at in padded:
            out[:, at] = w
        return out

    def pad_bias(vec):
        out = np.zeros(G * P, f32)
        for at in padded:
            out[at] = vec
        return out.reshape(G, P).T

    def rows(array, n=P):
        array = np.asarray(array, f32).reshape(array.shape[0], -1) if array.ndim > 1 else array.reshape(1, -1)
        out = np.zeros((P, array.shape[1]), f32)
        out[:array.shape[0]] = array
        return out

    def packed(names, parts):
        return np.ascontiguousarray(np.concatenate([rows(parts[name]) for name, _ in names], axis=1))

    part = np.arange(P)
    r = part % 32
    parts_a = {
        "wq": pad_cols(a["L0_attn_Wq"].T), "wk": pad_cols(a["L0_attn_Wk"].T), "wv": a["L0_attn_Wv"].T,
        "k_bias": -(r == MAXROW).astype(f32)[:, None], "ident": np.eye(P, dtype=f32),
        "q_low": ((r >= 2 * HD) & (r < MAXROW)).astype(f32)[:, None],
        "k_low": ((r >= HD) & (r < 2 * HD)).astype(f32)[:, None],
        "wq2": pad_cols(a["L0_xattn_Wq"]), "wk2": pad_cols(a["L0_xattn_Wk"]), "wv2": a["L0_xattn_Wv"],
        "bq2": pad_bias(a["L0_xattn_bq"]), "bk2": pad_bias(a["L0_xattn_bk"]), "bv2": a["L0_xattn_bv"],
        "wo": a["L0_xattn_Wo"], "bo": a["L0_xattn_bo"], "router": a["L0_ffn_w_router"],
    }
    nh = np.arange(NH)
    enc_q = a["L1_attn_encoder_query"].transpose(1, 0, 2)
    enc_v = a["L1_attn_encoder_value"].transpose(1, 0, 2)

    def doubled(w):
        w = w.reshape(w.shape[0], G2, 4, 1, HE)
        return np.broadcast_to(w, (w.shape[0], G2, 4, 2, HE)).reshape(w.shape[0], G2 * P)

    mn_w1 = np.zeros((G2, 4, 2, HE, HID), f32)
    mn_w1[:, :, 0] = a["L1_attn_mn_w1"].reshape(G2, 4, HE, HID)
    heb_u = np.zeros((4, 4, G2, 4, 32), f32)
    heb_v = np.zeros((4, 4, G2, 4, HE), f32)
    for h in nh:
        heb_u[h % 4, :, h // 4, h % 4, :HE] = a["L1_attn_hebbian_U"][h].T
        heb_v[h % 4, :, h // 4, h % 4, :] = a["L1_attn_hebbian_V"][h]
    col = np.arange(SEEN)[None, :]
    mask = np.where((col >= r[:, None]) & (col < r[:, None] + WIN), 0.0, MASKED).astype(f32)
    parts_b = {
        "tri": (part[:, None] > part[None, :]).astype(f32),
        "iota_e": np.broadcast_to(np.arange(E, dtype=f32), (P, E)),
        "slot_e": np.broadcast_to(np.arange(E, dtype=f32) * CAP, (P, E)),
        "ffn_bias": np.broadcast_to(a["L0_ffn_bias"].reshape(1, D), (P, D)),
        "key_w": doubled(enc_q), "qv_w": np.concatenate([enc_q.reshape(D, D), enc_v.reshape(D, D)], axis=1),
        "mn_w1": mn_w1.reshape(G2, P, HID).transpose(1, 0, 2), "mn_b1": a["L1_attn_mn_b1"][:, None],
        "mn_w2": doubled(a["L1_attn_mn_w2"].reshape(HID, NH, HE)),
        "mn_b2": doubled(a["L1_attn_mn_b2"].reshape(1, NH, HE)).reshape(G2, P).T,
        "base_metric": doubled(a["L1_attn_base_metric"].reshape(1, NH, HE)).reshape(G2, P).T,
        "is_square": (r >= HE).astype(f32)[:, None],
        "heb_u": heb_u.reshape(16, G2 * P), "heb_v": heb_v.reshape(16, G2 * 64), "decoder": a["L1_attn_decoder"],
        "mask": mask, "w1f": a["L1_ffn_w1"].reshape(FC, P, D).transpose(1, 0, 2),
        "b1f": a["L1_ffn_b1"].reshape(FC, P).T, "w2f": a["L1_ffn_w2"], "b2f": a["L1_ffn_b2"][:, None],
    }
    x = a["x"][:, ::-1, :]
    arrays = {
        "x_rows": x, "x_cols": x.transpose(0, 2, 1), "ctx_rows": a["ctx_1024"], "ctx_cols": a["ctx_1024"].transpose(0, 2, 1),
        "pack_a": packed(PACK_A, parts_a), "pack_b": packed(PACK_B, parts_b),
        "w1": a["L0_ffn_w1"], "w2": a["L0_ffn_w2"].reshape(E, FC, P, D).transpose(0, 2, 1, 3),
    }
    arrays = {k: np.ascontiguousarray(v) for k, v in arrays.items()}
    nc = bacc.Bacc("TRN2", target_bir_lowering=False, num_devices=1)
    args = [nc.dram_tensor(k, v.shape, mybir.dt.from_np(v.dtype), kind="ExternalInput").ap() for k, v in arrays.items()]
    out = nc.dram_tensor("out", (B, T, D), F32, kind="ExternalOutput").ap()
    xb_dram = nc.dram_tensor("xb_dram", (SLOTS, D), F32, kind="Internal").ap()
    y_dram = nc.dram_tensor("y_dram", (SLOTS, D), F32, kind="Internal").ap()
    decoder_kernel(nc, *args, out, xb_dram, y_dram)
    result = run_bass_kernel_spmd(nc, [arrays], core_ids=[0])
    return np.ascontiguousarray(result.results[0]["out"][:, ::-1, :])
```
